# Optimizing a Trainium2 kernel written in Bass

```python
import numpy as np
import jax
import jax.numpy as jnp

def _softmax(x, axis=-1):
    return jax.nn.softmax(x, axis=axis)

def _gelu(x):
    return jax.nn.gelu(x, approximate=True)

def _silu(x):
    return jax.nn.silu(x)

def _sigmoid(x):
    return jax.nn.sigmoid(x)

def _layernorm(x, axis=-1, eps=1e-05):
    m = jnp.mean(x, axis=axis, keepdims=True)
    v = jnp.var(x, axis=axis, keepdims=True)
    return (x - m) / jnp.sqrt(v + eps)

def _scatter_add(tgt, idx, src, axis=0):
    return tgt.at[idx].add(src)

def _segment_sum(src, seg, n):
    return jax.ops.segment_sum(src, seg, n)
kernel_name = 'mk_xattn_seq_d4_seqx_r8_e51969'

def setup_inputs(seed: int=0):
    np.random.seed(seed)
    _w = jnp.asarray

    def _rec_inputs():
        import jax
        import jax.numpy as jnp
        _rk = jax.random.key(seed)
        x = -0.0002928 + 1 * jax.random.normal(jax.random.fold_in(_rk, 1), (64, 64, 256), jnp.float32)
        _lenS = 64 - jax.random.randint(jax.random.fold_in(_rk, 7), (64,), 0, max(1, 64 // 4) + 1, jnp.int32)
        _lenS2 = 64 - jax.random.randint(jax.random.fold_in(_rk, 8), (64,), 0, max(1, 64 // 4) + 1, jnp.int32)
        _ctx_2048P = jax.random.normal(jax.random.fold_in(_rk, 11), (64, 16, 256), jnp.float32)
        _ctx_2048c = jax.random.dirichlet(jax.random.fold_in(_rk, 511), 0.3 * jnp.ones((16,), jnp.float32), (64, 64))
        _ctx_2048t = jnp.einsum('bsk,bkd->bsd', _ctx_2048c, _ctx_2048P)
        _ctx_2048t = _ctx_2048t * jax.lax.rsqrt(jnp.mean(jnp.square(_ctx_2048t)) + 1e-12) * 0.953939
        ctx_2048 = -1.39393e-06 + 0.999914 * (_ctx_2048t + 0.3 * jax.random.normal(jax.random.fold_in(_rk, 611), (64, 64, 256), jnp.float32))
        _validS = jnp.arange(64)[None, :] < _lenS[:, None]
        _validS2 = jnp.arange(64)[None, :] < _lenS2[:, None]
        _causal = jnp.tril(jnp.ones((64, 64), dtype=bool))
        mask_Bx1xSxS2_ff0 = jnp.where(jnp.ones((64, 1, 64, 64), dtype=bool), 0.0, -1000000000.0).astype(jnp.float32)
        mask_BxS2_ik0 = jnp.where(jnp.broadcast_to(_validS2[:, :], (64, 64)), 0, 1).astype(jnp.int32)
        return (x, ctx_2048, mask_Bx1xSxS2_ff0, mask_BxS2_ik0)
    x, ctx_2048, mask_Bx1xSxS2_ff0, mask_BxS2_ik0 = _rec_inputs()

    def _L0_xattn_setup():
        import jax, jax.numpy as jnp
        import numpy as np
        EPS = 1e-05

        def _inorm(x):
            m = jnp.mean(x, axis=-1, keepdims=True)
            v = jnp.var(x, axis=-1, keepdims=True)
            return (x - m) * jax.lax.rsqrt(v + EPS)

        def _conv1x1(W, b, x):
            return jnp.einsum('oc,bct->bot', W, x) + b[None, :, None]
        key = jax.random.key(seed)
        ks = jax.random.split(key, 10)
        B, C, T = (4, 64, 256)
        s = 1.0 / np.sqrt(C)
        return {'x_c': jax.random.normal(ks[0], (B, C, T), jnp.float32), 'x_s': jax.random.normal(ks[1], (B, C, T), jnp.float32), 'Wn': jax.random.normal(ks[2], (C, C), jnp.float32) * s, 'bn': jax.random.normal(ks[3], (C,), jnp.float32) * s, 'Wm': jax.random.normal(ks[4], (C, C), jnp.float32) * s, 'bm': jax.random.normal(ks[5], (C,), jnp.float32) * s, 'Wl': jax.random.normal(ks[6], (C, C), jnp.float32) * s, 'bl': jax.random.normal(ks[7], (C,), jnp.float32) * s, 'Wo': jax.random.normal(ks[8], (C, C), jnp.float32) * s, 'bo': jax.random.normal(ks[9], (C,), jnp.float32) * s}
    _L0_xattn_all = _L0_xattn_setup()
    _L0_xattn_in = {k: v for k, v in _L0_xattn_all.items() if k in ('Wn', 'bn', 'Wm', 'bm', 'Wl', 'bl', 'Wo', 'bo')}
    del _L0_xattn_all

    def _L1_xattn_setup():
        import jax, jax.numpy as jnp
        import numpy as np
        H = 256
        NH = 32
        KVH = 8
        HD = H // NH
        GROUPS = NH // KVH
        EPS = 1e-06
        B, L, S = (4, 128, 128)

        def _gqa_forward(hidden_state, encoder_hidden_state, encoder_attention_mask, Wq, bq, Wk, bk, Wv, bv, Wo, bo, gamma, beta):
            b, l, _ = hidden_state.shape
            s = encoder_hidden_state.shape[1]
            q = hidden_state @ Wq + bq
            k = encoder_hidden_state @ Wk + bk
            v = encoder_hidden_state @ Wv + bv
            q = q.reshape(b, l, KVH, GROUPS, HD).transpose(0, 2, 3, 1, 4)
            k = k.reshape(b, s, KVH, HD).transpose(0, 2, 1, 3)
            v = v.reshape(b, s, KVH, HD).transpose(0, 2, 1, 3)
            scale = 1.0 / jnp.sqrt(jnp.asarray(HD, q.dtype))
            scores = jnp.einsum('bkgld,bksd->bkgls', q, k) * scale
            scores = scores + encoder_attention_mask[:, :, None, :, :]
            attn = jax.nn.softmax(scores, axis=-1)
            out = jnp.einsum('bkgls,bksd->bkgld', attn, v)
            out = out.transpose(0, 3, 1, 2, 4).reshape(b, l, H)
            out = out @ Wo + bo
            x = out + hidden_state
            mu = jnp.mean(x, axis=-1, keepdims=True)
            var = jnp.var(x, axis=-1, keepdims=True)
            return (x - mu) * jax.lax.rsqrt(var + EPS) * gamma + beta
        key = jax.random.key(seed)
        ks = jax.random.split(key, 12)
        sd = 0.02
        return {'hidden_state': jax.random.normal(ks[0], (B, L, H), jnp.float32), 'encoder_hidden_state': jax.random.normal(ks[1], (B, S, H), jnp.float32), 'encoder_attention_mask': jnp.zeros((B, 1, L, S), jnp.float32), 'Wq': jax.random.normal(ks[2], (H, H), jnp.float32) * sd, 'bq': jnp.zeros((H,), jnp.float32), 'Wk': jax.random.normal(ks[3], (H, KVH * HD), jnp.float32) * sd, 'bk': jnp.zeros((KVH * HD,), jnp.float32), 'Wv': jax.random.normal(ks[4], (H, KVH * HD), jnp.float32) * sd, 'bv': jnp.zeros((KVH * HD,), jnp.float32), 'Wo': jax.random.normal(ks[5], (H, H), jnp.float32) * sd, 'bo': jnp.zeros((H,), jnp.float32), 'gamma': jnp.ones((H,), jnp.float32), 'beta': jnp.zeros((H,), jnp.float32)}
    _L1_xattn_all = _L1_xattn_setup()
    _L1_xattn_in = {k: v for k, v in _L1_xattn_all.items() if k in ('Wq', 'bq', 'Wk', 'bk', 'Wv', 'bv', 'Wo', 'bo', 'gamma', 'beta')}
    del _L1_xattn_all

    def _L2_xattn_setup():
        import jax, jax.numpy as jnp
        import numpy as np
        B, P, K, H, NH = (4, 256, 32, 256, 16)
        DH = H // NH
        EPS = 1e-06

        def rmsnorm(x, w):
            var = jnp.mean(jnp.square(x), axis=-1, keepdims=True)
            return x * jax.lax.rsqrt(var + EPS) * w
        key = jax.random.key(seed)
        ks = jax.random.split(key, 12)
        s = 0.02
        return {'x': jax.random.normal(ks[0], (B, P, H), jnp.float32), 'latents': jax.random.normal(ks[1], (B, K, H), jnp.float32), 'attention_mask': jax.random.randint(ks[2], (B, P), 0, 2, jnp.int32), 'q_w': s * jax.random.normal(ks[3], (H, H), jnp.float32), 'q_b': jnp.zeros((H,), jnp.float32), 'kv_w': s * jax.random.normal(ks[4], (H, 2 * H), jnp.float32), 'kv_b': jnp.zeros((2 * H,), jnp.float32), 'out_w': s * jax.random.normal(ks[5], (H, H), jnp.float32), 'out_b': jnp.zeros((H,), jnp.float32), 'postnorm_w': jnp.ones((H,), jnp.float32), 'mlp_w1': s * jax.random.normal(ks[6], (H, 4 * H), jnp.float32), 'mlp_b1': jnp.zeros((4 * H,), jnp.float32), 'mlp_w2': s * jax.random.normal(ks[7], (4 * H, H), jnp.float32), 'mlp_b2': jnp.zeros((H,), jnp.float32)}
    _L2_xattn_all = _L2_xattn_setup()
    _L2_xattn_in = {k: v for k, v in _L2_xattn_all.items() if k in ('q_w', 'q_b', 'kv_w', 'kv_b', 'out_w', 'out_b', 'postnorm_w', 'mlp_w1', 'mlp_b1', 'mlp_w2', 'mlp_b2')}
    del _L2_xattn_all

    def _L3_xattn_setup():
        import jax, jax.numpy as jnp
        import numpy as np
        E, H, L, B = (256, 32, 128, 4)
        S = E // H
        DM, DD = (32, 64)

        def _ln(x, w, b, eps=1e-05):
            m = x.mean(-1, keepdims=True)
            v = ((x - m) ** 2).mean(-1, keepdims=True)
            return (x - m) / jnp.sqrt(v + eps) * w + b

        def _block(x, state, ln1_w, ln1_b, ln2_w, ln2_b, maa_x, maa_w1, maa_w2, maa_stack, time_decay, td_w1, td_w2, u, Wr, Wk, Wv, Wg, Wo, gn_w, gn_b, ffn_maa_k, ffn_maa_r, Wfk, Wfr, Wfv):
            b, l, e = x.shape
            h = u.shape[0]
            s_ = e // h
            xa = _ln(x, ln1_w, ln1_b)
            sx = jnp.concatenate([state[:, 1:2] - xa[:, :1], xa[:, :-1] - xa[:, 1:]], axis=1)
            xxx = jnp.tanh((xa + sx * maa_x) @ maa_w1).reshape(b, l, 5, DM)
            xxx = jnp.einsum('blfd,fde->blfe', xxx, maa_w2)
            xm = xa[:, :, None] + sx[:, :, None] * (maa_stack + xxx)
            xk, xw, xv, xr, xg = (xm[:, :, j] for j in range(5))
            w = jnp.exp(-jnp.exp(time_decay + jnp.tanh(xw @ td_w1) @ td_w2)).reshape(b, l, h, s_)
            r = (xr @ Wr.T).reshape(b, l, h, s_)
            k = (xk @ Wk.T).reshape(b, l, h, s_)
            v = (xv @ Wv.T).reshape(b, l, h, s_)
            g = jax.nn.silu(xg @ Wg.T)
            s0 = state[:, 2:2 + s_].reshape(b, h, s_, s_)

            def step(s, rkvw):
                r_t, k_t, v_t, w_t = rkvw
                a = k_t[..., :, None] * v_t[..., None, :]
                out = jnp.einsum('bhi,bhij->bhj', r_t, u * a + s)
                s = a + w_t[..., :, None] * s
                return (s, out)
            rkvw = tuple((jnp.moveaxis(t, 1, 0) for t in (r, k, v, w)))
            _, out = jax.lax.scan(step, s0, rkvw)
            out = jnp.moveaxis(out, 0, 1).reshape(b, l, e)
            og = out.reshape(b, l, h, s_)
            m = og.mean(-1, keepdims=True)
            va = ((og - m) ** 2).mean(-1, keepdims=True)
            og = ((og - m) / jnp.sqrt(va + 1e-05)).reshape(b, l, e) * gn_w + gn_b
            x1 = x + og * g @ Wo.T
            xc = _ln(x1, ln2_w, ln2_b)
            sx2 = jnp.concatenate([state[:, 0:1] - xc[:, :1], xc[:, :-1] - xc[:, 1:]], axis=1)
            xk2 = xc + sx2 * ffn_maa_k
            xr2 = xc + sx2 * ffn_maa_r
            rr = jax.nn.sigmoid(xr2 @ Wfr.T)
            kk = jnp.square(jax.nn.relu(xk2 @ Wfk.T))
            return x1 + rr * (kk @ Wfv.T)
        key = jax.random.key(seed)
        ks = jax.random.split(key, 24)
        sc = 0.02
        d = {'x': jax.random.normal(ks[0], (B, L, E), jnp.float32), 'state': jax.random.normal(ks[1], (B, 2 + S, E), jnp.float32) * 0.1, 'ln1_w': jnp.ones((E,), jnp.float32), 'ln1_b': jnp.zeros((E,), jnp.float32), 'ln2_w': jnp.ones((E,), jnp.float32), 'ln2_b': jnp.zeros((E,), jnp.float32), 'maa_x': jax.random.normal(ks[2], (E,), jnp.float32) * 0.1, 'maa_w1': jax.random.normal(ks[3], (E, 5 * DM), jnp.float32) * sc, 'maa_w2': jax.random.normal(ks[4], (5, DM, E), jnp.float32) * sc, 'maa_stack': jax.random.normal(ks[5], (1, 5, E), jnp.float32) * 0.1, 'time_decay': jax.random.normal(ks[6], (E,), jnp.float32) * 0.5, 'td_w1': jax.random.normal(ks[7], (E, DD), jnp.float32) * sc, 'td_w2': jax.random.normal(ks[8], (DD, E), jnp.float32) * sc, 'u': jax.random.normal(ks[9], (H, S, 1), jnp.float32) * 0.1, 'Wr': jax.random.normal(ks[10], (E, E), jnp.float32) * sc, 'Wk': jax.random.normal(ks[11], (E, E), jnp.float32) * sc, 'Wv': jax.random.normal(ks[12], (E, E), jnp.float32) * sc, 'Wg': jax.random.normal(ks[13], (E, E), jnp.float32) * sc, 'Wo': jax.random.normal(ks[14], (E, E), jnp.float32) * sc, 'gn_w': jnp.ones((E,), jnp.float32), 'gn_b': jnp.zeros((E,), jnp.float32), 'ffn_maa_k': jax.random.normal(ks[15], (E,), jnp.float32) * 0.1, 'ffn_maa_r': jax.random.normal(ks[16], (E,), jnp.float32) * 0.1, 'Wfk': jax.random.normal(ks[17], (E, E), jnp.float32) * sc, 'Wfr': jax.random.normal(ks[18], (E, E), jnp.float32) * sc, 'Wfv': jax.random.normal(ks[19], (E, E), jnp.float32) * sc}
        return d
    _L3_xattn_all = _L3_xattn_setup()
    _L3_xattn_in = {k: v for k, v in _L3_xattn_all.items() if k in ('ln1_w', 'ln1_b', 'ln2_w', 'ln2_b', 'maa_x', 'maa_w1', 'maa_w2', 'maa_stack', 'time_decay', 'td_w1', 'td_w2', 'u', 'Wr', 'Wk', 'Wv', 'Wg', 'Wo', 'gn_w', 'gn_b', 'ffn_maa_k', 'ffn_maa_r', 'Wfk', 'Wfr', 'Wfv')}
    del _L3_xattn_all
    return {'x': x, 'ctx_2048': ctx_2048, 'mask_Bx1xSxS2_ff0': mask_Bx1xSxS2_ff0, 'mask_BxS2_ik0': mask_BxS2_ik0, 'L0_xattn_Wn': _L0_xattn_in['Wn'], 'L0_xattn_bn': _L0_xattn_in['bn'], 'L0_xattn_Wm': _L0_xattn_in['Wm'], 'L0_xattn_bm': _L0_xattn_in['bm'], 'L0_xattn_Wl': _L0_xattn_in['Wl'], 'L0_xattn_bl': _L0_xattn_in['bl'], 'L0_xattn_Wo': _L0_xattn_in['Wo'], 'L0_xattn_bo': _L0_xattn_in['bo'], 'L1_xattn_Wq': _L1_xattn_in['Wq'], 'L1_xattn_bq': _L1_xattn_in['bq'], 'L1_xattn_Wk': _L1_xattn_in['Wk'], 'L1_xattn_bk': _L1_xattn_in['bk'], 'L1_xattn_Wv': _L1_xattn_in['Wv'], 'L1_xattn_bv': _L1_xattn_in['bv'], 'L1_xattn_Wo': _L1_xattn_in['Wo'], 'L1_xattn_bo': _L1_xattn_in['bo'], 'L1_xattn_gamma': _L1_xattn_in['gamma'], 'L1_xattn_beta': _L1_xattn_in['beta'], 'L2_xattn_q_w': _L2_xattn_in['q_w'], 'L2_xattn_q_b': _L2_xattn_in['q_b'], 'L2_xattn_kv_w': _L2_xattn_in['kv_w'], 'L2_xattn_kv_b': _L2_xattn_in['kv_b'], 'L2_xattn_out_w': _L2_xattn_in['out_w'], 'L2_xattn_out_b': _L2_xattn_in['out_b'], 'L2_xattn_postnorm_w': _L2_xattn_in['postnorm_w'], 'L2_xattn_mlp_w1': _L2_xattn_in['mlp_w1'], 'L2_xattn_mlp_b1': _L2_xattn_in['mlp_b1'], 'L2_xattn_mlp_w2': _L2_xattn_in['mlp_w2'], 'L2_xattn_mlp_b2': _L2_xattn_in['mlp_b2'], 'L3_xattn_ln1_w': _L3_xattn_in['ln1_w'], 'L3_xattn_ln1_b': _L3_xattn_in['ln1_b'], 'L3_xattn_ln2_w': _L3_xattn_in['ln2_w'], 'L3_xattn_ln2_b': _L3_xattn_in['ln2_b'], 'L3_xattn_maa_x': _L3_xattn_in['maa_x'], 'L3_xattn_maa_w1': _L3_xattn_in['maa_w1'], 'L3_xattn_maa_w2': _L3_xattn_in['maa_w2'], 'L3_xattn_maa_stack': _L3_xattn_in['maa_stack'], 'L3_xattn_time_decay': _L3_xattn_in['time_decay'], 'L3_xattn_td_w1': _L3_xattn_in['td_w1'], 'L3_xattn_td_w2': _L3_xattn_in['td_w2'], 'L3_xattn_u': _L3_xattn_in['u'], 'L3_xattn_Wr': _L3_xattn_in['Wr'], 'L3_xattn_Wk': _L3_xattn_in['Wk'], 'L3_xattn_Wv': _L3_xattn_in['Wv'], 'L3_xattn_Wg': _L3_xattn_in['Wg'], 'L3_xattn_Wo': _L3_xattn_in['Wo'], 'L3_xattn_gn_w': _L3_xattn_in['gn_w'], 'L3_xattn_gn_b': _L3_xattn_in['gn_b'], 'L3_xattn_ffn_maa_k': _L3_xattn_in['ffn_maa_k'], 'L3_xattn_ffn_maa_r': _L3_xattn_in['ffn_maa_r'], 'L3_xattn_Wfk': _L3_xattn_in['Wfk'], 'L3_xattn_Wfr': _L3_xattn_in['Wfr'], 'L3_xattn_Wfv': _L3_xattn_in['Wfv']}

def reference(x, ctx_2048, mask_Bx1xSxS2_ff0, mask_BxS2_ik0, L0_xattn_Wn, L0_xattn_bn, L0_xattn_Wm, L0_xattn_bm, L0_xattn_Wl, L0_xattn_bl, L0_xattn_Wo, L0_xattn_bo, L1_xattn_Wq, L1_xattn_bq, L1_xattn_Wk, L1_xattn_bk, L1_xattn_Wv, L1_xattn_bv, L1_xattn_Wo, L1_xattn_bo, L1_xattn_gamma, L1_xattn_beta, L2_xattn_q_w, L2_xattn_q_b, L2_xattn_kv_w, L2_xattn_kv_b, L2_xattn_out_w, L2_xattn_out_b, L2_xattn_postnorm_w, L2_xattn_mlp_w1, L2_xattn_mlp_b1, L2_xattn_mlp_w2, L2_xattn_mlp_b2, L3_xattn_ln1_w, L3_xattn_ln1_b, L3_xattn_ln2_w, L3_xattn_ln2_b, L3_xattn_maa_x, L3_xattn_maa_w1, L3_xattn_maa_w2, L3_xattn_maa_stack, L3_xattn_time_decay, L3_xattn_td_w1, L3_xattn_td_w2, L3_xattn_u, L3_xattn_Wr, L3_xattn_Wk, L3_xattn_Wv, L3_xattn_Wg, L3_xattn_Wo, L3_xattn_gn_w, L3_xattn_gn_b, L3_xattn_ffn_maa_k, L3_xattn_ffn_maa_r, L3_xattn_Wfk, L3_xattn_Wfr, L3_xattn_Wfv):
    import jax
    import jax.numpy as jnp

    def _L0_xattn_ref(x_c, x_s, Wn, bn, Wm, bm, Wl, bl, Wo, bo):
        import jax, jax.numpy as jnp
        import numpy as np
        EPS = 1e-05

        def _inorm(x):
            m = jnp.mean(x, axis=-1, keepdims=True)
            v = jnp.var(x, axis=-1, keepdims=True)
            return (x - m) * jax.lax.rsqrt(v + EPS)

        def _conv1x1(W, b, x):
            return jnp.einsum('oc,bct->bot', W, x) + b[None, :, None]
        Mn = _conv1x1(Wn, bn, _inorm(x_c))
        Mm = _conv1x1(Wm, bm, _inorm(x_s))
        A = jax.nn.softmax(jnp.einsum('bct,bcs->bts', Mn, Mm), axis=-1)
        Ml = _conv1x1(Wl, bl, x_s)
        Mo = jnp.einsum('bcs,bts->bct', Ml, A)
        return _conv1x1(Wo, bo, Mo) + x_c

    def _L1_xattn_ref(hidden_state, encoder_hidden_state, encoder_attention_mask, Wq, bq, Wk, bk, Wv, bv, Wo, bo, gamma, beta):
        import jax, jax.numpy as jnp
        import numpy as np
        H = 256
        NH = 32
        KVH = 8
        HD = H // NH
        GROUPS = NH // KVH
        EPS = 1e-06
        B, L, S = (4, 128, 128)

        def _gqa_forward(hidden_state, encoder_hidden_state, encoder_attention_mask, Wq, bq, Wk, bk, Wv, bv, Wo, bo, gamma, beta):
            b, l, _ = hidden_state.shape
            s = encoder_hidden_state.shape[1]
            q = hidden_state @ Wq + bq
            k = encoder_hidden_state @ Wk + bk
            v = encoder_hidden_state @ Wv + bv
            q = q.reshape(b, l, KVH, GROUPS, HD).transpose(0, 2, 3, 1, 4)
            k = k.reshape(b, s, KVH, HD).transpose(0, 2, 1, 3)
            v = v.reshape(b, s, KVH, HD).transpose(0, 2, 1, 3)
            scale = 1.0 / jnp.sqrt(jnp.asarray(HD, q.dtype))
            scores = jnp.einsum('bkgld,bksd->bkgls', q, k) * scale
            scores = scores + encoder_attention_mask[:, :, None, :, :]
            attn = jax.nn.softmax(scores, axis=-1)
            out = jnp.einsum('bkgls,bksd->bkgld', attn, v)
            out = out.transpose(0, 3, 1, 2, 4).reshape(b, l, H)
            out = out @ Wo + bo
            x = out + hidden_state
            mu = jnp.mean(x, axis=-1, keepdims=True)
            var = jnp.var(x, axis=-1, keepdims=True)
            return (x - mu) * jax.lax.rsqrt(var + EPS) * gamma + beta
        return _gqa_forward(hidden_state, encoder_hidden_state, encoder_attention_mask, Wq, bq, Wk, bk, Wv, bv, Wo, bo, gamma, beta)

    def _L2_xattn_ref(x, latents, attention_mask, q_w, q_b, kv_w, kv_b, out_w, out_b, postnorm_w, mlp_w1, mlp_b1, mlp_w2, mlp_b2):
        import jax, jax.numpy as jnp
        import numpy as np
        B, P, K, H, NH = (4, 256, 32, 256, 16)
        DH = H // NH
        EPS = 1e-06

        def rmsnorm(x, w):
            var = jnp.mean(jnp.square(x), axis=-1, keepdims=True)
            return x * jax.lax.rsqrt(var + EPS) * w
        b, p, _ = x.shape
        k_len = latents.shape[1]
        residual = latents
        h = jnp.concatenate([x, latents], axis=1)
        q = (latents @ q_w + q_b).reshape(b, k_len, NH, DH)
        kv = (h @ kv_w + kv_b).reshape(b, p + k_len, NH, DH, 2)
        kmat, v = (kv[..., 0], kv[..., 1])
        attn = jnp.einsum('bkhd,bnhd->bhkn', q, kmat) / DH
        full_mask = jnp.concatenate([attention_mask.astype(bool), jnp.ones((b, k_len), bool)], axis=-1)
        attn = jnp.where(full_mask[:, None, None, :], attn, -jnp.inf)
        attn = jax.nn.softmax(attn.astype(jnp.float32), axis=-1).astype(q.dtype)
        attn_out = jnp.einsum('bhkn,bnhd->bkhd', attn, v).reshape(b, k_len, H)
        attn_out = attn_out @ out_w + out_b + residual
        out = rmsnorm(attn_out, postnorm_w)
        out = jax.nn.gelu(out @ mlp_w1 + mlp_b1) @ mlp_w2 + mlp_b2
        return out + residual

    def _L3_xattn_ref(x, state, ln1_w, ln1_b, ln2_w, ln2_b, maa_x, maa_w1, maa_w2, maa_stack, time_decay, td_w1, td_w2, u, Wr, Wk, Wv, Wg, Wo, gn_w, gn_b, ffn_maa_k, ffn_maa_r, Wfk, Wfr, Wfv):
        import jax, jax.numpy as jnp
        import numpy as np
        E, H, L, B = (256, 32, 128, 4)
        S = E // H
        DM, DD = (32, 64)

        def _ln(x, w, b, eps=1e-05):
            m = x.mean(-1, keepdims=True)
            v = ((x - m) ** 2).mean(-1, keepdims=True)
            return (x - m) / jnp.sqrt(v + eps) * w + b

        def _block(x, state, ln1_w, ln1_b, ln2_w, ln2_b, maa_x, maa_w1, maa_w2, maa_stack, time_decay, td_w1, td_w2, u, Wr, Wk, Wv, Wg, Wo, gn_w, gn_b, ffn_maa_k, ffn_maa_r, Wfk, Wfr, Wfv):
            b, l, e = x.shape
            h = u.shape[0]
            s_ = e // h
            xa = _ln(x, ln1_w, ln1_b)
            sx = jnp.concatenate([state[:, 1:2] - xa[:, :1], xa[:, :-1] - xa[:, 1:]], axis=1)
            xxx = jnp.tanh((xa + sx * maa_x) @ maa_w1).reshape(b, l, 5, DM)
            xxx = jnp.einsum('blfd,fde->blfe', xxx, maa_w2)
            xm = xa[:, :, None] + sx[:, :, None] * (maa_stack + xxx)
            xk, xw, xv, xr, xg = (xm[:, :, j] for j in range(5))
            w = jnp.exp(-jnp.exp(time_decay + jnp.tanh(xw @ td_w1) @ td_w2)).reshape(b, l, h, s_)
            r = (xr @ Wr.T).reshape(b, l, h, s_)
            k = (xk @ Wk.T).reshape(b, l, h, s_)
            v = (xv @ Wv.T).reshape(b, l, h, s_)
            g = jax.nn.silu(xg @ Wg.T)
            s0 = state[:, 2:2 + s_].reshape(b, h, s_, s_)

            def step(s, rkvw):
                r_t, k_t, v_t, w_t = rkvw
                a = k_t[..., :, None] * v_t[..., None, :]
                out = jnp.einsum('bhi,bhij->bhj', r_t, u * a + s)
                s = a + w_t[..., :, None] * s
                return (s, out)
            rkvw = tuple((jnp.moveaxis(t, 1, 0) for t in (r, k, v, w)))
            _, out = jax.lax.scan(step, s0, rkvw)
            out = jnp.moveaxis(out, 0, 1).reshape(b, l, e)
            og = out.reshape(b, l, h, s_)
            m = og.mean(-1, keepdims=True)
            va = ((og - m) ** 2).mean(-1, keepdims=True)
            og = ((og - m) / jnp.sqrt(va + 1e-05)).reshape(b, l, e) * gn_w + gn_b
            x1 = x + og * g @ Wo.T
            xc = _ln(x1, ln2_w, ln2_b)
            sx2 = jnp.concatenate([state[:, 0:1] - xc[:, :1], xc[:, :-1] - xc[:, 1:]], axis=1)
            xk2 = xc + sx2 * ffn_maa_k
            xr2 = xc + sx2 * ffn_maa_r
            rr = jax.nn.sigmoid(xr2 @ Wfr.T)
            kk = jnp.square(jax.nn.relu(xk2 @ Wfk.T))
            return x1 + rr * (kk @ Wfv.T)
        return _block(x, state, ln1_w, ln1_b, ln2_w, ln2_b, maa_x, maa_w1, maa_w2, maa_stack, time_decay, td_w1, td_w2, u, Wr, Wk, Wv, Wg, Wo, gn_w, gn_b, ffn_maa_k, ffn_maa_r, Wfk, Wfr, Wfv)
    x = _L0_xattn_ref(x, ctx_2048, L0_xattn_Wn, L0_xattn_bn, L0_xattn_Wm, L0_xattn_bm, L0_xattn_Wl, L0_xattn_bl, L0_xattn_Wo, L0_xattn_bo)
    x = _L1_xattn_ref(x, ctx_2048, mask_Bx1xSxS2_ff0, L1_xattn_Wq, L1_xattn_bq, L1_xattn_Wk, L1_xattn_bk, L1_xattn_Wv, L1_xattn_bv, L1_xattn_Wo, L1_xattn_bo, L1_xattn_gamma, L1_xattn_beta)
    x = _L2_xattn_ref(ctx_2048, x, mask_BxS2_ik0, L2_xattn_q_w, L2_xattn_q_b, L2_xattn_kv_w, L2_xattn_kv_b, L2_xattn_out_w, L2_xattn_out_b, L2_xattn_postnorm_w, L2_xattn_mlp_w1, L2_xattn_mlp_b1, L2_xattn_mlp_w2, L2_xattn_mlp_b2)
    x = _L3_xattn_ref(x, ctx_2048, L3_xattn_ln1_w, L3_xattn_ln1_b, L3_xattn_ln2_w, L3_xattn_ln2_b, L3_xattn_maa_x, L3_xattn_maa_w1, L3_xattn_maa_w2, L3_xattn_maa_stack, L3_xattn_time_decay, L3_xattn_td_w1, L3_xattn_td_w2, L3_xattn_u, L3_xattn_Wr, L3_xattn_Wk, L3_xattn_Wv, L3_xattn_Wg, L3_xattn_Wo, L3_xattn_gn_w, L3_xattn_gn_b, L3_xattn_ffn_maa_k, L3_xattn_ffn_maa_r, L3_xattn_Wfk, L3_xattn_Wfr, L3_xattn_Wfv)
    return x

_drawn_inputs = setup_inputs


def setup_inputs(seed=0):
    import zlib

    import numpy as np

    out = dict(_drawn_inputs(seed))
    spreads = {'L1_xattn_bq': (0.0, 0.8),
     'L1_xattn_bk': (0.0, 0.8),
     'L1_xattn_bv': (0.0, 0.357),
     'L1_xattn_bo': (0.0, 0.1),
     'L1_xattn_gamma': (1.0, 0.2),
     'L1_xattn_beta': (0.0, 0.1),
     'L2_xattn_q_b': (0.0, 0.8),
     'L2_xattn_kv_b': (0.0, 0.8),
     'L2_xattn_out_b': (0.0, 0.676),
     'L2_xattn_postnorm_w': (1.0, 0.6),
     'L2_xattn_mlp_b1': (0.0, 0.1),
     'L2_xattn_mlp_b2': (0.0, 0.1),
     'L3_xattn_ln1_w': (1.0, 0.536),
     'L3_xattn_ln1_b': (0.0, 0.548),
     'L3_xattn_ln2_w': (1.0, 0.6),
     'L3_xattn_ln2_b': (0.0, 0.8),
     'L3_xattn_gn_w': (1.0, 0.6),
     'L3_xattn_gn_b': (0.0, 0.8)}
    factors = {'L0_xattn_bm': 8.0,
     'L0_xattn_bl': 8.0,
     'L0_xattn_bo': 8.0,
     'L1_xattn_Wq': 8.0,
     'L1_xattn_Wk': 8.0,
     'L2_xattn_q_w': 8.0,
     'L2_xattn_kv_w': 8.0,
     'L2_xattn_out_w': 8.0,
     'L3_xattn_maa_x': 8.0,
     'L3_xattn_maa_w1': 7.257,
     'L3_xattn_maa_w2': 7.262,
     'L3_xattn_maa_stack': 2.704,
     'L3_xattn_td_w1': 8.0,
     'L3_xattn_td_w2': 8.0,
     'L3_xattn_u': 5.699,
     'L3_xattn_ffn_maa_k': 8.0,
     'L3_xattn_ffn_maa_r': 8.0,
     'L3_xattn_Wfk': 2.776,
     'L3_xattn_Wfr': 8.0}
    for name, (base, spread) in spreads.items():
        noise = np.random.default_rng([zlib.crc32(name.encode()), seed]).standard_normal(out[name].shape)
        drawn = base * np.exp(spread * noise) if base else spread * noise
        out[name] = jnp.asarray(drawn.astype(out[name].dtype))
    for name, factor in factors.items():
        out[name] = (out[name] * factor).astype(out[name].dtype)
    return out
```

```python
from contextlib import ExitStack

import concourse.bass as bass
from concourse import mybir
from concourse.alu_op_type import AluOpType as ALU

F32 = mybir.dt.float32
I32 = mybir.dt.int32
ACT = mybir.ActivationFunctionType
X = mybir.AxisListType.X

B, L, E = 64, 64, 256
NB = 8
NP = NB // 2
GROUPS = B // NB
TOK = NB * L
KT = E // 128
KVH, GQ, HD1 = 8, 4, 8
HD2, KEYS = 16, 2 * L
HPT = 128 // HD2
HID = 4 * E
HS = 8
NMIX, DM, DD = 5, 32, 64
LP = L + 1
MASKED = -1.0e30


def _vector_rows():
    rows, at = {}, 0
    for name, n in (("bn", 1), ("bm", 1), ("bl", 1), ("bo", 1), ("bq", GQ), ("bk", 1), ("bv", 1),
                    ("gamma", 2), ("beta", 2), ("q_b", 2), ("k_b", 2), ("v_b", 2), ("post", 2), ("b1", HID // 128),
                    ("ln1_w", 2), ("ln1_b", 2), ("ln2_w", 2), ("ln2_b", 2), ("maa_x", 2), ("maa", 2 * NMIX),
                    ("decay", 2), ("u", 2), ("gn_w", 2), ("gn_b", 2), ("ffn_k", 2), ("ffn_r", 2)):
        rows[name] = (at, n)
        at += n
    return rows, at


def build(nc, a, out, debug=None):
    with ExitStack() as ctx:
        def sb(name, shape, dt=F32):
            return ctx.enter_context(nc.sbuf_tensor(name, shape, dt))

        sems = {}

        def sig(name):
            if name not in sems:
                sems[name] = ctx.enter_context(nc.semaphore(name))
            return sems[name]

        banks = [ctx.enter_context(nc.psum_tensor(f"bank{i}", [128, 512], F32)) for i in range(8)]
        RINGS = {"score": [0, 1], "turn": [2, 3], "value": [4], "total": [5], "dense": [6, 7]}
        turns, fills, place = {}, {}, {}

        def new_block():
            turns.clear()
            fills.clear()
            place.clear()

        def fill(pe, ring, tile):
            b = RINGS[ring][turns.get(ring, 0) % len(RINGS[ring])]
            turns[ring] = turns.get(ring, 0) + 1
            n = fills.get(b, 0)
            if n:
                pe.wait_ge(sig(f"bank{b}_free"), n)
            fills[b] = n + 1
            place[tile] = (b, n + 1)
            return banks[b], sig(f"bank{b}_full")

        def take(eng, tile):
            b, n = place[tile]
            eng.wait_ge(sig(f"bank{b}_full"), n)
            return banks[b], sig(f"bank{b}_free")

        def linker(eng, name):
            count = [0]

            def link(ins):
                count[0] += 1
                ins.then_inc(sig(name), 1)
                eng.wait_ge(sig(name), count[0])
            return link

        ident = sb("ident", [128, 128])
        block8 = sb("block8", [128, 16, 8])
        center8 = sb("center8", [128, 128])
        pick = sb("pick", [128, HS, 128])
        kvmask = sb("kvmask", [128, KVH])
        hmask = sb("hmask", [128, HPT])
        parity = sb("parity", [128, 2])
        half = sb("half", [128, 2, 8])
        ones2 = sb("ones2", [128, 32])
        ones32 = sb("ones32", [128, 32])
        eps5 = sb("eps5", [128, 1])
        eps6 = sb("eps6", [128, 1])
        ROWS, NROWS = _vector_rows()
        vrows = sb("vrows", [128, 128])
        vec = sb("vec", [128, 128])

        def v(name, n=0):
            return vec[:, ROWS[name][0] + n:ROWS[name][0] + n + 1]

        conv = {w: sb(f"conv_{w}", [128, 128]) for w in ("Wn", "Wm", "Wl", "Wo")}
        wq1 = sb("wq1", [128, KT, GQ, 64])
        wk1 = sb("wk1", [128, KT, KVH * HD1])
        wv1 = sb("wv1", [128, KT, KVH * HD1])
        wo1 = sb("wo1", [128, GQ, E])
        wq2 = sb("wq2", [128, KT, E])
        wkv2 = sb("wkv2", [128, KT, 2 * E])
        wo2 = sb("wo2", [128, KT, 2, E])
        w1 = sb("w1", [128, KT, HID])
        w2 = sb("w2", [128, HID // 128, E])
        maa1 = sb("maa1", [128, KT, NMIX * DM])
        maa2 = sb("maa2", [128, NMIX, E])
        td1 = sb("td1", [128, KT, DD])
        td2 = sb("td2", [128, E])
        SQUARE = ("Wr", "Wk", "Wv", "Wg", "Wo", "Wfk", "Wfr", "Wfv")
        wt = {w: sb(f"t_{w}", [128, KT, E]) for w in SQUARE}
        row1 = sb("row1", [128, E])
        row2 = sb("row2", [128, E])
        row_b2 = sb("row_b2", [128, E])
        row_gamma = sb("row_gamma", [128, E])
        row_beta = sb("row_beta", [128, E])

        x0 = sb("x0", [128, NP, E])
        c0 = sb("c0", [128, NP, E])
        mask1 = sb("mask1", [128, NP, L])
        imask = sb("imask", [128, NB, L], I32)
        mask2 = sb("mask2", [128, NB, KEYS])
        s0 = sb("s0", [128, KT, NB, HS])
        hT = sb("hT", [128, KT, NB, 2, L])
        stats = sb("stats", [128, 2 * NP, 6])
        mv = sb("mv", [128, 2 * NP, 2])
        rstd = sb("rstd", [128, 2 * NP])
        xA = sb("xA", [128, NP, E])
        xB = sb("xB", [128, NP, E])
        xh = sb("xh", [128, NP, E])
        xr = sb("xr", [128, NP, E])

        A = sb("A", [128, 4096])
        C = sb("C", [128, 4096])
        D = sb("D", [128, 4096])
        F = sb("F", [128, 2048])
        G = sb("G", [128, 2112])
        soft_mem = sb("soft_mem", [128, 2048])
        qring = sb("qring", [128, 2, HPT, L])
        seg_max = sb("seg_max", [128, 4, 8])
        over = sb("over", [128, 2, 512])
        den0 = sb("den0", [128, 2 * NP, 2])
        rden0 = sb("rden0", [128, 2 * NP, 2])
        nmax0 = sb("nmax0", [128, 2 * NP, 2])

        def lhsT_cols(ap):
            n = 1
            for size in ap.shape[1:]:
                n *= size
            return n

        def cut(t, at, *shape):
            n = 1
            for s in shape:
                n *= s
            flat = t[:, at:at + n]
            if len(shape) == 1:
                return flat
            names = "abcde"[:len(shape)]
            return flat.rearrange(f"p ({' '.join(names)}) -> p {' '.join(names)}",
                                  **{k: s for k, s in zip(names, shape)})

        soft = cut(soft_mem, 0, 4, 512)
        ch = cut(A, 0, NP, E)
        mn = cut(A, 1024, NP, E)
        mlT = cut(A, 2048, NP, 2, 128)
        mo = cut(A, 3072, NP, E)
        mmb = cut(C, 0, NP, 2, E)
        pT0 = cut(D, 0, 2, 2, 2, 2, 128)
        x1T = cut(F, 0, KT, TOK)
        qz = cut(D, 2048, GQ, NP, 2, L)
        kbd = cut(A, 2048, NP, KVH, L)
        kT1 = cut(F, 1024, NP, L)
        vbd = sb("vbd", [128, NB, 4, 32])
        pT1 = cut(C, 0, 2, 4, 2, GQ, L)
        at1 = cut(D, 0, 2, GQ, 2 * L)
        k2T = cut(A, 0, KT, NB, KEYS)
        q2T = cut(A, 2048, KT, NB, L)
        v2 = cut(D, 1024, NB, E)
        pT2 = cut(C, 0, 4, KT, 512)
        at2 = cut(D, 3072, 2, 4, 2 * L)
        xnT = cut(F, 0, KT, TOK)
        gT = cut(C, 0, HID // 128, TOK)
        PT = NB * LP
        xaP = cut(A, 0, KT, NB, LP)
        sx = cut(A, 1040, KT, TOK)
        xf = sb("xf", [128, 2, TOK])
        xm = cut(C, 0, 2, KT, TOK)
        mtmp = cut(C, 2048, 2, TOK)
        tdT = sb("tdT", [128, TOK])
        decay = cut(C, 3072, 2, TOK)
        kP = cut(soft_mem, 0, KT, NB, LP)
        vP = sb("vP", [128, KT, NB, LP])
        wP = cut(A, 2064, KT, NB, LP)
        rT = cut(F, 0, KT, TOK)
        gg = cut(F, 1024, KT, TOK)
        vj = cut(D, 0, 4, PT)
        aj = cut(D, 4 * PT, 3, PT)
        sj = cut(G, 0, 2, PT)
        rs = cut(G, 2 * PT, 2, 512)
        oT = cut(C, 0, KT, TOK)
        sq = cut(C, 1024, KT, TOK)
        ogT = cut(C, 2048, KT, TOK)
        xcP = cut(A, 0, KT, NB, LP)
        xk2 = cut(C, 0, KT, TOK)
        xr2 = cut(C, 1024, KT, TOK)
        kkT = cut(C, 2048, KT, TOK)
        thn = cut(D, 0, NP, E)

        def nat(name):
            return a[name].rearrange("b c t -> (b c) t").rearrange("(n p q) t -> n q p t", p=NP, q=128)
        x_in, c_in = nat("x"), nat("ctx_2048")
        out_v = out.rearrange("b c t -> (b c) t").rearrange("(n p q) t -> n q p t", p=NP, q=128)
        mask1_in = a["mask_Bx1xSxS2_ff0"].rearrange("b o l s -> (b o l) s").rearrange(
            "(n p q) s -> n q p s", p=NP, q=128)
        mask2_in = a["mask_BxS2_ik0"].rearrange("(n b) s -> n b s", b=NB)
        s0_in = a["ctx_2048"].rearrange("b c t -> b (c t)")[:, 2 * E:2 * E + HS * E].rearrange(
            "(n b) (k p j) -> n k p b j", b=NB, k=KT, j=HS)

        new_block()
        with nc.Block() as block:
            @block.gpsimd
            def _(pool):
                link = linker(pool, "pool_step")
                link(nc.gpsimd.memset(vrows[:, :], 0.0))
                for w in conv.values():
                    nc.gpsimd.memset(w[:, :], 0.0)
                for t in (wo1, maa2, td2, vbd, xf, tdT, vP, pick):
                    nc.gpsimd.memset(t[:, :] if len(t.shape) == 2 else t[tuple([slice(None)] * len(t.shape))], 0.0)
                nc.gpsimd.memset(eps5[:, :], 1e-5)
                nc.gpsimd.memset(eps6[:, :], 1e-6)
                nc.gpsimd.memset(ones32[:, :], 1.0)
                nc.gpsimd.memset(ones2[:, :], 1.0)
                link(nc.gpsimd.memset(mask2[:, :, :], 0.0))
                pool.sem_inc(sig("zeroed"), 1)

                def band(t, shape, step, width):
                    pattern = [[-step, shape[0]]] + ([[0, shape[1]]] if len(shape) > 1 else [])
                    up = [[step, shape[0]]] + ([[0, shape[1]]] if len(shape) > 1 else [])
                    link(nc.gpsimd.memset(t, 1.0))
                    link(nc.gpsimd.affine_select(out=t, in_=t, compare_op=ALU.is_ge, fill=0.0, base=0,
                                                 pattern=pattern, channel_multiplier=1))
                    link(nc.gpsimd.affine_select(out=t, in_=t, compare_op=ALU.is_ge, fill=0.0, base=width - 1,
                                                 pattern=up, channel_multiplier=-1))
                band(block8[:, :, :], (16, 8), 8, 8)
                band(hmask[:, :], (HPT,), HD2, HD2)
                band(half[:, :, :], (2, 8), 64, 64)
                band(ident[:, :], (128,), 1, 1)
                pool.sem_inc(sig("bands"), 1)

            @block.sync
            def _(sp):
                sp.wait_ge(sig("zeroed"), 1)
                for w in conv:
                    for h in range(2):
                        sp.dma_start(conv[w][64 * h:64 * h + 64, 64 * h:64 * h + 64], a[f"L0_xattn_{w}"]).then_inc(sig("conv_in"), 16)
                L3 = "L3_xattn_"
                srcs = [("gamma", "L1_xattn_gamma"), ("beta", "L1_xattn_beta"), ("q_b", "L2_xattn_q_b"),
                        ("post", "L2_xattn_postnorm_w"), ("b1", "L2_xattn_mlp_b1"), ("ln1_w", L3 + "ln1_w"),
                        ("ln1_b", L3 + "ln1_b"), ("ln2_w", L3 + "ln2_w"), ("ln2_b", L3 + "ln2_b"),
                        ("maa_x", L3 + "maa_x"), ("decay", L3 + "time_decay"), ("gn_w", L3 + "gn_w"),
                        ("gn_b", L3 + "gn_b"), ("ffn_k", L3 + "ffn_maa_k"), ("ffn_r", L3 + "ffn_maa_r")]
                for row, name in srcs:
                    r, n = ROWS[row]
                    sp.dma_start(vrows[r:r + n, :], a[name].rearrange("(n p) -> n p", p=128)).then_inc(sig("rows_in"), 16)
                r, n = ROWS["maa"]
                sp.dma_start(vrows[r:r + n, :], a[L3 + "maa_stack"].rearrange("o f (n p) -> (o f n) p", p=128)).then_inc(sig("rows_in"), 16)
                r, n = ROWS["u"]
                sp.dma_start(vrows[r:r + n, :], a[L3 + "u"].rearrange("h s o -> (h s o)").rearrange("(n p) -> n p", p=128)).then_inc(sig("rows_in"), 16)
                for h in range(2):
                    for row, name in (("bn", "L0_xattn_bn"), ("bm", "L0_xattn_bm"), ("bl", "L0_xattn_bl"),
                                      ("bo", "L0_xattn_bo"), ("bk", "L1_xattn_bk")):
                        r = ROWS[row][0]
                        sp.dma_start(vrows[r:r + 1, 64 * h:64 * h + 64], a[name].rearrange("(o c) -> o c", o=1)).then_inc(sig("rows_in"), 16)
                    r = ROWS["bq"][0]
                    for g in range(GQ):
                        sp.dma_start(vrows[r + g:r + g + 1, 64 * h:64 * h + 64].rearrange("o (k d) -> o k d", d=HD1),
                                     a["L1_xattn_bq"].rearrange("(o k g d) -> g o k d", o=1, g=GQ, d=HD1)[g]).then_inc(sig("rows_in"), 16)
                r = ROWS["bv"][0]
                sp.dma_start(vrows[r:r + 1, :].rearrange("o (j e) -> o j e", e=32)[:, :, 0:16],
                             a["L1_xattn_bv"].rearrange("(o j e) -> o j e", o=1, e=16)).then_inc(sig("rows_in"), 16)
                with nc.allow_non_contiguous_dma(reason="interleaved biases"):
                    for row, s in (("k_b", 0), ("v_b", 1)):
                        r, n = ROWS[row]
                        sp.dma_start(vrows[r:r + n, :].unsqueeze(2),
                                     a["L2_xattn_kv_b"].rearrange("(n p s) -> s n p", p=128, s=2)[s].unsqueeze(2)).then_inc(sig("rows_in"), 16)
                sp.wait_ge(sig("rows_in"), 16 * (len(srcs) + 2 + 10 + 2 * GQ + 1 + 2))
                sp.sem_inc(sig("rows_all"), 1)
                for t, name in ((row1, "L1_xattn_bo"), (row2, "L2_xattn_out_b"), (row_b2, "L2_xattn_mlp_b2"),
                                (row_gamma, "L1_xattn_gamma"), (row_beta, "L1_xattn_beta")):
                    sp.dma_start(t[:, :], a[name].rearrange("(o n) -> o n", o=1).broadcast_to([128, E])).then_inc(sig("spread_in"), 16)
                sp.wait_ge(sig("spread_in"), 80)
                sp.sem_inc(sig("spread_all"), 1)

            @block.scalar
            def _(act):
                act.wait_ge(sig("zeroed"), 1)
                for n, w in enumerate(SQUARE):
                    act.dma_start(cut(A if n < 4 else C, 512 * (n % 4), KT, E), a[f"L3_xattn_{w}"].rearrange("(k p) n -> p k n", p=128)).then_inc(sig("square_in"), 16)
                act.dma_start(D[:, 0:512].rearrange("p (k n) -> p k n", k=KT), a["L2_xattn_out_w"].rearrange("(k p) n -> p k n", p=128)).then_inc(sig("plain_in"), 16)
                for t, name in ((cut(D, 512, KT, E), "L1_xattn_Wq"), (wk1, "L1_xattn_Wk"), (wv1, "L1_xattn_Wv"), (wq2, "L2_xattn_q_w"),
                                (wkv2, "L2_xattn_kv_w"), (w1, "L2_xattn_mlp_w1"), (w2, "L2_xattn_mlp_w2"),
                                (maa1, "L3_xattn_maa_w1"), (td1, "L3_xattn_td_w1")):
                    act.dma_start(t[:, :, :], a[name].rearrange("(k p) n -> p k n", p=128)).then_inc(sig("plain_in"), 16)
                for j in range(4):
                    for k in range(2):
                        act.dma_start(wo1[32 * j + 8 * k:32 * j + 8 * k + 8, :, :],
                                      a["L1_xattn_Wo"].rearrange("(k g d) n -> k d g n", g=GQ, d=HD1)[2 * j + k]).then_inc(sig("plain_in"), 16)
                act.dma_start(maa2[:, 0, :][0:32], a["L3_xattn_maa_w2"][0]).then_inc(sig("plain_in"), 16)
                for f in range(1, NMIX):
                    r = 32 * (f % 4)
                    act.dma_start(maa2[r:r + 32, f, :], a["L3_xattn_maa_w2"][f]).then_inc(sig("plain_in"), 16)
                act.dma_start(td2[0:DD, :], a["L3_xattn_td_w2"]).then_inc(sig("plain_in"), 16)
                act.wait_ge(sig("plain_in"), 16 * (1 + 9 + 8 + 5 + 1))
                act.sem_inc(sig("plain_all"), 1)

            @block.tensor
            def _(pe):
                pe.wait_ge(sig("bands"), 1)
                pe.wait_ge(sig("rows_all"), 1)
                t, full = fill(pe, "dense", "vec")
                nc.tensor.transpose(t[:, 0:128], vrows[:, :], ident[:, :]).then_inc(full, 1)
                pe.wait_ge(sig("conv_in"), 128)
                t, full = fill(pe, "dense", "conv")
                for n, w in enumerate(conv):
                    ins = nc.tensor.transpose(t[:, 128 * n:128 * n + 128], conv[w][:, :], ident[:, :])
                ins.then_inc(full, 1)
                pe.wait_ge(sig("square_in"), 16 * len(SQUARE))
                for n, w in enumerate(SQUARE):
                    t, full = fill(pe, "dense", w)
                    src = cut(A if n < 4 else C, 512 * (n % 4), KT, E)
                    for i in range(KT):
                        for o in range(KT):
                            ins = nc.tensor.transpose(t[:, 256 * i + 128 * o:256 * i + 128 * o + 128],
                                                      src[:, o, 128 * i:128 * i + 128], ident[:, :])
                    ins.then_inc(full, 1)
                pe.wait_ge(sig("plain_all"), 1)
                pe.wait_ge(sig("bias_spread"), 1)
                t, full = fill(pe, "dense", "row1")
                for g in range(GQ):
                    ins = nc.tensor.matmul(t[:, 0:E], cut(G, 0, 3, 128)[:, 0, :], wo1[:, g, :], start=g == 0, stop=g == GQ - 1)
                ins.then_inc(full, 1)
                t, full = fill(pe, "dense", "row2")
                for k in range(KT):
                    ins = nc.tensor.matmul(t[:, 0:E], cut(G, 0, 3, 128)[:, 1 + k, :], cut(D, 0, KT, E)[:, k, :], start=k == 0, stop=k == KT - 1)
                ins.then_inc(full, 1)

            @block.vector
            def _(dve):
                link = linker(dve, "dve_step")
                dve.wait_ge(sig("bands"), 1)
                flat8 = block8[:, :, :].rearrange("p a b -> p (a b)")
                nc.vector.tensor_tensor(kvmask[:, :], block8[:, 0:8, 0], block8[:, 8:16, 0], ALU.add)
                nc.vector.tensor_reduce(parity[:, :], hmask[:, :].rearrange("p (j h) -> p h j", h=2), X, ALU.add)
                nc.vector.tensor_copy(ones2[:, 0:16], half[:, :, :].rearrange("p a b -> p (a b)"))
                link(nc.vector.scalar_tensor_tensor(out=center8[:, :], in0=flat8, scalar=-1.0 / HS, in1=ident[:, :], op0=ALU.mult, op1=ALU.add))
                for j in range(HS):
                    nc.vector.tensor_copy(pick[:, j, :].rearrange("p (h j) -> p h j", j=HS)[:, :, j], block8[:, :, j])
                t, free = take(dve, "vec")
                link(nc.vector.tensor_copy(vec[:, :], t[:, 0:128]))
                dve.sem_inc(free, 1)
                for w in ("gn_w", "gn_b"):
                    r = ROWS[w][0]
                    nc.vector.tensor_scalar(vec[:, r:r + 2], vec[:, r:r + 2], 0.5, None, ALU.mult)
                bias = cut(G, 0, 3, 128)
                for n, col in enumerate((v("bv"), v("v_b", 0), v("v_b", 1))):
                    ins = nc.vector.tensor_copy(bias[:, n, :], col.broadcast_to([128, 128]))
                ins.then_inc(sig("bias_spread"), 1)
                t, free = take(dve, "conv")
                for n, w in enumerate(conv):
                    ins = nc.vector.tensor_copy(conv[w][:, :], t[:, 128 * n:128 * n + 128])
                ins.then_inc(free, 1)
                for w in SQUARE:
                    t, free = take(dve, w)
                    nc.vector.tensor_copy(wt[w][:, :, :].rearrange("p k n -> p (k n)"), t[:, :]).then_inc(free, 1)
                dve.wait_ge(sig("plain_all"), 1)
                for k in range(KT):
                    nc.vector.tensor_copy(wq1[:, k, :, :].rearrange("p g (h d) -> p h g d", d=HD1),
                                          cut(D, 512, KT, KVH, GQ, HD1)[:, k])
                    for h in range(2):
                        nc.vector.tensor_scalar(wo2[:, k, h, :], cut(D, 0, KT, E)[:, k, :], parity[:, h:h + 1], None, ALU.mult)
                dve.wait_ge(sig("spread_all"), 1)
                t, free = take(dve, "row1")
                nc.vector.tensor_tensor(row1[:, :], t[:, 0:E], row1[:, :], ALU.add).then_inc(free, 1)
                t, free = take(dve, "row2")
                nc.vector.tensor_tensor(row2[:, :], t[:, 0:E], row2[:, :], ALU.add).then_inc(free, 1)

        def clear_all():
            nums = sorted(s.num for s in sems.values())
            with nc.Block() as between:
                @between.gpsimd
                def _(pool):
                    lo = nums[0]
                    for n, m in zip(nums, nums[1:] + [None]):
                        if m != n + 1:
                            pool.sem_clear(range(lo, n + 1))
                            lo = m
        stop = 4 if debug is None else debug[0]
        xout = xA if stop in (0, 1) else xB
        clear_all()
        with nc.Fori(0, GROUPS if debug is None else debug[1]) as turn:
            new_block()
            with nc.Block() as block:
                @block.sync
                def _(sp):
                    sp.dma_start(c0[:, :, :], c_in[turn]).then_inc(sig("c0_in"), 16)
                    sp.dma_start(x0[:, :, :], x_in[turn]).then_inc(sig("x0_in"), 16)
                    sp.dma_start(mask1[:, :, :], mask1_in[turn]).then_inc(sig("mask1_in"), 16)
                    sp.dma_start(imask[:, :, :], mask2_in[turn].unsqueeze(0).broadcast_to([128, NB, L])).then_inc(sig("mask2_in"), 16)
                    for k in range(KT):
                        sp.dma_start(s0[:, k, :, :], s0_in[turn][k]).then_inc(sig("s0_in"), 16)
                    if stop < 4:
                        sp.wait_ge(sig("dbg"), 1)
                        sp.dma_start(out_v[turn], xout[:, :, :]).then_inc(sig("stored"), 16)
                        sp.wait_ge(sig("stored"), 16)
                        return
                    for k in range(KT):
                        for j in range(HS):
                            n = HS * k + j
                            sp.wait_ge(sig("vP_ready"), k + 1)
                            if n >= 4:
                                sp.wait_ge(sig("kv_done"), n - 3)
                            src = vP[j::HS, k, :, :].rearrange("h b t -> h (b t)")
                            sp.dma_start(vj[:, n % 4, :], src.unsqueeze(1).broadcast_to([16, HS, PT])).then_inc(sig(f"vj_in{n % 4}"), 16)
                    sp.wait_ge(sig("out_ready"), NP)
                    sp.dma_start(out_v[turn], xr[:, :, :]).then_inc(sig("stored"), 16)
                    sp.wait_ge(sig("stored"), 16)

                @block.tensor
                def _(pe):
                    mm, tr = nc.tensor.matmul, nc.tensor.transpose

                    def wait(name, n=1):
                        pe.wait_ge(sig(name), n)

                    def product(tile, cols, terms, ring="dense"):
                        t, full = fill(pe, ring, tile)
                        for n, (lhsT, rhs) in enumerate(terms):
                            ins = mm(t[0:lhsT_cols(lhsT), 0:cols], lhsT, rhs, start=n == 0, stop=n == len(terms) - 1)
                        ins.then_inc(full, 1)

                    def flip(tile, src):
                        for k in range(KT):
                            t, full = fill(pe, "dense", (tile, k))
                            for p in range(NP):
                                ins = tr(t[:, 128 * p:128 * p + 128], src[:, p, 128 * k:128 * k + 128], ident[:, :])
                            ins.then_inc(full, 1)

                    def natural(tile, lhsT, rhs):
                        for q in range(NP // 2):
                            t, full = fill(pe, "dense", (tile, q))
                            for p in range(2):
                                for k, r in enumerate(rhs):
                                    ins = mm(t[:, E * p:E * p + E], lhsT(2 * q + p, k), r, start=k == 0, stop=k == len(rhs) - 1)
                            ins.then_inc(full, 1)

                    wait("c0_in", 16)
                    flip("cT", c0)
                    for q in range(2):
                        t, full = fill(pe, "dense", ("ml", q))
                        for p in range(2):
                            for s in range(2):
                                ins = mm(t[:, 256 * p + 128 * s:256 * p + 128 * s + 128], c0[:, 2 * q + p, 128 * s:128 * s + 128],
                                         conv["Wl"][:, :], start=True, stop=True)
                        ins.then_inc(full, 1)
                    wait("ch_ready", NP)
                    for q in range(2):
                        product(("mm", q), 512, [(conv["Wm"][:, :], ch[:, 2 * q:2 * q + 2, :])])
                    wait("xh_ready", NP)
                    for q in range(2):
                        product(("mn", q), 512, [(conv["Wn"][:, :], xh[:, 2 * q:2 * q + 2, :])])

                    def scores0(u):
                        wait("mn_ready", u // 4 + 1)
                        wait("mmb_ready", u // 4 + 1)
                        product(("s0", u), 512, [(mn[:, u // 2, 128 * (u % 2):128 * (u % 2) + 128], mmb[:, u // 2, :, :])], "score")

                    def turn0(u):
                        wait("p0_ready", u + 1)
                        t, full = fill(pe, "turn", ("t0", u))
                        for n in range(4):
                            ins = tr(t[:, 128 * n:128 * n + 128], soft[:, u % 4, 128 * n:128 * n + 128], ident[:, :])
                        ins.then_inc(full, 1)

                    def value0(p):
                        wait("pT0_ready", 2 * p + 2)
                        wait("ml_ready", p // 2 + 1)
                        t, full = fill(pe, "value", ("o0", p))
                        for b in range(2):
                            for s in range(2):
                                ins = mm(t[64 * b:64 * b + 64, 0:E], mlT[:, p, s, 64 * b:64 * b + 64], pT0[:, p % 2, :, b, s, :],
                                         start=s == 0, stop=s == 1)
                        ins.then_inc(full, 1)

                    def out0(p):
                        wait("mo_ready", p + 1)
                        product(("x1", p), E, [(conv["Wo"][:, :], mo[:, p, :])])

                    U0 = 2 * NP
                    for i in range(U0 + 6):
                        if i < U0:
                            scores0(i)
                        if 2 <= i < U0 + 2:
                            turn0(i - 2)
                        if i >= 5 and (i - 5) % 2 == 0 and (i - 5) // 2 < NP:
                            value0((i - 5) // 2)
                        if i >= 7 and (i - 7) % 2 == 0 and (i - 7) // 2 < NP:
                            out0((i - 7) // 2)
                    if stop < 1:
                        return

                    wait("cT_ready", KT)
                    t, full = fill(pe, "dense", "k1")
                    for b in range(2):
                        for k in range(KT):
                            ins = mm(t[64 * b:64 * b + 64, 0:256], wk1[:, k, :], hT[:, k, b::2, 0, :], start=k == 0, stop=k == KT - 1)
                    ins.then_inc(full, 1)
                    t, full = fill(pe, "dense", "v1")
                    for b in range(NB):
                        r = 64 * (b % 2)
                        for k in range(KT):
                            ins = mm(t[r:r + 64, 64 * (b // 2):64 * (b // 2) + 64], hT[:, k, b, 0, :], wv1[:, k, :], start=k == 0, stop=k == KT - 1)
                    ins.then_inc(full, 1)
                    wait("x1_ready", NP)
                    flip("x1T", xA)
                    wait("x1T_ready", KT)
                    for q in range(2):
                        t, full = fill(pe, "dense", ("q1", q))
                        for g in range(2):
                            for b in range(2):
                                for k in range(KT):
                                    ins = mm(t[64 * b:64 * b + 64, 256 * g:256 * g + 256],
                                             wq1[:, k, 2 * q + g, :],
                                             x1T[:, k, :].rearrange("p (n b l) -> p b n l", b=2, l=L)[:, b],
                                             start=k == 0, stop=k == KT - 1)
                        ins.then_inc(full, 1)

                    def softmax_layer(y, scores, value, total, result):
                        def turn1(u):
                            wait(f"exp{y}", u + 1)
                            t, full = fill(pe, "turn", (f"t{y}", u))
                            for n in range(4):
                                ins = tr(t[:, 128 * n:128 * n + 128], soft[:, u % 4, 128 * n:128 * n + 128], ident[:, :])
                            ins.then_inc(full, 1)

                        def pair(p):
                            wait(f"pT{y}_ready", 4 * p + 4)
                            for ring, terms in (("value", value), ("total", total)):
                                t, full = fill(pe, ring, (f"{ring}{y}", p))
                                for dst, cols, lhsT, rhs in terms(p):
                                    ins = mm(t[dst:dst + 32, cols[0]:cols[1]], lhsT, rhs, start=True, stop=True)
                                ins.then_inc(full, 1)

                        def pair_out(p):
                            wait(f"at{y}_ready", p + 1)
                            product((f"out{y}", p), E, result(p))

                        for i in range(4 * NP + 10):
                            if i < 4 * NP:
                                scores(i)
                            if 3 <= i < 4 * NP + 3:
                                turn1(i - 3)
                            if i >= 8 and (i - 8) % 4 == 0 and (i - 8) // 4 < NP:
                                pair((i - 8) // 4)
                            if i >= 10 and (i - 10) % 4 == 0 and (i - 10) // 4 < NP:
                                pair_out((i - 10) // 4)

                    def scores1(u):
                        p, g = u // 4, u % 4
                        wait("kbd_ready", p + 1)
                        wait("qz_ready", g // 2 + 1)
                        product(("s1", u), 512, [(qz[:, g, p, :, :], kbd[:, p, :, :])], "score")

                    softmax_layer(
                        1, scores1,
                        lambda p: [(32 * j, (256 * b, 256 * b + 256), vbd[:, 2 * p + b, j, :], pT1[:, p % 2, j, b, :, :])
                                   for b in range(2) for j in range(4)],
                        lambda p: [(32 * j, (256 * b, 256 * b + 256), ones2[:, :], pT1[:, p % 2, j, b, :, :])
                                   for b in range(2) for j in range(4)],
                        lambda p: [(at1[:, p % 2, g, :], wo1[:, g, :]) for g in range(GQ)])
                    wait("xh1_ready", NP)
                    flip("lT", xh)
                    if stop < 2:
                        return

                    wait("lT_ready", KT)
                    for h in range(KT):
                        product(("q2", h), 512, [(wq2[:, k, 128 * h:128 * h + 128], hT[:, k, :, 1, :]) for k in range(KT)])
                    kv = wkv2[:, :, :].rearrange("p k (n s) -> p s k n", s=2)
                    for h in range(KT):
                        for q in range(2):
                            product(("k2", h, q), 512, [(kv[:, 0, k, 128 * h:128 * h + 128], hT[:, k, 4 * q:4 * q + 4, :, :]) for k in range(KT)])
                    for p in range(NP):
                        t, full = fill(pe, "dense", ("v2", p))
                        for b in range(2):
                            for k in range(KT):
                                ins = mm(t[:, 256 * b:256 * b + 256], hT[:, k, 2 * p + b, :, :], kv[:, 1, k, :], start=k == 0, stop=k == KT - 1)
                        ins.then_inc(full, 1)

                    def scores2(u):
                        b, h = u // 2, u % 2
                        wait("k2_ready", 4)
                        wait("qring_ready", u + 1)
                        t, full = fill(pe, "score", ("s2", u))
                        for j in range(4):
                            ins = mm(t[:, 128 * j:128 * j + 128], qring[:, u % 2, 2 * j:2 * j + 2, :], k2T[:, h, b, :], start=True, stop=True)
                        ins.then_inc(full, 1)

                    wait("v2_ready", NP)
                    softmax_layer(
                        2, scores2,
                        lambda p: [(32 * j, (256 * b + 128 * h, 256 * b + 128 * h + 128), v2[:, 2 * p + b, 128 * h + 32 * j:128 * h + 32 * j + 32],
                                    pT2[:, (2 * p + b) % 4, h, 128 * j:128 * j + 128]) for b in range(2) for h in range(2) for j in range(4)],
                        lambda p: [(32 * j, (256 * b + 128 * h, 256 * b + 128 * h + 128), ones32[:, :],
                                    pT2[:, (2 * p + b) % 4, h, 128 * j:128 * j + 128]) for b in range(2) for h in range(2) for j in range(4)],
                        lambda p: [(at2[:, p % 2, 2 * h + e, :], wo2[:, h, e, :]) for h in range(KT) for e in range(2)])
                    wait("xh2_ready", NP)
                    flip("xnT", xh)
                    wait("xnT_ready", KT)
                    for n in range(HID // 128):
                        product(("u", n), 512, [(w1[:, k, 128 * n:128 * n + 128], xnT[:, k, :]) for k in range(KT)])
                    wait("gT_ready", HID // 128)
                    natural("y2", lambda p, k: gT[:, k, 128 * p:128 * p + 128], [w2[:, k, :] for k in range(HID // 128)])
                    if stop < 3:
                        return

                    def square(tile, w, moving):
                        for m in range(KT):
                            product((tile, m), 512, [(wt[w][:, k, 128 * m:128 * m + 128], moving(k)) for k in range(KT)])

                    wait("xh3_ready", NP)
                    flip("xaT", xh)
                    wait("x1m_ready", KT)
                    product("maaA", 512, [(maa1[:, k, 0:128], xm[:, 0, k, :]) for k in range(KT)])
                    product("maaB", 512, [(maa1[:, k, 128:160], xm[:, 0, k, :]) for k in range(KT)])
                    wait("xf_ready", 2)

                    def mix(n, f):
                        for m in range(KT):
                            product(("mix", n, m), 512, [(maa2[:, f, 128 * m:128 * m + 128], xf[:, f // 4, :])])

                    def mixed(n, tile, w):
                        wait("xm_ready", KT * (n + 1))
                        square(tile, w, lambda k: xm[:, (n + 1) % 2, k, :])
                    mix(0, 1)
                    mix(1, 0)
                    wait("xm_ready", KT)
                    product("td", 512, [(td1[:, k, :], xm[:, 1, k, :]) for k in range(KT)])
                    mix(2, 2)
                    mixed(1, "k", "Wk")
                    wait("td_ready", 1)
                    for m in range(KT):
                        product(("decay", m), 512, [(td2[:, 128 * m:128 * m + 128], tdT[:, :])])
                    mix(3, 3)
                    mixed(2, "v", "Wv")
                    mix(4, 4)
                    mixed(3, "r", "Wr")
                    mixed(4, "g", "Wg")
                    for k in range(KT):
                        t, full = fill(pe, "score", ("o3", k))
                        for j in range(HS):
                            wait("rs_ready", HS * k + j + 1)
                            ins = mm(t[:, :], pick[:, j, :], rs[:, j % 2, :], start=j == 0, stop=j == HS - 1)
                            if j < HS - 1:
                                ins.then_inc(sig("rs_used"), 1)
                        ins.then_inc(full, 1)
                        wait("ruk_ready", k + 1)
                        product(("bonus", k), 512, [(block8[:, :, :], cut(C, 1024 * 3, 2, 512)[:, k, :])], "turn")
                    for k in range(KT):
                        wait("o3_ready", k + 1)
                        product(("oc", k), 512, [(center8[:, :], oT[:, k, :])], "turn")
                    for k in range(KT):
                        wait("sq_ready", k + 1)
                        product(("var", k), 512, [(block8[:, :, :], sq[:, k, :])])
                    wait("ogT_ready", KT)
                    natural("x4", lambda p, k: ogT[:, k, 128 * p:128 * p + 128], [wt["Wo"][:, k, :] for k in range(KT)])
                    wait("xh4_ready", NP)
                    flip("xcT", xh)
                    wait("xk2_ready", KT)
                    square("fk", "Wfk", lambda k: xk2[:, k, :])
                    wait("xr2_ready", KT)
                    natural("fr", lambda p, k: xr2[:, k, 128 * p:128 * p + 128], [wt["Wfr"][:, k, :] for k in range(KT)])
                    wait("kk_ready", KT)
                    natural("fv", lambda p, k: kkT[:, k, 128 * p:128 * p + 128], [wt["Wfv"][:, k, :] for k in range(KT)])

                @block.scalar
                def _(act):
                    link = linker(act, "act_step")
                    af = nc.scalar.activation

                    def wait(name, n=1):
                        act.wait_ge(sig(name), n)

                    def rsqrt(dst, src, eps, scale, name):
                        link(af(dst, src, ACT.Ln, bias=eps[:, :], scale=scale))
                        af(dst, dst, ACT.Exp, scale=-0.5).then_inc(sig(name), 1)

                    wait("stats0_ready")
                    rsqrt(rstd[:, :], mv[:, :, 1], eps5, 1.0, "rstd0_ready")
                    for k in range(KT):
                        t, free = take(act, ("cT", k))
                        af(hT[:, k, :, 0, :], t[:, :], ACT.Identity).then_inc(free, 1)
                        act.wait_ge(free, place[("cT", k)][1])
                    act.sem_inc(sig("cT_ready"), KT)
                    for q in range(2):
                        t, free = take(act, ("mm", q))
                        for b in range(2):
                            if q == 0 and b == 0:
                                wait("mmb_zero")
                            ins = af(mmb[64 * b:64 * b + 64, 2 * q:2 * q + 2, b, :], t[64 * b:64 * b + 64, :].rearrange("p (n t) -> p n t", n=2),
                                     ACT.Identity, bias=v("bm")[64 * b:64 * b + 64])
                        ins.then_inc(free, 1)
                        act.wait_ge(free, place[("mm", q)][1])
                        act.sem_inc(sig("mmb_ready"), 1)

                    for u in range(2 * NP):
                        t, free = take(act, ("s0", u))
                        wait("nmax0_ready", u + 1)
                        if u >= 4:
                            wait("pT0_ready", u - 3)
                        for b in range(2):
                            link(af(soft[:, u % 4, 256 * b:256 * b + 256], t[:, 256 * b:256 * b + 256], ACT.Exp,
                                    bias=nmax0[:, u, b:b + 1], accum_out=den0[:, u, b:b + 1]))
                        act.sem_inc(free, 1)
                        act.sem_inc(sig("exp0"), 1)
                    if stop < 1:
                        return

                    for k in range(KT):
                        t, free = take(act, ("x1T", k))
                        link(af(x1T[:, k, :], t[:, :], ACT.Identity))
                        act.sem_inc(free, 1)
                        act.sem_inc(sig("x1T_ready"), 1)
                    for q in range(2):
                        t, free = take(act, ("q1", q))
                        if q == 0:
                            wait("qz_zero")
                        for g in range(2):
                            for b in range(2):
                                r = slice(64 * b, 64 * b + 64)
                                ins = af(qz[r, 2 * q + g, :, b, :], t[r, 256 * g:256 * g + 256].rearrange("p (n l) -> p n l", l=L),
                                         ACT.Identity, bias=v("bq", 2 * q + g)[r])
                        link(ins)
                        act.sem_inc(free, 1)
                        act.sem_inc(sig("qz_ready"), 1)

                    def softmax_layer(y, keep):
                        def exps(u):
                            wait(f"sub{y}", u + 1)
                            af(soft[:, u % 4, :], soft[:, u % 4, :], ACT.Exp).then_inc(sig(f"exp{y}"), 1)

                        def turned(u):
                            t, free = take(act, (f"t{y}", u))
                            keep(u, t).then_inc(sig(f"pT{y}_ready"), 1)
                            wait(f"pT{y}_ready", u + 1)
                            act.sem_inc(free, 1)

                        def totals(p):
                            t, free = take(act, (f"total{y}", p))
                            if p >= 2:
                                wait(f"at{y}_ready", p - 1)
                            link(af(over[:, p % 2, :], t[:, :], ACT.Ln))
                            act.sem_inc(free, 1)
                            af(over[:, p % 2, :], over[:, p % 2, :], ACT.Exp, scale=-1.0).then_inc(sig(f"over{y}_ready"), 1)

                        for i in range(4 * NP + 10):
                            if i < 4 * NP:
                                exps(i)
                            if 2 <= i < 4 * NP + 2:
                                turned(i - 2)
                            if i >= 7 and (i - 7) % 4 == 0 and (i - 7) // 4 < NP:
                                totals((i - 7) // 4)

                    softmax_layer(1, lambda u, t: af(pT1[:, (u // 4) % 2, :, :, u % 4, :],
                                                     t[:, :].rearrange("p (j b l) -> p j b l", j=4, b=2), ACT.Identity))
                    wait("stats1_ready")
                    rsqrt(rstd[:, 0:NP], mv[:, 0:NP, 1], eps6, 1.0, "rstd1_ready")
                    for k in range(KT):
                        t, free = take(act, ("lT", k))
                        link(af(hT[:, k, :, 1, :], t[:, :].rearrange("p (b l) -> p b l", l=L), ACT.Identity, bias=v("beta", k), scale=v("gamma", k)))
                        act.sem_inc(free, 1)
                        act.sem_inc(sig("lT_ready"), 1)
                    if stop < 2:
                        return

                    for h in range(KT):
                        for q in range(2):
                            t, free = take(act, ("k2", h, q))
                            link(af(k2T[:, h, 4 * q:4 * q + 4, :], t[:, :].rearrange("p (b n) -> p b n", n=KEYS), ACT.Identity, bias=v("k_b", h)))
                            act.sem_inc(free, 1)
                            act.sem_inc(sig("k2_ready"), 1)
                    softmax_layer(2, lambda u, t: af(pT2[:, (u // 2) % 4, u % 2, :], t[:, :], ACT.Identity))
                    for p in range(NP):
                        wait("ao_ready", p + 1)
                        link(af(xh[:, p, :], xB[:, p, :], ACT.Square, accum_out=stats[:, p, 0:1]))
                    rsqrt(rstd[:, 0:NP], stats[:, 0:NP, 0], eps6, 1.0 / E, "rstd2_ready")
                    for k in range(KT):
                        t, free = take(act, ("xnT", k))
                        link(af(xnT[:, k, :], t[:, :], ACT.Identity, scale=v("post", k)))
                        act.sem_inc(free, 1)
                        act.sem_inc(sig("xnT_ready"), 1)
                    for n in range(HID // 128):
                        t, free = take(act, ("u", n))
                        link(af(gT[:, n, :], t[:, :], ACT.Gelu_apprx_tanh, bias=v("b1", n)))
                        act.sem_inc(free, 1)
                        act.sem_inc(sig("gT_ready"), 1)
                    if stop < 3:
                        return

                    wait("stats3_ready")
                    rsqrt(rstd[:, 0:NP], mv[:, 0:NP, 1], eps5, 1.0, "rstd3_ready")
                    for k in range(KT):
                        t, free = take(act, ("xaT", k))
                        link(af(xaP[:, k, :, 1:LP], t[:, :].rearrange("p (b l) -> p b l", l=L), ACT.Identity, bias=v("ln1_b", k), scale=v("ln1_w", k)))
                        act.sem_inc(free, 1)
                        act.sem_inc(sig("xaP_ready"), 1)
                    t, free = take(act, "maaA")
                    link(af(xf[:, 0, :], t[:, :], ACT.Tanh))
                    act.sem_inc(free, 1)
                    act.sem_inc(sig("xf_ready"), 1)
                    t, free = take(act, "maaB")
                    link(af(xf[0:DM, 1, :], t[0:DM, :], ACT.Tanh))
                    act.sem_inc(free, 1)
                    act.sem_inc(sig("xf_ready"), 1)
                    t, free = take(act, "td")
                    link(af(tdT[0:DD, :], t[0:DD, :], ACT.Tanh))
                    act.sem_inc(free, 1)
                    act.sem_inc(sig("td_ready"), 1)

                    def padded(tile, dst, name, func=ACT.Identity, shift=1):
                        for k in range(KT):
                            t, free = take(act, (tile, k))
                            link(af(dst[:, k, :, shift:LP], t[:, :].rearrange("p (b l) -> p b l", l=L), func))
                            act.sem_inc(free, 1)
                            act.sem_inc(sig(name), 1)
                    padded("k", kP, "kP_ready")
                    for k in range(KT):
                        t, free = take(act, ("decay", k))
                        link(af(decay[:, k, :], t[:, :], ACT.Exp, bias=v("decay", k)))
                        act.sem_inc(free, 1)
                        link(af(wP[:, k, :, 1:LP], decay[:, k, :].rearrange("p (b l) -> p b l", l=L), ACT.Exp, scale=-1.0))
                        act.sem_inc(sig("wP_ready"), 1)
                    padded("v", vP, "vP_ready")
                    for k in range(KT):
                        t, free = take(act, ("r", k))
                        link(af(rT[:, k, :], t[:, :], ACT.Identity))
                        act.sem_inc(free, 1)
                        act.sem_inc(sig("rT_ready"), 1)
                    for k in range(KT):
                        t, free = take(act, ("g", k))
                        af(gg[:, k, :], t[:, :], ACT.Tanh, scale=0.5).then_inc(sig("tanh_g"), 1)
                    for k in range(KT):
                        t, free = take(act, ("oc", k))
                        wait("o3_ready", KT)
                        af(sq[:, k, :], t[:, :], ACT.Square).then_inc(sig("sq_ready"), 1)
                    for k in range(KT):
                        t, free = take(act, ("var", k))
                        link(af(decay[:, k, :], t[:, :], ACT.Ln, bias=eps5[:, :], scale=1.0 / HS))
                        act.sem_inc(free, 1)
                    for k in range(KT):
                        af(decay[:, k, :], decay[:, k, :], ACT.Exp, scale=-0.5).then_inc(sig("rgn_ready"), 1)
                    wait("stats4_ready")
                    rsqrt(rstd[:, 0:NP], mv[:, 0:NP, 1], eps5, 1.0, "rstd4_ready")
                    for k in range(KT):
                        t, free = take(act, ("xcT", k))
                        link(af(xcP[:, k, :, 1:LP], t[:, :].rearrange("p (b l) -> p b l", l=L), ACT.Identity, bias=v("ln2_b", k), scale=v("ln2_w", k)))
                        act.sem_inc(free, 1)
                        act.sem_inc(sig("xcP_ready"), 1)
                    for k in range(KT):
                        t, free = take(act, ("fk", k))
                        if k == 0:
                            wait("ogT_used")
                        link(af(kkT[:, k, :], t[:, :], ACT.Relu))
                        act.sem_inc(free, 1)
                        af(kkT[:, k, :], kkT[:, k, :], ACT.Square).then_inc(sig("kk_ready"), 1)
                    for q in range(2):
                        t, free = take(act, ("fr", q))
                        link(af(thn[:, 2 * q:2 * q + 2, :], t[:, :].rearrange("p (n e) -> p n e", n=2), ACT.Tanh, scale=0.5))
                        act.sem_inc(free, 1)
                        act.sem_inc(sig("thn_ready"), 1)

                @block.vector
                def _(dve):
                    link = linker(dve, "dve_step")
                    tt, ts, stt = nc.vector.tensor_tensor, nc.vector.tensor_scalar, nc.vector.scalar_tensor_tensor

                    def wait(name, n=1):
                        dve.wait_ge(sig(name), n)

                    def moments(srcs, name):
                        for n, s in enumerate(srcs):
                            ins = nc.vector.bn_stats(stats[:, n, :], s)
                        link(ins)
                        for n in range(len(srcs)):
                            ins = nc.vector.bn_aggr(mv[:, n, :], stats[:, n, :])
                        ins.then_inc(sig(name), 1)
                        wait(name, 1)

                    def normalize(src, name, n0=0):
                        for p in range(NP):
                            ts(xh[:, p, :], src[:, p, :], mv[:, n0 + p, 0:1], rstd[:, n0 + p:n0 + p + 1],
                               ALU.subtract, ALU.mult).then_inc(sig(name), 1)

                    wait("c0_in", 16)
                    wait("x0_in", 16)
                    moments([c0[:, p, :] for p in range(NP)] + [x0[:, p, :] for p in range(NP)], "stats0_ready")
                    for q in range(2):
                        t, free = take(dve, ("ml", q))
                        link(nc.vector.tensor_copy(mlT[:, 2 * q:2 * q + 2, :, :].rearrange("p n s o -> p (n s o)"), t[:, :]))
                        dve.sem_inc(free, 1)
                        dve.sem_inc(sig("ml_ready"), 1)
                    wait("rstd0_ready")
                    for p in range(NP):
                        ts(ch[:, p, :], c0[:, p, :], mv[:, p, 0:1], rstd[:, p:p + 1], ALU.subtract, ALU.mult).then_inc(sig("ch_ready"), 1)
                    normalize(x0, "xh_ready", NP)
                    for q in range(2):
                        t, free = take(dve, ("mn", q))
                        link(ts(mn[:, 2 * q:2 * q + 2, :].rearrange("p n t -> p (n t)"), t[:, :], v("bn"), None, ALU.add))
                        dve.sem_inc(free, 1)
                        dve.sem_inc(sig("mn_ready"), 1)
                    U0 = 2 * NP
                    for i in range(U0 + 8):
                        if i < U0:
                            t, _ = take(dve, ("s0", i))
                            nc.vector.tensor_reduce(nmax0[:, i, :], t[:, :].rearrange("p (b s) -> p b s", b=2), X, ALU.max,
                                                    negate=True).then_inc(sig("nmax0_ready"), 1)
                        if 1 <= i < U0 + 1:
                            wait("exp0", i)
                            nc.vector.reciprocal(rden0[:, i - 1, :], den0[:, i - 1, :]).then_inc(sig("rden0_ready"), 1)
                        if 3 <= i < U0 + 3:
                            u = i - 3
                            t, free = take(dve, ("t0", u))
                            if u >= 4:
                                dve.wait_ge(sig("bank4_full"), place[("o0", u // 2 - 2)][1])
                            nc.vector.tensor_copy(pT0[:, (u // 2) % 2, u % 2].rearrange("p b s t -> p (b s t)"), t[:, :]).then_inc(sig("pT0_ready"), 1)
                            wait("pT0_ready", u + 1)
                            dve.sem_inc(free, 1)
                        if i >= 6 and (i - 6) % 2 == 0 and (i - 6) // 2 < NP:
                            p = (i - 6) // 2
                            t, free = take(dve, ("o0", p))
                            link(ts(mo[:, p, :], t[:, 0:E], v("bl"), None, ALU.add))
                            dve.sem_inc(free, 1)
                            dve.sem_inc(sig("mo_ready"), 1)
                        if i >= 8 and (i - 8) % 2 == 0 and (i - 8) // 2 < NP:
                            p = (i - 8) // 2
                            t, free = take(dve, ("x1", p))
                            link(stt(out=xA[:, p, :], in0=t[:, 0:E], scalar=v("bo"), in1=x0[:, p, :], op0=ALU.add, op1=ALU.add))
                            dve.sem_inc(free, 1)
                            dve.sem_inc(sig("x1_ready"), 1)
                    if stop < 1:
                        dve.sem_inc(sig("dbg"), 1)
                        return

                    t, free = take(dve, "k1")
                    link(ts(kT1[:, :, :].rearrange("p n s -> p (n s)"), t[:, 0:256], v("bk"), None, ALU.add))
                    dve.sem_inc(free, 1)
                    dve.sem_inc(sig("kT1_ready"), 1)
                    t, free = take(dve, "v1")
                    for b in range(2):
                        for h in range(2):
                            src = t[64 * b:64 * b + 64, 0:256].rearrange("p (n j h d) -> p h n j d", n=NP, h=2, d=HD1)[:, h]
                            ins = nc.vector.tensor_copy(vbd[64 * h:64 * h + 64, b::2, :, 8 * h:8 * h + 8], src)
                    link(ins)
                    dve.sem_inc(free, 1)
                    dve.sem_inc(sig("vbd_ready"), 1)

                    def softmax_layer(y, segs, scale, mask, queries, at, xres, name):
                        n = 512 // segs

                        def masked(u):
                            t, free = take(dve, (f"s{y}", u))
                            if u >= 4:
                                wait(f"pT{y}_ready", u - 3)
                            stt(out=soft[:, u % 4, :].rearrange("p (h s) -> p h s", s=n), in0=t[:, :].rearrange("p (h s) -> p h s", s=n),
                                scalar=scale, in1=mask(u).unsqueeze(1).broadcast_to([128, segs, n]),
                                op0=ALU.mult, op1=ALU.add).then_inc(free, 1)

                        def largest(u):
                            b, k = place[(f"s{y}", u)]
                            dve.wait_ge(sig(f"bank{b}_free"), k)
                            nc.vector.tensor_reduce(seg_max[:, u % 4, 0:segs], soft[:, u % 4, :].rearrange("p (h s) -> p h s", s=n),
                                                    X, ALU.max).then_inc(sig(f"max{y}"), 1)

                        def divide(p):
                            t, free = take(dve, (f"value{y}", p))
                            wait(f"over{y}_ready", p + 1)
                            if p >= 2:
                                b, k = place[(f"out{y}", p - 2)]
                                dve.wait_ge(sig(f"bank{b}_full"), k)
                            link(tt(at(p), t[:, :].rearrange("p (b g l) -> p b g l", b=2, g=4),
                                    over[:, p % 2, :].rearrange("p (b g l) -> p b g l", b=2, g=4), ALU.mult))
                            dve.sem_inc(free, 1)
                            dve.sem_inc(sig(f"at{y}_ready"), 1)

                        def add(p):
                            t, free = take(dve, (f"out{y}", p))
                            wait(xres, p + 1)
                            link(tt(xB[:, p, :], t[:, 0:E], xr[:, p, :], ALU.add))
                            dve.sem_inc(free, 1)
                            dve.sem_inc(sig(name), 1)

                        for i in range(4 * NP + 11):
                            if i < 4 * NP:
                                queries(i)
                                masked(i)
                            if 1 <= i < 4 * NP + 1:
                                largest(i - 1)
                            if i >= 9 and (i - 9) % 4 == 0 and (i - 9) // 4 < NP:
                                divide((i - 9) // 4)
                            if i >= 11 and (i - 11) % 4 == 0 and (i - 11) // 4 < NP:
                                add((i - 11) // 4)
                        add(NP - 1) if (4 * NP + 10 - 11) // 4 < NP - 1 else None

                    wait("mask1_in", 16)
                    softmax_layer(1, KVH, HD1 ** -0.5, lambda u: mask1[:, u // 4, :], lambda u: None,
                                  lambda p: at1[:, p % 2].rearrange("p g (b l) -> p b g l", b=2), "xr1_ready", "x2_ready")
                    moments([xB[:, p, :] for p in range(NP)], "stats1_ready")
                    wait("rstd1_ready")
                    normalize(xB, "xh1_ready")
                    if stop < 2:
                        wait("lat_ready", NP)
                        dve.sem_inc(sig("dbg"), 1)
                        return

                    for h in range(KT):
                        t, free = take(dve, ("q2", h))
                        link(ts(q2T[:, h, :, :].rearrange("p b l -> p (b l)"), t[:, :], v("q_b", h), None, ALU.add))
                        dve.sem_inc(free, 1)
                    for p in range(NP):
                        t, free = take(dve, ("v2", p))
                        link(nc.vector.tensor_copy(v2[:, 2 * p:2 * p + 2, :].rearrange("p b n -> p (b n)"), t[:, :]))
                        dve.sem_inc(free, 1)
                        dve.sem_inc(sig("v2_ready"), 1)

                    def queries2(u):
                        if u == 0:
                            one_query(0)
                        if u + 1 < 4 * NP:
                            one_query(u + 1)

                    def one_query(u):
                        if u >= 2:
                            b, k = place[("s2", u - 2)]
                            dve.wait_ge(sig(f"bank{b}_full"), k)
                        tt(qring[:, u % 2, :, :], q2T[:, u % 2, u // 2, :].unsqueeze(1).broadcast_to([128, HPT, L]),
                           hmask[:, :].unsqueeze(2).broadcast_to([128, HPT, L]), ALU.mult).then_inc(sig("qring_ready"), 1)

                    wait("mask2_ready")
                    softmax_layer(2, 4, 1.0 / HD2, lambda u: mask2[:, u // 2, :], queries2,
                                  lambda p: at2[:, p % 2].rearrange("p g (b l) -> p b g l", b=2), "xr2a_ready", "ao_ready")
                    wait("rstd2_ready")
                    for p in range(NP):
                        ts(xh[:, p, :], xB[:, p, :], rstd[:, p:p + 1], None, ALU.mult).then_inc(sig("xh2_ready"), 1)
                    wait("xh2_ready", NP)
                    for q in range(2):
                        t, free = take(dve, ("y2", q))
                        wait("xr3_ready", NP)
                        link(tt(xB[:, 2 * q:2 * q + 2, :].rearrange("p n e -> p (n e)"), t[:, :], xr[:, 2 * q:2 * q + 2, :].rearrange("p n e -> p (n e)"), ALU.add))
                        dve.sem_inc(free, 1)
                    if stop < 3:
                        dve.sem_inc(sig("dbg"), 1)
                        return

                    moments([xB[:, p, :] for p in range(NP)], "stats3_ready")
                    wait("rstd3_ready")
                    normalize(xB, "xh3_ready")
                    wait("edge3_ready")
                    for k in range(KT):
                        wait("xaP_ready", k + 1)
                        s = sx[:, k, :].rearrange("p (b l) -> p b l", l=L)
                        link(tt(s, xaP[:, k, :, 0:L], xaP[:, k, :, 1:LP], ALU.subtract))
                        stt(out=xm[:, 0, k, :].rearrange("p (b l) -> p b l", l=L), in0=s, scalar=v("maa_x", k), in1=xaP[:, k, :, 1:LP],
                            op0=ALU.mult, op1=ALU.add).then_inc(sig("x1m_ready"), 1)
                    wait("x1m_ready", KT)

                    def mix(n, f):
                        if n >= 2:
                            last = {2: ("td", None), 3: ("k", 1), 4: ("v", 1)}[n]
                            b, c = place["td" if n == 2 else last]
                            dve.wait_ge(sig(f"bank{b}_full"), c)
                        for k in range(KT):
                            t, free = take(dve, ("mix", n, k))
                            if n == 1 and k == 0:
                                b, c = place["maaB"]
                                dve.wait_ge(sig(f"bank{b}_full"), c)
                            link(stt(out=mtmp[:, k, :], in0=t[:, :], scalar=v("maa", 2 * f + k), in1=sx[:, k, :], op0=ALU.add, op1=ALU.mult))
                            dve.sem_inc(free, 1)
                            tt(xm[:, (n + 1) % 2, k, :].rearrange("p (b l) -> p b l", l=L), mtmp[:, k, :].rearrange("p (b l) -> p b l", l=L),
                               xaP[:, k, :, 1:LP], ALU.add).then_inc(sig("xm_ready"), 1)
                            wait("xm_ready", KT * n + k + 1)
                    for n, f in enumerate((1, 0, 2, 3, 4)):
                        mix(n, f)
                    for k in range(KT):
                        t, free = take(dve, ("g", k))
                        wait("tanh_g", k + 1)
                        link(stt(out=gg[:, k, :], in0=gg[:, k, :], scalar=1.0, in1=t[:, :], op0=ALU.add, op1=ALU.mult))
                        dve.sem_inc(free, 1)
                    ruk = cut(C, 1024 * 3, 2, 512)
                    wait("rT_ready", KT)
                    wait("wP_ready", KT)
                    wait("wP_edge")
                    for k in range(KT):
                        stt(out=ruk[:, k, :].rearrange("p (b l) -> p b l", l=L), in0=rT[:, k, :].rearrange("p (b l) -> p b l", l=L), scalar=v("u", k),
                            in1=kP[:, k, :, 1:LP], op0=ALU.mult, op1=ALU.mult).then_inc(sig("ruk_ready"), 1)

                    def scan(n):
                        k = n // HS
                        wait("aj_ready", n + 1)
                        if n >= 2:
                            wait("rs_ready", n - 1)
                        nc.vector.tensor_tensor_scan(sj[:, n % 2, :], wP[:, k, :, :].rearrange("p b t -> p (b t)"), aj[:, n % 3, :], 0.0,
                                                     ALU.mult, ALU.add).then_inc(sig("sj_ready"), 1)

                    def read(n):
                        k = n // HS
                        wait("sj_ready", n + 1)
                        if n >= 2:
                            m = n - 2
                            if m % HS == HS - 1:
                                b, c = place[("o3", m // HS)]
                                dve.wait_ge(sig(f"bank{b}_full"), c)
                            else:
                                wait("rs_used", m - m // HS + 1)
                        tt(rs[:, n % 2, :].rearrange("p (b l) -> p b l", l=L), rT[:, k, :].rearrange("p (b l) -> p b l", l=L),
                           sj[:, n % 2, :].rearrange("p (b t) -> p b t", t=LP)[:, :, 0:L], ALU.mult).then_inc(sig("rs_ready"), 1)

                    for n in range(KT * HS + 1):
                        if n < KT * HS:
                            scan(n)
                        if n >= 1:
                            read(n - 1)
                    for k in range(KT):
                        t, free = take(dve, ("bonus", k))
                        link(tt(oT[:, k, :].rearrange("p (b l) -> p b l", l=L), t[:, :].rearrange("p (b l) -> p b l", l=L), vP[:, k, :, 1:LP], ALU.mult))
                        dve.sem_inc(free, 1)
                        t, free = take(dve, ("o3", k))
                        link(tt(oT[:, k, :], t[:, :], oT[:, k, :], ALU.add))
                        dve.sem_inc(free, 1)
                        dve.sem_inc(sig("o3_ready"), 1)
                    for k in range(KT):
                        t, free = take(dve, ("oc", k))
                        wait("rgn_ready", k + 1)
                        link(tt(ogT[:, k, :], t[:, :], decay[:, k, :], ALU.mult))
                        dve.sem_inc(free, 1)
                        link(ts(ogT[:, k, :], ogT[:, k, :], v("gn_w", k), v("gn_b", k), ALU.mult, ALU.add))
                        tt(ogT[:, k, :], ogT[:, k, :], gg[:, k, :], ALU.mult).then_inc(sig("ogT_ready"), 1)
                    for q in range(2):
                        t, free = take(dve, ("x4", q))
                        link(tt(xA[:, 2 * q:2 * q + 2, :].rearrange("p n e -> p (n e)"), t[:, :], xB[:, 2 * q:2 * q + 2, :].rearrange("p n e -> p (n e)"), ALU.add))
                        dve.sem_inc(free, 1)
                    dve.sem_inc(sig("ogT_used"), 1)
                    for p in range(NP):
                        ins = nc.vector.bn_stats(stats[:, p, :], xA[:, p, :])
                    link(ins)
                    for p in range(NP):
                        ins = nc.vector.bn_aggr(mv[:, p, :], stats[:, p, :])
                    ins.then_inc(sig("stats4_ready"), 1)
                    wait("rstd4_ready")
                    normalize(xA, "xh4_ready")
                    wait("edge4_ready")
                    for k in range(KT):
                        wait("xcP_ready", k + 1)
                        s = sx[:, k, :].rearrange("p (b l) -> p b l", l=L)
                        link(tt(s, xcP[:, k, :, 0:L], xcP[:, k, :, 1:LP], ALU.subtract))
                        stt(out=xk2[:, k, :].rearrange("p (b l) -> p b l", l=L), in0=s, scalar=v("ffn_k", k), in1=xcP[:, k, :, 1:LP],
                            op0=ALU.mult, op1=ALU.add).then_inc(sig("xk2_ready"), 1)
                        stt(out=xr2[:, k, :].rearrange("p (b l) -> p b l", l=L), in0=s, scalar=v("ffn_r", k), in1=xcP[:, k, :, 1:LP],
                            op0=ALU.mult, op1=ALU.add).then_inc(sig("xr2_ready"), 1)
                    for q in range(2):
                        t, free = take(dve, ("fv", q))
                        wait("thn_ready", q + 1)
                        th = thn[:, 2 * q:2 * q + 2, :].rearrange("p n e -> p (n e)")
                        link(stt(out=th, in0=th, scalar=1.0, in1=t[:, :], op0=ALU.add, op1=ALU.mult))
                        dve.sem_inc(free, 1)
                        stt(out=xr[:, 2 * q:2 * q + 2, :].rearrange("p n e -> p (n e)"), in0=th, scalar=0.5,
                            in1=xA[:, 2 * q:2 * q + 2, :].rearrange("p n e -> p (n e)"), op0=ALU.mult, op1=ALU.add).then_inc(sig("out_ready"), 2)

                @block.gpsimd
                def _(pool):
                    link = linker(pool, "pool_step")
                    tt, ts = nc.gpsimd.tensor_tensor, nc.gpsimd.tensor_scalar

                    def wait(name, n=1):
                        pool.wait_ge(sig(name), n)

                    link(nc.gpsimd.memset(mmb[0:64, :, 1, :], 0.0))
                    link(nc.gpsimd.memset(mmb[64:128, :, 0, :], 0.0))
                    pool.sem_inc(sig("mmb_zero"), 1)
                    link(nc.gpsimd.memset(qz[0:64, :, :, 1, :], 0.0))
                    link(nc.gpsimd.memset(qz[64:128, :, :, 0, :], 0.0))
                    pool.sem_inc(sig("qz_zero"), 1)
                    wait("mask2_in", 16)
                    ts(mask2[:, :, 0:L], imask[:, :, :], 0, MASKED, ALU.is_equal, ALU.mult).then_inc(sig("mask2_ready"), 1)
                    for u in range(2 * NP):
                        wait("rden0_ready", u + 1)
                        for b in range(2):
                            s = soft[:, u % 4, 256 * b:256 * b + 256]
                            ins = ts(s, s, rden0[:, u, b:b + 1], None, ALU.mult)
                        ins.then_inc(sig("p0_ready"), 1)
                    if stop < 1:
                        return

                    wait("kT1_ready")
                    for p in range(NP):
                        tt(kbd[:, p, :, :], kT1[:, p, :].unsqueeze(1).broadcast_to([128, KVH, L]),
                           kvmask[:, :].unsqueeze(2).broadcast_to([128, KVH, L]), ALU.mult).then_inc(sig("kbd_ready"), 1)
                    wait("x1_ready", NP)
                    for p in range(NP):
                        tt(xr[:, p, :], xA[:, p, :], row1[:, :], ALU.add).then_inc(sig("xr1_ready"), 1)

                    def softmax_layer(y, segs):
                        for u in range(4 * NP):
                            wait(f"max{y}", u + 1)
                            s = soft[:, u % 4, :].rearrange("p (h s) -> p h s", s=512 // segs)
                            tt(s, s, seg_max[:, u % 4, 0:segs].unsqueeze(2).broadcast_to([128, segs, 512 // segs]),
                               ALU.subtract).then_inc(sig(f"sub{y}"), 1)
                    softmax_layer(1, KVH)
                    wait("xh1_ready", NP)
                    for p in range(NP):
                        link(tt(xA[:, p, :], xh[:, p, :], row_gamma[:, :], ALU.mult))
                        link(tt(xA[:, p, :], xA[:, p, :], row_beta[:, :], ALU.add))
                        if stop >= 2:
                            tt(xr[:, p, :], xA[:, p, :], row2[:, :], ALU.add).then_inc(sig("xr2a_ready"), 1)
                        pool.sem_inc(sig("lat_ready"), 1)
                    if stop < 2:
                        return

                    softmax_layer(2, 4)
                    wait("ao_ready", NP)
                    for p in range(NP):
                        tt(xr[:, p, :], xA[:, p, :], row_b2[:, :], ALU.add).then_inc(sig("xr3_ready"), 1)
                    if stop < 3:
                        return

                    wait("gT_ready", HID // 128)
                    for k in range(KT):
                        ins = nc.gpsimd.tensor_copy(xaP[:, k, :, 0], hT[:, k, :, 0, 1])
                    ins.then_inc(sig("edge3_ready"), 1)
                    for k in range(KT):
                        nc.gpsimd.memset(kP[:, k, :, 0], 0.0)
                        ins = nc.gpsimd.memset(wP[:, k, :, 0], 0.0)
                    ins.then_inc(sig("wP_edge"), 1)
                    wait("wP_edge")
                    wait("s0_in", 16 * KT)
                    wait("kP_ready", KT)
                    for n in range(KT * HS):
                        k = n // HS
                        wait(f"vj_in{n % 4}", 16 * (n // 4 + 1))
                        if n >= 3:
                            wait("sj_ready", n - 2)
                        if n == 0:
                            wait("ruk_ready", KT)
                        tt(aj[:, n % 3, :], kP[:, k, :, :].rearrange("p b t -> p (b t)"), vj[:, n % 4, :], ALU.mult).then_inc(sig("kv_done"), 1)
                        wait("kv_done", n + 1)
                        nc.gpsimd.tensor_copy(aj[:, n % 3, :].rearrange("p (b t) -> p b t", t=LP)[:, :, 0], s0[:, k, :, n % HS]).then_inc(sig("aj_ready"), 1)
                    wait("x1m_ready", KT)
                    wait("xm_ready", KT * NMIX)
                    for k in range(KT):
                        ins = nc.gpsimd.tensor_copy(xcP[:, k, :, 0], hT[:, k, :, 0, 0])
                    ins.then_inc(sig("edge4_ready"), 1)
            clear_all()


_OUT = (B, L, E)


def kernel(**inputs):
    import numpy as np
    import concourse.bacc as bacc
    from concourse.bass_utils import run_bass_kernel_spmd

    nc = bacc.Bacc("TRN2", target_bir_lowering=False, num_devices=1)
    arrays, aps = {}, {}
    for name, value in inputs.items():
        value = np.ascontiguousarray(value)
        arrays[f"in_{name}"] = value
        aps[name] = nc.dram_tensor(f"in_{name}", value.shape, mybir.dt.from_np(value.dtype), kind="ExternalInput").ap()
    out = nc.dram_tensor("out_x", _OUT, F32, kind="ExternalOutput").ap()
    build(nc, aps, out)
    result = run_bass_kernel_spmd(nc, [arrays], core_ids=[0])
    return result.results[0]["out_x"]
```

```python
from contextlib import ExitStack

import concourse.bass as bass
from concourse import mybir
from concourse.alu_op_type import AluOpType as ALU

F32 = mybir.dt.float32
I32 = mybir.dt.int32
ACT = mybir.ActivationFunctionType
X = mybir.AxisListType.X

B, L, E = 64, 64, 256
NB = 8
NP = NB // 2
GROUPS = B // NB
TOK = NB * L
KT = E // 128
KVH, GQ, HD1 = 8, 4, 8
HD2, KEYS = 16, 2 * L
HPT = 128 // HD2
HID = 4 * E
HS = 8
NMIX, DM, DD = 5, 32, 64
LP = L + 1
SOFT = 6
MASKED = -1.0e30


def _vector_rows():
    rows, at = {}, 0
    for name, n in (("bn", 1), ("bm", 1), ("bl", 1), ("bo", 1), ("bq", GQ), ("bk", 1), ("bv", 1),
                    ("gamma", 2), ("beta", 2), ("q_b", 2), ("k_b", 2), ("v_b", 2), ("post", 2), ("b1", HID // 128),
                    ("ln1_w", 2), ("ln1_b", 2), ("ln2_w", 2), ("ln2_b", 2), ("maa_x", 2), ("maa", 2 * NMIX),
                    ("decay", 2), ("u", 2), ("gn_w", 2), ("gn_b", 2), ("ffn_k", 2), ("ffn_r", 2)):
        rows[name] = (at, n)
        at += n
    return rows, at


def build(nc, a, out):
    with ExitStack() as ctx:
        def sb(name, shape, dt=F32):
            return ctx.enter_context(nc.sbuf_tensor(name, shape, dt))

        sems = {}

        def sig(name):
            if name not in sems:
                sems[name] = ctx.enter_context(nc.semaphore(name))
            return sems[name]

        banks = [ctx.enter_context(nc.psum_tensor(f"bank{i}", [128, 512], F32)) for i in range(8)]
        RINGS = {"score": [0, 1], "turn": [2, 3], "value": [4], "total": [5], "late": [6, 7]}
        turns, fills, place = {}, {}, {}

        def new_block():
            turns.clear()
            fills.clear()
            place.clear()

        def fill(pe, ring, tile):
            b = RINGS[ring][turns.get(ring, 0) % len(RINGS[ring])]
            turns[ring] = turns.get(ring, 0) + 1
            n = fills.get(b, 0)
            if n:
                pe.wait_ge(sig(f"bank{b}_free"), n)
            fills[b] = n + 1
            place[tile] = (b, n + 1)
            return banks[b], sig(f"bank{b}_full")

        def take(eng, tile):
            b, n = place[tile]
            eng.wait_ge(sig(f"bank{b}_full"), n)
            return banks[b], sig(f"bank{b}_free")

        def linker(eng, name):
            count = [0]

            def link(ins):
                count[0] += 1
                ins.then_inc(sig(name), 1)
                eng.wait_ge(sig(name), count[0])
            return link

        ident = sb("ident", [128, 128])
        block8 = sb("block8", [128, 16, 8])
        center8 = sb("center8", [128, 128])
        pick = sb("pick", [128, HS, 128])
        kvmask = sb("kvmask", [128, KVH])
        hmask = sb("hmask", [128, HPT])
        parity = sb("parity", [128, 2])
        half = sb("half", [128, 2, 8])
        ones2 = sb("ones2", [128, 32])
        ones32 = sb("ones32", [128, 32])
        eps5 = sb("eps5", [128, 1])
        eps6 = sb("eps6", [128, 1])
        ROWS, NROWS = _vector_rows()
        vec = sb("vec", [128, 128])

        def v(name, n=0):
            return vec[:, ROWS[name][0] + n:ROWS[name][0] + n + 1]

        conv = {w: sb(f"conv_{w}", [128, 128]) for w in ("Wn", "Wm", "Wl", "Wo")}
        wq1 = sb("wq1", [128, KT, GQ, 64])
        wk1 = sb("wk1", [128, KT, KVH * HD1])
        wv1 = sb("wv1", [128, KT, KVH * HD1])
        wo1 = sb("wo1", [128, GQ, E])
        wq2 = sb("wq2", [128, KT, E])
        wkv2 = sb("wkv2", [128, KT, 2 * E])
        wo2 = sb("wo2", [128, KT, 2, E])
        w1 = sb("w1", [128, KT, HID])
        w2 = sb("w2", [128, HID // 128, E])
        maa1 = sb("maa1", [128, KT, NMIX * DM])
        maa2 = sb("maa2", [128, NMIX, E])
        td1 = sb("td1", [128, KT, DD])
        td2 = sb("td2", [128, E])
        SQUARE = ("Wr", "Wk", "Wv", "Wg", "Wo", "Wfk", "Wfr", "Wfv")
        wt = {w: sb(f"t_{w}", [128, KT, E]) for w in SQUARE}
        row1 = sb("row1", [128, E])
        row2 = sb("row2", [128, E])
        row_b2 = sb("row_b2", [128, E])
        row_gamma = sb("row_gamma", [128, E])

        x0 = sb("x0", [128, NP, E])
        c0 = sb("c0", [128, NP, E])
        mask1 = sb("mask1", [128, NP, L])
        mask2 = sb("mask2", [128, NB, KEYS])
        s0 = sb("s0", [128, KT, NB, HS])
        hT = sb("hT", [128, KT, NB, 2, L])
        stats = sb("stats", [128, 2 * NP, 6])
        mv = sb("mv", [128, 2 * NP, 2])
        rstd = sb("rstd", [128, 2 * NP])
        xA = sb("xA", [128, NP, E])
        xh, xr = c0, x0

        early = sb("early", [128, 10752])
        soft_ring = sb("soft_ring", [128, SOFT, 512])
        qring = sb("qring", [128, 2, HPT, L])
        seg_max = sb("seg_max", [128, SOFT, 8])
        vbd = sb("vbd", [128, NB, 4, 32])
        den0 = sb("den0", [128, 2 * NP, 2])
        rden0 = sb("rden0", [128, 2 * NP, 2])
        nmax0 = sb("nmax0", [128, 2 * NP, 2])
        late = sb("late", [128, 10856])
        x3 = sb("x3", [128, NP, E])
        edge = sb("edge", [128, 2, KT, NB])
        stats3 = sb("stats3", [128, NP, 6])
        mv3 = sb("mv3", [128, NP, 2])
        rstd3 = sb("rstd3", [128, NP])

        def lhsT_cols(ap):
            n = 1
            for size in ap.shape[1:]:
                n *= size
            return n

        def cut(t, at, *shape):
            n = 1
            for size in shape:
                n *= size
            flat = t[:, at:at + n]
            if len(shape) == 1:
                return flat
            names = "abcde"[:len(shape)]
            return flat.rearrange(f"p ({' '.join(names)}) -> p {' '.join(names)}",
                                  **{k: size for k, size in zip(names, shape)})

        vrows = early[:, 4096:4224]
        soft = soft_ring[:, :, :]
        ch = cut(early, 0, NP, E)
        mn = cut(early, 1024, NP, E)
        mlT = cut(early, 2048, NP, 2, 128)
        mo = cut(early, 3072, NP, E)
        mmb = cut(early, 4096, NP, 2, E)
        xh0 = cut(early, 6144, NP, E)
        pT0 = cut(early, 6144, 2, 2, 2, 2, 128)
        qz = cut(early, 8192, GQ, NP, 2, L)
        pT1 = cut(early, 0, 2, 4, 2, GQ, L)
        kbd = cut(early, 4096, NP, KVH, L)
        at1 = cut(early, 6144, 2, GQ, 2 * L)
        x1T = cut(early, 7168, KT, TOK)
        kT1 = cut(early, 10240, NP, L)
        over1 = cut(early, 7168, 2, 512)
        pT2 = cut(early, 0, 4, KT, 512)
        k2T = cut(early, 4096, KT, NB, KEYS)
        q2T = cut(early, 6144, KT, NB, L)
        v2 = cut(early, 7168, NB, E)
        at2 = cut(early, 9216, 2, 4, 2 * L)
        over2 = cut(early, 10240, 1, 512)
        gT = cut(early, 0, HID // 128, TOK)
        xnT = cut(early, 6144, KT, TOK)
        PT = NB * LP
        kP = cut(late, 0, KT, NB, LP)
        vP = cut(late, 1040, KT, NB, LP)
        wP = cut(late, 2080, KT, NB, LP)
        rT = cut(late, 3120, KT, TOK)
        gg = cut(late, 4144, KT, TOK)
        xh3 = cut(late, 3120, NP, E)
        xaP = cut(late, 5168, KT, NB, LP)
        sx = cut(late, 6208, KT, TOK)
        xm = cut(late, 7232, 2, KT, TOK)
        xf = cut(late, 9280, 2, TOK)
        vj = cut(late, 5168, 3, PT)
        aj = cut(late, 6728, 2, PT)
        sj = cut(late, 7768, 2, PT)
        rs = cut(late, 8808, 2, 512)
        ruk = cut(late, 9832, KT, TOK)
        sq = cut(late, 6192, KT, TOK)
        rgn = cut(late, 7216, KT, TOK)
        ogT = cut(late, 8240, KT, TOK)
        x4 = cut(late, 3120, NP, E)
        xh4 = cut(late, 4144, NP, E)
        xcP = cut(late, 0, KT, NB, LP)
        sx2 = cut(late, 1040, KT, TOK)
        xk2 = cut(late, 5168, KT, TOK)
        xr2 = cut(late, 6192, KT, TOK)
        kkT = cut(late, 7216, KT, TOK)
        thn = cut(late, 9264, NP, E)

        def nat(name):
            return a[name].rearrange("b c t -> (b c) t").rearrange("(n p q) t -> n q p t", p=NP, q=128)
        x_in, c_in = nat("x"), nat("ctx_2048")
        out_v = out.rearrange("b c t -> (b c) t").rearrange("(n p q) t -> n q p t", p=NP, q=128)
        mask1_in = a["mask_Bx1xSxS2_ff0"].rearrange("b o l s -> (b o l) s").rearrange(
            "(n p q) s -> n q p s", p=NP, q=128)
        mask2_in = a["mask_BxS2_ik0"].rearrange("(n b) s -> n b s", b=NB)
        s0_in = a["ctx_2048"].rearrange("b c t -> b (c t)")[:, 2 * E:2 * E + HS * E].rearrange(
            "(n b) (k p j) -> n k p b j", b=NB, k=KT, j=HS)

        new_block()
        with nc.Block() as block:
            @block.gpsimd
            def _(pool):
                link = linker(pool, "pool_step")
                link(nc.gpsimd.memset(vrows, 0.0))
                for w in conv.values():
                    nc.gpsimd.memset(w[:, :], 0.0)
                for t in (wo1, maa2, td2, vbd, pick):
                    nc.gpsimd.memset(t[:, :] if len(t.shape) == 2 else t[tuple([slice(None)] * len(t.shape))], 0.0)
                nc.gpsimd.memset(eps5[:, :], 1e-5)
                nc.gpsimd.memset(eps6[:, :], 1e-6)
                nc.gpsimd.memset(ones32[:, :], 1.0)
                nc.gpsimd.memset(ones2[:, :], 1.0)
                link(nc.gpsimd.memset(mask2[:, :, :], 0.0))
                pool.sem_inc(sig("zeroed"), 1)

                def band(t, shape, step, width):
                    pattern = [[-step, shape[0]]] + ([[0, shape[1]]] if len(shape) > 1 else [])
                    up = [[step, shape[0]]] + ([[0, shape[1]]] if len(shape) > 1 else [])
                    link(nc.gpsimd.memset(t, 1.0))
                    link(nc.gpsimd.affine_select(out=t, in_=t, compare_op=ALU.is_ge, fill=0.0, base=0,
                                                 pattern=pattern, channel_multiplier=1))
                    link(nc.gpsimd.affine_select(out=t, in_=t, compare_op=ALU.is_ge, fill=0.0, base=width - 1,
                                                 pattern=up, channel_multiplier=-1))
                band(block8[:, :, :], (16, 8), 8, 8)
                band(hmask[:, :], (HPT,), HD2, HD2)
                band(half[:, :, :], (2, 8), 64, 64)
                band(ident[:, :], (128,), 1, 1)
                pool.sem_inc(sig("bands"), 1)

            @block.sync
            def _(sp):
                sp.wait_ge(sig("zeroed"), 1)
                for w in conv:
                    for h in range(2):
                        sp.dma_start(conv[w][64 * h:64 * h + 64, 64 * h:64 * h + 64], a[f"L0_xattn_{w}"]).then_inc(sig("conv_in"), 16)
                L3 = "L3_xattn_"
                srcs = [("gamma", "L1_xattn_gamma"), ("beta", "L1_xattn_beta"), ("q_b", "L2_xattn_q_b"),
                        ("post", "L2_xattn_postnorm_w"), ("b1", "L2_xattn_mlp_b1"), ("ln1_w", L3 + "ln1_w"),
                        ("ln1_b", L3 + "ln1_b"), ("ln2_w", L3 + "ln2_w"), ("ln2_b", L3 + "ln2_b"),
                        ("maa_x", L3 + "maa_x"), ("decay", L3 + "time_decay"), ("gn_w", L3 + "gn_w"),
                        ("gn_b", L3 + "gn_b"), ("ffn_k", L3 + "ffn_maa_k"), ("ffn_r", L3 + "ffn_maa_r")]
                for row, name in srcs:
                    r, n = ROWS[row]
                    sp.dma_start(vrows[r:r + n, :], a[name].rearrange("(n p) -> n p", p=128)).then_inc(sig("rows_in"), 16)
                r, n = ROWS["maa"]
                sp.dma_start(vrows[r:r + n, :], a[L3 + "maa_stack"].rearrange("o f (n p) -> (o f n) p", p=128)).then_inc(sig("rows_in"), 16)
                r, n = ROWS["u"]
                sp.dma_start(vrows[r:r + n, :], a[L3 + "u"].rearrange("h s o -> (h s o)").rearrange("(n p) -> n p", p=128)).then_inc(sig("rows_in"), 16)
                for h in range(2):
                    for row, name in (("bn", "L0_xattn_bn"), ("bm", "L0_xattn_bm"), ("bl", "L0_xattn_bl"),
                                      ("bo", "L0_xattn_bo"), ("bk", "L1_xattn_bk")):
                        r = ROWS[row][0]
                        sp.dma_start(vrows[r:r + 1, 64 * h:64 * h + 64], a[name].rearrange("(o c) -> o c", o=1)).then_inc(sig("rows_in"), 16)
                    r = ROWS["bq"][0]
                    for g in range(GQ):
                        sp.dma_start(vrows[r + g:r + g + 1, 64 * h:64 * h + 64].rearrange("o (k d) -> o k d", d=HD1),
                                     a["L1_xattn_bq"].rearrange("(o k g d) -> g o k d", o=1, g=GQ, d=HD1)[g]).then_inc(sig("rows_in"), 16)
                r = ROWS["bv"][0]
                sp.dma_start(vrows[r:r + 1, :].rearrange("o (j e) -> o j e", e=32)[:, :, 0:16],
                             a["L1_xattn_bv"].rearrange("(o j e) -> o j e", o=1, e=16)).then_inc(sig("rows_in"), 16)
                with nc.allow_non_contiguous_dma(reason="interleaved biases"):
                    for row, s in (("k_b", 0), ("v_b", 1)):
                        r, n = ROWS[row]
                        sp.dma_start(vrows[r:r + n, :].unsqueeze(2),
                                     a["L2_xattn_kv_b"].rearrange("(n p s) -> s n p", p=128, s=2)[s].unsqueeze(2)).then_inc(sig("rows_in"), 16)
                sp.wait_ge(sig("rows_in"), 16 * (len(srcs) + 2 + 10 + 2 * GQ + 1 + 2))
                sp.sem_inc(sig("rows_all"), 1)
                for t, name in ((row1, "L1_xattn_bo"), (row2, "L2_xattn_out_b"), (row_b2, "L2_xattn_mlp_b2"),
                                (row_gamma, "L1_xattn_gamma"), (cut(late, 1536, E), "L1_xattn_beta")):
                    sp.dma_start(t[:, :], a[name].rearrange("(o n) -> o n", o=1).broadcast_to([128, E])).then_inc(sig("spread_in"), 16)
                sp.wait_ge(sig("spread_in"), 80)
                sp.sem_inc(sig("spread_all"), 1)

            @block.scalar
            def _(act):
                act.wait_ge(sig("zeroed"), 1)
                for n, w in enumerate(SQUARE):
                    act.dma_start(cut(early, 512 * n, KT, E), a[f"L3_xattn_{w}"].rearrange("(k p) n -> p k n", p=128)).then_inc(sig("square_in"), 16)
                act.dma_start(cut(late, 0, KT, E), a["L2_xattn_out_w"].rearrange("(k p) n -> p k n", p=128)).then_inc(sig("plain_in"), 16)
                for t, name in ((cut(late, 512, KT, E), "L1_xattn_Wq"), (wk1, "L1_xattn_Wk"), (wv1, "L1_xattn_Wv"), (wq2, "L2_xattn_q_w"),
                                (wkv2, "L2_xattn_kv_w"), (w1, "L2_xattn_mlp_w1"), (w2, "L2_xattn_mlp_w2"),
                                (maa1, "L3_xattn_maa_w1"), (td1, "L3_xattn_td_w1")):
                    act.dma_start(t[:, :, :], a[name].rearrange("(k p) n -> p k n", p=128)).then_inc(sig("plain_in"), 16)
                for j in range(4):
                    for k in range(2):
                        act.dma_start(wo1[32 * j + 8 * k:32 * j + 8 * k + 8, :, :],
                                      a["L1_xattn_Wo"].rearrange("(k g d) n -> k d g n", g=GQ, d=HD1)[2 * j + k]).then_inc(sig("plain_in"), 16)
                act.dma_start(maa2[:, 0, :][0:32], a["L3_xattn_maa_w2"][0]).then_inc(sig("plain_in"), 16)
                for f in range(1, NMIX):
                    r = 32 * (f % 4)
                    act.dma_start(maa2[r:r + 32, f, :], a["L3_xattn_maa_w2"][f]).then_inc(sig("plain_in"), 16)
                act.dma_start(td2[64:64 + DD, :], a["L3_xattn_td_w2"]).then_inc(sig("plain_in"), 16)
                act.wait_ge(sig("plain_in"), 16 * (1 + 9 + 8 + 5 + 1))
                act.sem_inc(sig("plain_all"), 1)

            @block.tensor
            def _(pe):
                pe.wait_ge(sig("bands"), 1)
                pe.wait_ge(sig("rows_all"), 1)
                t, full = fill(pe, "turn", "vec")
                nc.tensor.transpose(t[:, 0:128], vrows, ident[:, :]).then_inc(full, 1)
                pe.wait_ge(sig("conv_in"), 128)
                t, full = fill(pe, "turn", "conv")
                for n, w in enumerate(conv):
                    ins = nc.tensor.transpose(t[:, 128 * n:128 * n + 128], conv[w][:, :], ident[:, :])
                ins.then_inc(full, 1)
                pe.wait_ge(sig("square_in"), 16 * len(SQUARE))
                for n, w in enumerate(SQUARE):
                    t, full = fill(pe, "turn", w)
                    src = cut(early, 512 * n, KT, E)
                    for i in range(KT):
                        for o in range(KT):
                            ins = nc.tensor.transpose(t[:, 256 * i + 128 * o:256 * i + 128 * o + 128],
                                                      src[:, o, 128 * i:128 * i + 128], ident[:, :])
                    ins.then_inc(full, 1)
                pe.wait_ge(sig("plain_all"), 1)
                pe.wait_ge(sig("bias_spread"), 1)
                t, full = fill(pe, "turn", "row1")
                for g in range(GQ):
                    ins = nc.tensor.matmul(t[:, 0:E], cut(late, 1024, 3, 128)[:, 0, :], wo1[:, g, :], start=g == 0, stop=g == GQ - 1)
                ins.then_inc(full, 1)
                t, full = fill(pe, "turn", "row2")
                for k in range(KT):
                    ins = nc.tensor.matmul(t[:, 0:E], cut(late, 1024, 3, 128)[:, 1 + k, :], cut(late, 0, KT, E)[:, k, :], start=k == 0, stop=k == KT - 1)
                ins.then_inc(full, 1)

            @block.vector
            def _(dve):
                link = linker(dve, "dve_step")
                dve.wait_ge(sig("bands"), 1)
                flat8 = block8[:, :, :].rearrange("p a b -> p (a b)")
                nc.vector.tensor_tensor(kvmask[:, :], block8[:, 0:8, 0], block8[:, 8:16, 0], ALU.add)
                nc.vector.tensor_reduce(parity[:, :], hmask[:, :].rearrange("p (j h) -> p h j", h=2), X, ALU.add)
                nc.vector.tensor_copy(ones2[:, 0:16], half[:, :, :].rearrange("p a b -> p (a b)"))
                link(nc.vector.scalar_tensor_tensor(out=center8[:, :], in0=flat8, scalar=-1.0 / HS, in1=ident[:, :], op0=ALU.mult, op1=ALU.add))
                for j in range(HS):
                    nc.vector.tensor_copy(pick[:, j, :].rearrange("p (h j) -> p h j", j=HS)[:, :, j], block8[:, :, j])
                t, free = take(dve, "vec")
                link(nc.vector.tensor_copy(vec[:, :], t[:, 0:128]))
                dve.sem_inc(free, 1)
                for w in ("gn_w", "gn_b"):
                    r = ROWS[w][0]
                    nc.vector.tensor_scalar(vec[:, r:r + 2], vec[:, r:r + 2], 0.5, None, ALU.mult)
                bias = cut(late, 1024, 3, 128)
                for n, col in enumerate((v("bv"), v("v_b", 0), v("v_b", 1))):
                    ins = nc.vector.tensor_copy(bias[:, n, :], col.broadcast_to([128, 128]))
                ins.then_inc(sig("bias_spread"), 1)
                t, free = take(dve, "conv")
                for n, w in enumerate(conv):
                    ins = nc.vector.tensor_copy(conv[w][:, :], t[:, 128 * n:128 * n + 128])
                ins.then_inc(free, 1)
                for w in SQUARE:
                    t, free = take(dve, w)
                    nc.vector.tensor_copy(wt[w][:, :, :].rearrange("p k n -> p (k n)"), t[:, :]).then_inc(free, 1)
                dve.wait_ge(sig("plain_all"), 1)
                for k in range(KT):
                    nc.vector.tensor_copy(wq1[:, k, :, :].rearrange("p g (h d) -> p h g d", d=HD1),
                                          cut(late, 512, KT, KVH, GQ, HD1)[:, k])
                    for h in range(2):
                        nc.vector.tensor_scalar(wo2[:, k, h, :], cut(late, 0, KT, E)[:, k, :], parity[:, h:h + 1], None, ALU.mult)
                dve.wait_ge(sig("spread_all"), 1)
                t, free = take(dve, "row1")
                nc.vector.tensor_tensor(row1[:, :], t[:, 0:E], row1[:, :], ALU.add).then_inc(free, 1)
                t, free = take(dve, "row2")
                link(nc.vector.tensor_tensor(row2[:, :], t[:, 0:E], row2[:, :], ALU.add))
                dve.sem_inc(free, 1)
                for t in (row2, row_b2):
                    nc.vector.tensor_tensor(t[:, :], t[:, :], cut(late, 1536, E), ALU.add)

        def clear_all():
            nums = sorted(s.num for s in sems.values())
            with nc.Block() as between:
                @between.gpsimd
                def _(pool):
                    lo = nums[0]
                    for n, m in zip(nums, nums[1:] + [None]):
                        if m != n + 1:
                            pool.sem_clear(range(lo, n + 1))
                            lo = m
        LOG_EXP, TANH, GELU = "natural_log_exp_and_others", "exp_and_others", "gelu_apprx_tanh_and_others"

        SCANS = KT * HS + 3
        STAGES = (["moments", "normalize", "turn", "shift", "maa", "mix 0", "mix 1", "td", "k", "mix 2", "decay", "v",
                   "mix 3", "mix 4", "r", "g", "r u k", "bonus"] + [("scan", n) for n in range(SCANS)] +
                  ["center", "variance", "gate", "project", "moments 2", "normalize 2", "turn 2", "shift 2", "ffn k", "ffn r", "ffn v"])
        MIXES = (1, 0, 2, 3, 4)
        due, at = {}, 0.0
        for stage in STAGES:
            due.setdefault(int(at), []).append(stage)
            at += 1.25 if stage[0] == "scan" else 2.1

        U0, STEPS0 = 2 * NP, 2 * NP + 8
        UNITS, STEPS = 4 * NP, 4 * NP + 11

        def group_block(now, before):
            new_block()

            def beside(layer3):
                count = [0]

                def step():
                    for stage in due.get(count[0], []) if before is not None else []:
                        layer3(stage)
                    count[0] += 1

                def rest():
                    while count[0] <= max(due):
                        step()
                return step, rest

            with nc.Block() as block:
                @block.sync
                def _(sp):
                    if now is not None:
                        sp.dma_start(c0[:, :, :], c_in[now]).then_inc(sig("c0_in"), 16)
                        sp.dma_start(x0[:, :, :], x_in[now]).then_inc(sig("x0_in"), 16)
                        sp.dma_start(mask1[:, :, :], mask1_in[now]).then_inc(sig("mask1_in"), 16)
                        sp.dma_start(mask2[:, :, 0:L].bitcast(I32), mask2_in[now].unsqueeze(0).broadcast_to([128, NB, L])).then_inc(sig("mask2_in"), 16)
                    if before is not None:
                        for k in range(KT):
                            sp.dma_start(s0[:, k, :, :], s0_in[before][k]).then_inc(sig("s0_in"), 16)
                        for n in range(KT * HS):
                            k, j = n // HS, n % HS
                            sp.wait_ge(sig("vP_ready"), k + 1)
                            if n < 3:
                                sp.wait_ge(sig("tanh_g"), KT)
                            else:
                                sp.wait_ge(sig("kv_done"), n - 2)
                            sp.dma_start(vj[:, n % 3, :], vP[j::HS, k, :, :].rearrange("h b t -> h (b t)").unsqueeze(1).broadcast_to(
                                [16, HS, PT])).then_inc(sig(f"vj{n % 3}_in"), 16)
                        sp.wait_ge(sig("out_ready"), NP)
                        sp.dma_start(out_v[before], thn[:, :, :]).then_inc(sig("stored"), 16)
                        sp.wait_ge(sig("stored"), 16)

                @block.tensor
                def _(pe):
                    mm, tr = nc.tensor.matmul, nc.tensor.transpose

                    def product(tile, cols, terms, ring="turn"):
                        t, full = fill(pe, ring, tile)
                        for n, (lhsT, rhs) in enumerate(terms):
                            ins = mm(t[0:lhsT_cols(lhsT), 0:cols], lhsT, rhs, start=n == 0, stop=n == len(terms) - 1)
                        ins.then_inc(full, 1)

                    def flip(tile, src, ring="turn"):
                        for k in range(KT):
                            t, full = fill(pe, ring, (tile, k))
                            for p in range(NP):
                                ins = tr(t[:, 128 * p:128 * p + 128], src[:, p, 128 * k:128 * k + 128], ident[:, :])
                            ins.then_inc(full, 1)

                    def natural(tile, q, lhsT, rhs, ring="turn"):
                        t, full = fill(pe, ring, (tile, q))
                        for p in range(2):
                            for k, r in enumerate(rhs):
                                ins = mm(t[:, E * p:E * p + E], lhsT(2 * q + p, k), r, start=k == 0, stop=k == len(rhs) - 1)
                        ins.then_inc(full, 1)

                    def layer3(stage):
                        def mix(f):
                            for m in range(KT):
                                product((stage, m), 512, [(maa2[:, f, 128 * m:128 * m + 128], xf[:, f // 4, :])], "late")

                        def square(w, moving):
                            for m in range(KT):
                                product((stage, m), 512, [(wt[w][:, k, 128 * m:128 * m + 128], moving(k)) for k in range(KT)], "late")

                        def mixed(n, w):
                            pe.wait_ge(sig("xm_ready"), KT * (n + 1))
                            square(w, lambda k: xm[:, (n + 1) % 2, k, :])

                        def project(w, moving):
                            for q in range(2):
                                natural(stage, q, lambda p, k: moving[:, k, 128 * p:128 * p + 128], [wt[w][:, k, :] for k in range(KT)], "late")

                        if stage == "turn":
                            pe.wait_ge(sig("xh3_ready"), NP)
                            flip(stage, xh3, "late")
                        elif stage == "maa":
                            pe.wait_ge(sig("x1m_ready"), KT)
                            product("maaA", 512, [(maa1[:, k, 0:128], xm[:, 0, k, :]) for k in range(KT)], "late")
                            product("maaB", 512, [(maa1[:, k, 128:160], xm[:, 0, k, :]) for k in range(KT)], "late")
                        elif stage[0:3] == "mix":
                            pe.wait_ge(sig("xf_ready"), 2)
                            pe.wait_ge(sig("xf_zero"), 1)
                            mix(MIXES[int(stage[4])])
                        elif stage == "td":
                            pe.wait_ge(sig("xm_ready"), KT)
                            product("td", 512, [(td1[:, k, :], xm[:, 1, k, :]) for k in range(KT)], "late")
                        elif stage == "decay":
                            pe.wait_ge(sig("td_ready"), 1)
                            for m in range(KT):
                                product((stage, m), 512, [(td2[:, 128 * m:128 * m + 128], xf[:, 1, :])], "late")
                        elif stage == "k":
                            mixed(1, "Wk")
                        elif stage == "v":
                            mixed(2, "Wv")
                        elif stage == "r":
                            mixed(3, "Wr")
                        elif stage == "g":
                            mixed(4, "Wg")
                        elif stage == "bonus":
                            for k in range(KT):
                                pe.wait_ge(sig("ruk_ready"), k + 1)
                                product((stage, k), 512, [(block8[:, :, :], ruk[:, k, :])], "late")
                        elif stage[0] == "scan":
                            n = stage[1] - 2
                            if 0 <= n < KT * HS:
                                k, j = n // HS, n % HS
                                if j == 0:
                                    t, full = fill(pe, "late", ("o3", k))
                                else:
                                    b, c = place["o3", k]
                                    t, full = banks[b], sig(f"bank{b}_full")
                                pe.wait_ge(sig("rs_ready"), n + 1)
                                mm(t[:, :], pick[:, j, :], rs[:, j % 2, :], start=j == 0, stop=j == HS - 1).then_inc(
                                    full if j == HS - 1 else sig("rs_used"), 1)
                        elif stage == "center":
                            for k in range(KT):
                                pe.wait_ge(sig("o3_ready"), k + 1)
                                product((stage, k), 512, [(center8[:, :], ruk[:, k, :])], "late")
                        elif stage == "variance":
                            for k in range(KT):
                                pe.wait_ge(sig("sq_ready"), k + 1)
                                product((stage, k), 512, [(block8[:, :, :], sq[:, k, :])], "late")
                        elif stage == "project":
                            pe.wait_ge(sig("ogT_ready"), KT)
                            project("Wo", ogT)
                        elif stage == "turn 2":
                            pe.wait_ge(sig("xh4_ready"), NP)
                            flip(stage, xh4, "late")
                        elif stage == "ffn k":
                            pe.wait_ge(sig("xk2_ready"), KT)
                            square("Wfk", lambda k: xk2[:, k, :])
                        elif stage == "ffn r":
                            pe.wait_ge(sig("xr2_ready"), KT)
                            project("Wfr", xr2)
                        elif stage == "ffn v":
                            pe.wait_ge(sig("kk_ready"), KT)
                            project("Wfv", kkT)

                    step, rest = beside(layer3)
                    if now is None:
                        rest()
                        return

                    pe.wait_ge(sig("c0_in"), 16)
                    flip("cT", c0)
                    for q in range(2):
                        t, full = fill(pe, "turn", ("ml", q))
                        for p in range(2):
                            for s in range(2):
                                ins = mm(t[:, 256 * p + 128 * s:256 * p + 128 * s + 128], c0[:, 2 * q + p, 128 * s:128 * s + 128],
                                         conv["Wl"][:, :], start=True, stop=True)
                        ins.then_inc(full, 1)
                    pe.wait_ge(sig("ch_ready"), NP)
                    for q in range(2):
                        product(("mm", q), 512, [(conv["Wm"][:, :], ch[:, 2 * q:2 * q + 2, :])])
                    pe.wait_ge(sig("xh_ready"), NP)
                    for q in range(2):
                        product(("mn", q), 512, [(conv["Wn"][:, :], xh0[:, 2 * q:2 * q + 2, :])])

                    def scores0(u):
                        pe.wait_ge(sig("mn_ready"), u // 4 + 1)
                        pe.wait_ge(sig("mmb_ready"), u // 4 + 1)
                        product(("s0", u), 512, [(mn[:, u // 2, 128 * (u % 2):128 * (u % 2) + 128], mmb[:, u // 2, :, :])], "score")

                    def turn0(u):
                        pe.wait_ge(sig("p0_ready"), u + 1)
                        t, full = fill(pe, "turn", ("t0", u))
                        for n in range(4):
                            ins = tr(t[:, 128 * n:128 * n + 128], soft[:, u % SOFT, 128 * n:128 * n + 128], ident[:, :])
                        ins.then_inc(full, 1)

                    def value0(p):
                        pe.wait_ge(sig("pT0_ready"), 2 * p + 2)
                        pe.wait_ge(sig("ml_ready"), p // 2 + 1)
                        t, full = fill(pe, "value", ("o0", p))
                        for b in range(2):
                            for s in range(2):
                                ins = mm(t[64 * b:64 * b + 64, 0:E], mlT[:, p, s, 64 * b:64 * b + 64], pT0[:, p % 2, :, b, s, :],
                                         start=s == 0, stop=s == 1)
                        ins.then_inc(full, 1)

                    for i in range(STEPS0):
                        step()
                        if i < U0:
                            scores0(i)
                        if 2 <= i < U0 + 2:
                            turn0(i - 2)
                        if i >= 5 and (i - 5) % 2 == 0 and (i - 5) // 2 < NP:
                            value0((i - 5) // 2)
                        if i >= 7 and (i - 7) % 2 == 0 and (i - 7) // 2 < NP:
                            p = (i - 7) // 2
                            pe.wait_ge(sig("mo_ready"), p + 1)
                            product(("x1", p), E, [(conv["Wo"][:, :], mo[:, p, :])])

                    pe.wait_ge(sig("cT_ready"), KT)
                    t, full = fill(pe, "turn", "k1")
                    for b in range(2):
                        for k in range(KT):
                            ins = mm(t[64 * b:64 * b + 64, 0:256], wk1[:, k, :], hT[:, k, b::2, 0, :], start=k == 0, stop=k == KT - 1)
                    ins.then_inc(full, 1)
                    t, full = fill(pe, "turn", "v1")
                    for b in range(NB):
                        r = 64 * (b % 2)
                        for k in range(KT):
                            ins = mm(t[r:r + 64, 64 * (b // 2):64 * (b // 2) + 64], hT[:, k, b, 0, :], wv1[:, k, :], start=k == 0, stop=k == KT - 1)
                    ins.then_inc(full, 1)
                    step()
                    pe.wait_ge(sig("x1_ready"), NP)
                    flip("x1T", xA)
                    step()
                    pe.wait_ge(sig("x1T_ready"), KT)
                    for q in range(2):
                        t, full = fill(pe, "turn", ("q1", q))
                        for g in range(2):
                            for b in range(2):
                                for k in range(KT):
                                    ins = mm(t[64 * b:64 * b + 64, 256 * g:256 * g + 256],
                                             wq1[:, k, 2 * q + g, :],
                                             x1T[:, k, :].rearrange("p (n b l) -> p b n l", b=2, l=L)[:, b],
                                             start=k == 0, stop=k == KT - 1)
                        ins.then_inc(full, 1)
                    step()

                    def softmax_layer(y, scores, value, total, result):
                        def turned(u):
                            pe.wait_ge(sig(f"exp{y}"), u + 1)
                            t, full = fill(pe, "turn", (f"t{y}", u))
                            for n in range(4):
                                ins = tr(t[:, 128 * n:128 * n + 128], soft[:, u % SOFT, 128 * n:128 * n + 128], ident[:, :])
                            ins.then_inc(full, 1)

                        def pair(p):
                            pe.wait_ge(sig(f"pT{y}_ready"), 4 * p + 4)
                            for ring, terms in (("value", value), ("total", total)):
                                t, full = fill(pe, ring, (f"{ring}{y}", p))
                                for dst, cols, lhsT, rhs in terms(p):
                                    ins = mm(t[dst:dst + 32, cols[0]:cols[1]], lhsT, rhs, start=True, stop=True)
                                ins.then_inc(full, 1)

                        for i in range(STEPS):
                            step()
                            if i < UNITS:
                                scores(i)
                            if 3 <= i < UNITS + 3:
                                turned(i - 3)
                            if i >= 8 and (i - 8) % 4 == 0 and (i - 8) // 4 < NP:
                                pair((i - 8) // 4)
                            if i >= 10 and (i - 10) % 4 == 0 and (i - 10) // 4 < NP:
                                p = (i - 10) // 4
                                pe.wait_ge(sig(f"at{y}_ready"), p + 1)
                                product((f"out{y}", p), E, result(p))

                    def scores1(u):
                        p, g = u // 4, u % 4
                        pe.wait_ge(sig("kbd_ready"), p + 1)
                        pe.wait_ge(sig("qz_ready"), g // 2 + 1)
                        product(("s1", u), 512, [(qz[:, g, p, :, :], kbd[:, p, :, :])], "score")

                    softmax_layer(
                        1, scores1,
                        lambda p: [(32 * j, (256 * b, 256 * b + 256), vbd[:, 2 * p + b, j, :], pT1[:, p % 2, j, b, :, :])
                                   for b in range(2) for j in range(4)],
                        lambda p: [(32 * j, (256 * b, 256 * b + 256), ones2[:, :], pT1[:, p % 2, j, b, :, :])
                                   for b in range(2) for j in range(4)],
                        lambda p: [(at1[:, p % 2, g, :], wo1[:, g, :]) for g in range(GQ)])
                    pe.wait_ge(sig("xh1_ready"), NP)
                    flip("lT", xh)
                    step()

                    pe.wait_ge(sig("lT_ready"), KT)
                    for h in range(KT):
                        product(("q2", h), 512, [(wq2[:, k, 128 * h:128 * h + 128], hT[:, k, :, 1, :]) for k in range(KT)])
                    step()
                    kv = wkv2[:, :, :].rearrange("p k (n s) -> p s k n", s=2)
                    for h in range(KT):
                        for q in range(2):
                            product(("k2", h, q), 512, [(kv[:, 0, k, 128 * h:128 * h + 128], hT[:, k, 4 * q:4 * q + 4, :, :]) for k in range(KT)])
                    step()
                    for p in range(NP):
                        t, full = fill(pe, "turn", ("v2", p))
                        for b in range(2):
                            for k in range(KT):
                                ins = mm(t[:, 256 * b:256 * b + 256], hT[:, k, 2 * p + b, :, :], kv[:, 1, k, :], start=k == 0, stop=k == KT - 1)
                        ins.then_inc(full, 1)
                    step()

                    def scores2(u):
                        b, h = u // 2, u % 2
                        pe.wait_ge(sig("k2_ready"), 4)
                        pe.wait_ge(sig("qring_ready"), u + 1)
                        t, full = fill(pe, "score", ("s2", u))
                        for j in range(4):
                            ins = mm(t[:, 128 * j:128 * j + 128], qring[:, u % 2, 2 * j:2 * j + 2, :], k2T[:, h, b, :], start=True, stop=True)
                        ins.then_inc(full, 1)

                    pe.wait_ge(sig("v2_ready"), NP)
                    softmax_layer(
                        2, scores2,
                        lambda p: [(32 * j, (256 * b + 128 * h, 256 * b + 128 * h + 128), v2[:, 2 * p + b, 128 * h + 32 * j:128 * h + 32 * j + 32],
                                    pT2[:, (2 * p + b) % 4, h, 128 * j:128 * j + 128]) for b in range(2) for h in range(2) for j in range(4)],
                        lambda p: [(32 * j, (256 * b + 128 * h, 256 * b + 128 * h + 128), ones32[:, :],
                                    pT2[:, (2 * p + b) % 4, h, 128 * j:128 * j + 128]) for b in range(2) for h in range(2) for j in range(4)],
                        lambda p: [(at2[:, p % 2, 2 * h + e, :], wo2[:, h, e, :]) for h in range(KT) for e in range(2)])
                    pe.wait_ge(sig("xh2_ready"), NP)
                    flip("xnT", xh)
                    step()
                    pe.wait_ge(sig("xnT_ready"), KT)
                    for n in range(HID // 128):
                        product(("u", n), 512, [(w1[:, k, 128 * n:128 * n + 128], xnT[:, k, :]) for k in range(KT)])
                        step()
                    pe.wait_ge(sig("gT_ready"), HID // 128)
                    for q in range(2):
                        natural("y2", q, lambda p, k: gT[:, k, 128 * p:128 * p + 128], [w2[:, k, :] for k in range(HID // 128)])
                        step()
                    rest()

                @block.scalar
                def _(act):
                    link = linker(act, "act_step")
                    af = nc.scalar.activation
                    loaded = [None]

                    def tables(name):
                        if loaded[0] != name:
                            nc.scalar.preload_act_table_set(name)
                        loaded[0] = name

                    def rsqrt(dst, src, eps, scale, name):
                        link(af(dst, src, ACT.Ln, bias=eps[:, :], scale=scale))
                        af(dst, dst, ACT.Exp, scale=-0.5).then_inc(sig(name), 1)

                    def batches(ap):
                        return ap.rearrange("p (b l) -> p b l", l=L)

                    def drain(tile, dst, src, func, name, **kw):
                        t, free = take(act, tile)
                        link(af(dst, src(t), func, **kw))
                        act.sem_inc(free, 1)
                        act.sem_inc(sig(name), 1)

                    def layer3(stage):
                        def tanh(work):
                            back = loaded[0]
                            if back != GELU:
                                tables(TANH)
                            work()
                            tables(back)

                        def whole(t):
                            return t[:, :]

                        if stage == "moments":
                            act.wait_ge(sig("stats3_ready"), 1)
                            rsqrt(rstd3[:, :], mv3[:, :, 1], eps5, 1.0, "rstd3_ready")
                        elif stage == "turn":
                            for k in range(KT):
                                drain((stage, k), xaP[:, k, :, 1:LP], lambda t: batches(t[:, :]), ACT.Identity, "xaP_ready",
                                      bias=v("ln1_b", k), scale=v("ln1_w", k))
                        elif stage == "maa":
                            @tanh
                            def _():
                                drain("maaA", xf[:, 0, :], whole, ACT.Tanh, "xf_ready")
                                drain("maaB", xf[0:DM, 1, :], lambda t: t[0:DM, :], ACT.Tanh, "xf_ready")
                        elif stage == "k":
                            for k in range(KT):
                                drain((stage, k), kP[:, k, :, 1:LP], lambda t: batches(t[:, :]), ACT.Identity, "kP_ready")
                        elif stage == "td":
                            @tanh
                            def _():
                                drain("td", xf[64:64 + DD, 1, :], lambda t: t[0:DD, :], ACT.Tanh, "td_ready")
                        elif stage == "decay":
                            for k in range(KT):
                                drain((stage, k), wP[:, k, :, 1:LP], lambda t: batches(t[:, :]), ACT.Exp, "decay_read", bias=v("decay", k))
                            for k in range(KT):
                                af(wP[:, k, :, 1:LP], wP[:, k, :, 1:LP], ACT.Exp, scale=-1.0).then_inc(sig("wP_ready"), 1)
                        elif stage == "v":
                            for k in range(KT):
                                drain((stage, k), vP[:, k, :, 1:LP], lambda t: batches(t[:, :]), ACT.Identity, "vP_ready")
                        elif stage == "r":
                            for k in range(KT):
                                drain((stage, k), rT[:, k, :], whole, ACT.Identity, "rT_ready")
                        elif stage == "g":
                            @tanh
                            def _():
                                for k in range(KT):
                                    t, free = take(act, (stage, k))
                                    link(af(gg[:, k, :], t[:, :], ACT.Tanh, scale=0.5))
                                    link(af(ruk[:, k, :], t[:, :], ACT.Identity))
                                    act.sem_inc(free, 1)
                                    act.sem_inc(sig("tanh_g"), 1)
                        elif stage == "center":
                            for k in range(KT):
                                t, free = take(act, (stage, k))
                                af(ogT[:, k, :], t[:, :], ACT.Identity).then_inc(sig("oc_ready"), 1)
                                link(af(sq[:, k, :], t[:, :], ACT.Square))
                                act.sem_inc(free, 1)
                                act.sem_inc(sig("sq_ready"), 1)
                        elif stage == "variance":
                            for k in range(KT):
                                drain((stage, k), rgn[:, k, :], whole, ACT.Ln, "var_read", bias=eps5[:, :], scale=1.0 / HS)
                            for k in range(KT):
                                af(rgn[:, k, :], rgn[:, k, :], ACT.Exp, scale=-0.5).then_inc(sig("rgn_ready"), 1)
                        elif stage == "moments 2":
                            act.wait_ge(sig("stats4_ready"), 1)
                            rsqrt(rstd3[:, :], mv3[:, :, 1], eps5, 1.0, "rstd4_ready")
                        elif stage == "turn 2":
                            for k in range(KT):
                                drain((stage, k), xcP[:, k, :, 1:LP], lambda t: batches(t[:, :]), ACT.Identity, "xcP_ready",
                                      bias=v("ln2_b", k), scale=v("ln2_w", k))
                        elif stage == "ffn k":
                            for k in range(KT):
                                drain((stage, k), kkT[:, k, :], whole, ACT.Relu, "fk_read")
                            for k in range(KT):
                                af(kkT[:, k, :], kkT[:, k, :], ACT.Square).then_inc(sig("kk_ready"), 1)
                        elif stage == "ffn r":
                            @tanh
                            def _():
                                for q in range(2):
                                    drain((stage, q), thn[:, 2 * q:2 * q + 2, :], lambda t: t[:, :].rearrange("p (n e) -> p n e", n=2),
                                          ACT.Tanh, "thn_ready", scale=0.5)

                    step, rest = beside(layer3)
                    tables(LOG_EXP)
                    if now is None:
                        rest()
                        return

                    act.wait_ge(sig("stats0_ready"), 1)
                    rsqrt(rstd[:, :], mv[:, :, 1], eps5, 1.0, "rstd0_ready")
                    for k in range(KT):
                        drain(("cT", k), hT[:, k, :, 0, :], lambda t: batches(t[:, :]), ACT.Identity, "cT_ready")
                    for q in range(2):
                        t, free = take(act, ("mm", q))
                        if q == 0:
                            act.wait_ge(sig("mmb_zero"), 1)
                        for b in range(2):
                            r = slice(64 * b, 64 * b + 64)
                            ins = af(mmb[r, 2 * q:2 * q + 2, b, :], t[r, :].rearrange("p (n t) -> p n t", n=2),
                                     ACT.Identity, bias=v("bm")[r])
                        link(ins)
                        act.sem_inc(free, 1)
                        act.sem_inc(sig("mmb_ready"), 1)
                    for u in range(STEPS0):
                        if u < U0:
                            t, free = take(act, ("s0", u))
                            act.wait_ge(sig("nmax0_ready"), u + 1)
                            if u >= SOFT:
                                act.wait_ge(sig("pT0_ready"), u - SOFT + 1)
                            for b in range(2):
                                ins = af(soft[:, u % SOFT, 256 * b:256 * b + 256], t[:, 256 * b:256 * b + 256], ACT.Exp,
                                         bias=nmax0[:, u, b:b + 1], accum_out=den0[:, u, b:b + 1])
                            link(ins)
                            act.sem_inc(free, 1)
                            act.sem_inc(sig("exp0"), 1)
                        step()

                    step()
                    for k in range(KT):
                        drain(("x1T", k), x1T[:, k, :], lambda t: t[:, :], ACT.Identity, "x1T_ready")
                    step()
                    for q in range(2):
                        t, free = take(act, ("q1", q))
                        if q == 0:
                            act.wait_ge(sig("qz_zero"), 1)
                        for g in range(2):
                            for b in range(2):
                                r = slice(64 * b, 64 * b + 64)
                                ins = af(qz[r, 2 * q + g, :, b, :], t[r, 256 * g:256 * g + 256].rearrange("p (n l) -> p n l", l=L),
                                         ACT.Identity, bias=v("bq", 2 * q + g)[r])
                        link(ins)
                        act.sem_inc(free, 1)
                        act.sem_inc(sig("qz_ready"), 1)
                    step()

                    def softmax_layer(y, keep, over, deep):
                        def exps(u):
                            act.wait_ge(sig(f"sub{y}"), u + 1)
                            af(soft[:, u % SOFT, :], soft[:, u % SOFT, :], ACT.Exp).then_inc(sig(f"exp{y}"), 1)

                        def turned(u):
                            t, free = take(act, (f"t{y}", u))
                            keep(u, t).then_inc(sig(f"pT{y}_ready"), 1)
                            act.wait_ge(sig(f"pT{y}_ready"), u + 1)
                            act.sem_inc(free, 1)

                        def totals(p):
                            t, free = take(act, (f"total{y}", p))
                            if p >= deep:
                                act.wait_ge(sig(f"at{y}_ready"), p - deep + 1)
                            link(af(over[:, p % deep, :], t[:, :], ACT.Ln))
                            act.sem_inc(free, 1)
                            af(over[:, p % deep, :], over[:, p % deep, :], ACT.Exp, scale=-1.0).then_inc(sig(f"over{y}_ready"), 1)

                        for i in range(STEPS):
                            if 3 <= i < UNITS + 3:
                                turned(i - 3)
                            if i < UNITS:
                                exps(i)
                            if i >= 8 and (i - 8) % 4 == 0 and (i - 8) // 4 < NP:
                                totals((i - 8) // 4)
                            step()

                    softmax_layer(1, lambda u, t: af(pT1[:, (u // 4) % 2, :, :, u % 4, :],
                                                     t[:, :].rearrange("p (j b l) -> p j b l", j=4, b=2), ACT.Identity), over1, 2)
                    act.wait_ge(sig("stats1_ready"), 1)
                    rsqrt(rstd[:, 0:NP], mv[:, 0:NP, 1], eps6, 1.0, "rstd1_ready")
                    for k in range(KT):
                        drain(("lT", k), hT[:, k, :, 1, :], lambda t: batches(t[:, :]), ACT.Identity, "lT_ready",
                              bias=v("beta", k), scale=v("gamma", k))
                    step()

                    step()
                    for h in range(KT):
                        for q in range(2):
                            drain(("k2", h, q), k2T[:, h, 4 * q:4 * q + 4, :], lambda t: t[:, :].rearrange("p (b n) -> p b n", n=KEYS),
                                  ACT.Identity, "k2_ready", bias=v("k_b", h))
                    step()
                    step()
                    softmax_layer(2, lambda u, t: af(pT2[:, (u // 2) % 4, u % 2, :], t[:, :], ACT.Identity), over2, 1)
                    for p in range(NP):
                        act.wait_ge(sig("ao_ready"), p + 1)
                        link(af(xh[:, p, :], xr[:, p, :], ACT.Square, accum_out=stats[:, p, 0:1]))
                    rsqrt(rstd[:, 0:NP], stats[:, 0:NP, 0], eps6, 1.0 / E, "rstd2_ready")
                    for k in range(KT):
                        drain(("xnT", k), xnT[:, k, :], lambda t: t[:, :], ACT.Identity, "xnT_ready", scale=v("post", k))
                    step()
                    tables(GELU)
                    for n in range(HID // 128):
                        drain(("u", n), gT[:, n, :], lambda t: t[:, :], ACT.Gelu_apprx_tanh, "gT_ready", bias=v("b1", n))
                        step()
                    for q in range(2):
                        step()
                    rest()

                @block.vector
                def _(dve):
                    link = linker(dve, "dve_step")
                    tt, ts, stt = nc.vector.tensor_tensor, nc.vector.tensor_scalar, nc.vector.scalar_tensor_tensor

                    def filled(tile):
                        b, n = place[tile]
                        dve.wait_ge(sig(f"bank{b}_full"), n)

                    def batches(ap):
                        return ap.rearrange("p (b l) -> p b l", l=L)

                    def flat(ap):
                        return ap.rearrange("p n e -> p (n e)")

                    def moments(srcs, st, out_mv, name):
                        for n, s in enumerate(srcs):
                            ins = nc.vector.bn_stats(st[:, n, :], s)
                        link(ins)
                        for n in range(len(srcs)):
                            ins = nc.vector.bn_aggr(out_mv[:, n, :], st[:, n, :])
                        link(ins)
                        dve.sem_inc(sig(name), 1)

                    def normalize(dst, src, m, r, name):
                        for p in range(NP):
                            ts(dst[:, p, :], src[:, p, :], m[:, p, 0:1], r[:, p:p + 1], ALU.subtract, ALU.mult).then_inc(sig(name), 1)

                    def layer3(stage):
                        def mix(n, f):
                            if n:
                                filled({1: "maaB", 2: "td", 3: ("k", 1), 4: ("v", 1)}[n])
                            for k in range(KT):
                                t, free = take(dve, (stage, k))
                                m = xm[:, (n + 1) % 2, k, :]
                                link(stt(out=m, in0=t[:, :], scalar=v("maa", 2 * f + k), in1=sx[:, k, :], op0=ALU.add, op1=ALU.mult))
                                dve.sem_inc(free, 1)
                                tt(batches(m), batches(m), xaP[:, k, :, 1:LP], ALU.add).then_inc(sig("xm_ready"), 1)

                        def scan(n):
                            k = n // HS
                            dve.wait_ge(sig("aj_ready"), n + 1)
                            if n >= 2:
                                dve.wait_ge(sig("rs_ready"), n - 1)
                            nc.vector.tensor_tensor_scan(sj[:, n % 2, :], wP[:, k, :, :].rearrange("p b t -> p (b t)"), aj[:, n % 2, :], 0.0,
                                                         ALU.mult, ALU.add).then_inc(sig("sj_ready"), 1)

                        def read(n):
                            k = n // HS
                            dve.wait_ge(sig("sj_ready"), n + 1)
                            if n >= 2:
                                m = n - 2
                                if m % HS == HS - 1:
                                    filled(("o3", m // HS))
                                else:
                                    dve.wait_ge(sig("rs_used"), m - m // HS + 1)
                            tt(batches(rs[:, n % 2, :]), batches(rT[:, k, :]),
                               sj[:, n % 2, :].rearrange("p (b t) -> p b t", t=LP)[:, :, 0:L], ALU.mult).then_inc(sig("rs_ready"), 1)

                        def heads(k):
                            t, free = take(dve, ("o3", k))
                            link(tt(ruk[:, k, :], t[:, :], ruk[:, k, :], ALU.add))
                            dve.sem_inc(free, 1)
                            dve.sem_inc(sig("o3_ready"), 1)

                        if stage == "moments":
                            moments([x3[:, p, :] for p in range(NP)], stats3, mv3, "stats3_ready")
                        elif stage == "normalize":
                            dve.wait_ge(sig("rstd3_ready"), 1)
                            normalize(xh3, x3, mv3, rstd3, "xh3_ready")
                        elif stage == "shift":
                            dve.wait_ge(sig("edge3_ready"), 1)
                            for k in range(KT):
                                dve.wait_ge(sig("xaP_ready"), k + 1)
                                s = batches(sx[:, k, :])
                                link(tt(s, xaP[:, k, :, 0:L], xaP[:, k, :, 1:LP], ALU.subtract))
                                stt(out=batches(xm[:, 0, k, :]), in0=s, scalar=v("maa_x", k), in1=xaP[:, k, :, 1:LP],
                                    op0=ALU.mult, op1=ALU.add).then_inc(sig("x1m_ready"), 1)
                        elif stage[0:3] == "mix":
                            n = int(stage[4])
                            mix(n, MIXES[n])
                        elif stage == "r u k":
                            dve.wait_ge(sig("rT_ready"), KT)
                            dve.wait_ge(sig("wP_ready"), KT)
                            dve.wait_ge(sig("kP_ready"), KT)
                            dve.wait_ge(sig("tanh_g"), KT)
                            for k in range(KT):
                                link(stt(out=gg[:, k, :], in0=gg[:, k, :], scalar=1.0, in1=ruk[:, k, :], op0=ALU.add, op1=ALU.mult))
                                stt(out=batches(ruk[:, k, :]), in0=batches(rT[:, k, :]), scalar=v("u", k),
                                    in1=kP[:, k, :, 1:LP], op0=ALU.mult, op1=ALU.mult).then_inc(sig("ruk_ready"), 1)
                        elif stage == "bonus":
                            dve.wait_ge(sig("vP_ready"), KT)
                            for k in range(KT):
                                t, free = take(dve, (stage, k))
                                link(tt(batches(ruk[:, k, :]), batches(t[:, :]), vP[:, k, :, 1:LP], ALU.mult))
                                dve.sem_inc(free, 1)
                        elif stage[0] == "scan":
                            n = stage[1]
                            if n < KT * HS:
                                scan(n)
                            if 1 <= n < KT * HS + 1:
                                read(n - 1)
                            if n in (HS + 2, 2 * HS + 2):
                                heads(n // HS - 1)
                        elif stage == "gate":
                            for k in range(KT):
                                dve.wait_ge(sig("oc_ready"), k + 1)
                                dve.wait_ge(sig("rgn_ready"), k + 1)
                                link(tt(ogT[:, k, :], ogT[:, k, :], rgn[:, k, :], ALU.mult))
                                link(ts(ogT[:, k, :], ogT[:, k, :], v("gn_w", k), v("gn_b", k), ALU.mult, ALU.add))
                                tt(ogT[:, k, :], ogT[:, k, :], gg[:, k, :], ALU.mult).then_inc(sig("ogT_ready"), 1)
                        elif stage == "project":
                            for q in range(2):
                                t, free = take(dve, (stage, q))
                                link(tt(flat(x4[:, 2 * q:2 * q + 2, :]), t[:, :], flat(x3[:, 2 * q:2 * q + 2, :]), ALU.add))
                                dve.sem_inc(free, 1)
                        elif stage == "moments 2":
                            moments([x4[:, p, :] for p in range(NP)], stats3, mv3, "stats4_ready")
                        elif stage == "normalize 2":
                            dve.wait_ge(sig("rstd4_ready"), 1)
                            normalize(xh4, x4, mv3, rstd3, "xh4_ready")
                        elif stage == "shift 2":
                            dve.wait_ge(sig("edge4_ready"), 1)
                            for k in range(KT):
                                dve.wait_ge(sig("xcP_ready"), k + 1)
                                s = batches(sx2[:, k, :])
                                link(tt(s, xcP[:, k, :, 0:L], xcP[:, k, :, 1:LP], ALU.subtract))
                                for dst, name in ((xk2, "k"), (xr2, "r")):
                                    stt(out=batches(dst[:, k, :]), in0=s, scalar=v(f"ffn_{name}", k), in1=xcP[:, k, :, 1:LP],
                                        op0=ALU.mult, op1=ALU.add).then_inc(sig(f"x{name}2_ready"), 1)
                        elif stage == "ffn v":
                            for q in range(2):
                                t, free = take(dve, (stage, q))
                                dve.wait_ge(sig("thn_ready"), q + 1)
                                th = flat(thn[:, 2 * q:2 * q + 2, :])
                                link(stt(out=th, in0=th, scalar=1.0, in1=t[:, :], op0=ALU.add, op1=ALU.mult))
                                dve.sem_inc(free, 1)
                                stt(out=th, in0=th, scalar=0.5, in1=flat(x4[:, 2 * q:2 * q + 2, :]),
                                    op0=ALU.mult, op1=ALU.add).then_inc(sig("out_ready"), 2)

                    step, rest = beside(layer3)
                    if now is None:
                        rest()
                        return

                    dve.wait_ge(sig("c0_in"), 16)
                    dve.wait_ge(sig("x0_in"), 16)
                    moments([c0[:, p, :] for p in range(NP)] + [x0[:, p, :] for p in range(NP)], stats, mv, "stats0_ready")
                    for q in range(2):
                        t, free = take(dve, ("ml", q))
                        link(nc.vector.tensor_copy(mlT[:, 2 * q:2 * q + 2, :, :].rearrange("p n s o -> p (n s o)"), t[:, :]))
                        dve.sem_inc(free, 1)
                        dve.sem_inc(sig("ml_ready"), 1)
                    dve.wait_ge(sig("rstd0_ready"), 1)
                    normalize(ch, c0, mv, rstd, "ch_ready")
                    normalize(xh0, x0, mv[:, NP:, :], rstd[:, NP:], "xh_ready")
                    for q in range(2):
                        t, free = take(dve, ("mn", q))
                        link(ts(flat(mn[:, 2 * q:2 * q + 2, :]), t[:, :], v("bn"), None, ALU.add))
                        dve.sem_inc(free, 1)
                        dve.sem_inc(sig("mn_ready"), 1)
                    for i in range(STEPS0 + 1):
                        if i < U0:
                            t, _ = take(dve, ("s0", i))
                            nc.vector.tensor_reduce(nmax0[:, i, :], t[:, :].rearrange("p (b s) -> p b s", b=2), X, ALU.max,
                                                    negate=True).then_inc(sig("nmax0_ready"), 1)
                        if 1 <= i < U0 + 1:
                            dve.wait_ge(sig("exp0"), i)
                            nc.vector.reciprocal(rden0[:, i - 1, :], den0[:, i - 1, :]).then_inc(sig("rden0_ready"), 1)
                        if 3 <= i < U0 + 3:
                            u = i - 3
                            t, free = take(dve, ("t0", u))
                            if u >= 4:
                                filled(("o0", u // 2 - 2))
                            nc.vector.tensor_copy(pT0[:, (u // 2) % 2, u % 2].rearrange("p b s t -> p (b s t)"), t[:, :]).then_inc(sig("pT0_ready"), 1)
                            dve.wait_ge(sig("pT0_ready"), u + 1)
                            dve.sem_inc(free, 1)
                        if i >= 6 and (i - 6) % 2 == 0 and (i - 6) // 2 < NP:
                            p = (i - 6) // 2
                            t, free = take(dve, ("o0", p))
                            link(ts(mo[:, p, :], t[:, 0:E], v("bl"), None, ALU.add))
                            dve.sem_inc(free, 1)
                            dve.sem_inc(sig("mo_ready"), 1)
                        if i >= 8 and (i - 8) % 2 == 0 and (i - 8) // 2 < NP:
                            p = (i - 8) // 2
                            t, free = take(dve, ("x1", p))
                            link(stt(out=xA[:, p, :], in0=t[:, 0:E], scalar=v("bo"), in1=x0[:, p, :], op0=ALU.add, op1=ALU.add))
                            dve.sem_inc(free, 1)
                            dve.sem_inc(sig("x1_ready"), 1)
                        if i < STEPS0:
                            step()

                    t, free = take(dve, "k1")
                    link(ts(kT1[:, :, :].rearrange("p n s -> p (n s)"), t[:, 0:256], v("bk"), None, ALU.add))
                    dve.sem_inc(free, 1)
                    dve.sem_inc(sig("kT1_ready"), 1)
                    t, free = take(dve, "v1")
                    for b in range(2):
                        for h in range(2):
                            src = t[64 * b:64 * b + 64, 0:256].rearrange("p (n j h d) -> p h n j d", n=NP, h=2, d=HD1)[:, h]
                            ins = nc.vector.tensor_copy(vbd[64 * h:64 * h + 64, b::2, :, 8 * h:8 * h + 8], src)
                    link(ins)
                    dve.sem_inc(free, 1)
                    for _ in range(3):
                        step()

                    def softmax_layer(y, segs, scale, mask, queries, at, xres, name, over, deep):
                        n = 512 // segs

                        def masked(u):
                            t, free = take(dve, (f"s{y}", u))
                            if u >= SOFT:
                                dve.wait_ge(sig(f"pT{y}_ready"), u - SOFT + 1)
                            stt(out=soft[:, u % SOFT, :].rearrange("p (h s) -> p h s", s=n), in0=t[:, :].rearrange("p (h s) -> p h s", s=n),
                                scalar=scale, in1=mask(u).unsqueeze(1).broadcast_to([128, segs, n]),
                                op0=ALU.mult, op1=ALU.add).then_inc(free, 1)

                        def largest(u):
                            b, k = place[(f"s{y}", u)]
                            dve.wait_ge(sig(f"bank{b}_free"), k)
                            nc.vector.tensor_reduce(seg_max[:, u % SOFT, 0:segs], soft[:, u % SOFT, :].rearrange("p (h s) -> p h s", s=n),
                                                    X, ALU.max).then_inc(sig(f"max{y}"), 1)

                        def pairs(ap):
                            return ap.rearrange("p (b g l) -> p b g l", b=2, g=4)

                        def divide(p):
                            t, free = take(dve, (f"value{y}", p))
                            dve.wait_ge(sig(f"over{y}_ready"), p + 1)
                            if p >= 2:
                                filled((f"out{y}", p - 2))
                            link(tt(at(p), pairs(t[:, :]), pairs(over[:, p % deep, :]), ALU.mult))
                            dve.sem_inc(free, 1)
                            dve.sem_inc(sig(f"at{y}_ready"), 1)

                        def add(p):
                            t, free = take(dve, (f"out{y}", p))
                            dve.wait_ge(sig(xres), p + 1)
                            link(tt(xr[:, p, :], t[:, 0:E], xr[:, p, :], ALU.add))
                            dve.sem_inc(free, 1)
                            dve.sem_inc(sig(name), 1)

                        for i in range(STEPS):
                            if 1 <= i < UNITS + 1:
                                largest(i - 1)
                            if i < UNITS:
                                masked(i)
                                queries(i)
                            if i >= 9 and (i - 9) % 4 == 0 and (i - 9) // 4 < NP:
                                divide((i - 9) // 4)
                            if i >= 11 and (i - 11) % 4 == 0 and (i - 11) // 4 < NP:
                                add((i - 11) // 4)
                            step()

                    dve.wait_ge(sig("mask1_in"), 16)
                    softmax_layer(1, KVH, HD1 ** -0.5, lambda u: mask1[:, u // 4, :], lambda u: None,
                                  lambda p: at1[:, p % 2].rearrange("p g (b l) -> p b g l", b=2), "xr1_ready", "x2_ready", over1, 2)
                    moments([xr[:, p, :] for p in range(NP)], stats, mv, "stats1_ready")
                    dve.wait_ge(sig("rstd1_ready"), 1)
                    normalize(xh, xr, mv, rstd, "xh1_ready")
                    step()

                    for h in range(KT):
                        t, free = take(dve, ("q2", h))
                        link(ts(q2T[:, h, :, :].rearrange("p b l -> p (b l)"), t[:, :], v("q_b", h), None, ALU.add))
                        dve.sem_inc(free, 1)
                    step()
                    step()
                    for p in range(NP):
                        t, free = take(dve, ("v2", p))
                        link(nc.vector.tensor_copy(v2[:, 2 * p:2 * p + 2, :].rearrange("p b n -> p (b n)"), t[:, :]))
                        dve.sem_inc(free, 1)
                        dve.sem_inc(sig("v2_ready"), 1)

                    def one_query(u):
                        if u >= 2:
                            filled(("s2", u - 2))
                        tt(qring[:, u % 2, :, :], q2T[:, u % 2, u // 2, :].unsqueeze(1).broadcast_to([128, HPT, L]),
                           hmask[:, :].unsqueeze(2).broadcast_to([128, HPT, L]), ALU.mult).then_inc(sig("qring_ready"), 1)

                    for u in range(2):
                        one_query(u)
                    dve.wait_ge(sig("mask2_ready"), 1)
                    step()
                    softmax_layer(2, 4, 1.0 / HD2, lambda u: mask2[:, u // 2, :], lambda u: one_query(u + 2) if u + 2 < UNITS else None,
                                  lambda p: at2[:, p % 2].rearrange("p g (b l) -> p b g l", b=2), "xr2_ready", "ao_ready", over2, 1)
                    dve.wait_ge(sig("rstd2_ready"), 1)
                    for p in range(NP):
                        ts(xh[:, p, :], xr[:, p, :], rstd[:, p:p + 1], None, ALU.mult).then_inc(sig("xh2_ready"), 1)
                    for _ in range(1 + HID // 128):
                        step()
                    for q in range(2):
                        t, free = take(dve, ("y2", q))
                        dve.wait_ge(sig("xr3_ready"), NP)
                        link(tt(flat(x3[:, 2 * q:2 * q + 2, :]), t[:, :], flat(xr[:, 2 * q:2 * q + 2, :]), ALU.add))
                        dve.sem_inc(free, 1)
                        step()
                    rest()

                @block.gpsimd
                def _(pool):
                    link = linker(pool, "pool_step")
                    tt, ts = nc.gpsimd.tensor_tensor, nc.gpsimd.tensor_scalar

                    def layer3(stage):
                        def products(n):
                            k = n // HS
                            pool.wait_ge(sig(f"vj{n % 3}_in"), 16 * (n // 3 + 1))
                            if n == 0:
                                pool.wait_ge(sig("s0_in"), 16 * KT)
                                pool.wait_ge(sig("kP_ready"), KT)
                            if n >= 2:
                                pool.wait_ge(sig("sj_ready"), n - 1)
                            tt(aj[:, n % 2, :], kP[:, k, :, :].rearrange("p b t -> p (b t)"), vj[:, n % 3, :], ALU.mult).then_inc(sig("kv_done"), 1)
                            pool.wait_ge(sig("kv_done"), n + 1)
                            nc.gpsimd.tensor_copy(aj[:, n % 2, :].rearrange("p (b t) -> p b t", t=LP)[:, :, 0], s0[:, k, :, n % HS]).then_inc(sig("aj_ready"), 1)

                        if stage == "turn":
                            for k in range(KT):
                                nc.gpsimd.tensor_copy(xaP[:, k, :, 0], edge[:, 1, k, :])
                                for t in (kP, vP, wP):
                                    ins = nc.gpsimd.memset(t[:, k, :, 0], 0.0)
                            link(ins)
                            pool.sem_inc(sig("edge3_ready"), 1)
                            link(nc.gpsimd.memset(xf[32:64, 1, :], 0.0))
                            pool.sem_inc(sig("xf_zero"), 1)
                        elif stage == "bonus":
                            products(0)
                        elif stage[0] == "scan" and stage[1] + 1 < KT * HS:
                            products(stage[1] + 1)
                        elif stage == "normalize 2":
                            pool.wait_ge(sig("o3_ready"), KT)
                            for k in range(KT):
                                ins = nc.gpsimd.tensor_copy(xcP[:, k, :, 0], edge[:, 0, k, :])
                            link(ins)
                            pool.sem_inc(sig("edge4_ready"), 1)

                    step, rest = beside(layer3)
                    if now is None:
                        rest()
                        return

                    link(nc.gpsimd.memset(mmb[0:64, :, 1, :], 0.0))
                    link(nc.gpsimd.memset(mmb[64:128, :, 0, :], 0.0))
                    pool.sem_inc(sig("mmb_zero"), 1)
                    link(nc.gpsimd.memset(qz[0:64, :, :, 1, :], 0.0))
                    link(nc.gpsimd.memset(qz[64:128, :, :, 0, :], 0.0))
                    pool.sem_inc(sig("qz_zero"), 1)
                    pool.wait_ge(sig("mask2_in"), 16)
                    m = mask2[:, :, 0:L]
                    ts(m, m.bitcast(I32), 0, MASKED, ALU.is_equal, ALU.mult).then_inc(sig("mask2_ready"), 1)
                    for u in range(STEPS0):
                        if u < U0:
                            pool.wait_ge(sig("rden0_ready"), u + 1)
                            for b in range(2):
                                s = soft[:, u % SOFT, 256 * b:256 * b + 256]
                                ins = ts(s, s, rden0[:, u, b:b + 1], None, ALU.mult)
                            ins.then_inc(sig("p0_ready"), 1)
                        step()

                    pool.wait_ge(sig("kT1_ready"), 1)
                    for p in range(NP):
                        tt(kbd[:, p, :, :], kT1[:, p, :].unsqueeze(1).broadcast_to([128, KVH, L]),
                           kvmask[:, :].unsqueeze(2).broadcast_to([128, KVH, L]), ALU.mult).then_inc(sig("kbd_ready"), 1)
                    pool.wait_ge(sig("x1_ready"), NP)
                    for p in range(NP):
                        tt(xr[:, p, :], xA[:, p, :], row1[:, :], ALU.add).then_inc(sig("xr1_ready"), 1)
                    for _ in range(3):
                        step()

                    def softmax_layer(y, segs):
                        for u in range(STEPS):
                            if u < UNITS:
                                pool.wait_ge(sig(f"max{y}"), u + 1)
                                s = soft[:, u % SOFT, :].rearrange("p (h s) -> p h s", s=512 // segs)
                                tt(s, s, seg_max[:, u % SOFT, 0:segs].unsqueeze(2).broadcast_to([128, segs, 512 // segs]),
                                   ALU.subtract).then_inc(sig(f"sub{y}"), 1)
                            step()
                    softmax_layer(1, KVH)
                    pool.wait_ge(sig("xh1_ready"), NP)
                    for p in range(NP):
                        link(tt(xA[:, p, :], xh[:, p, :], row_gamma[:, :], ALU.mult))
                        tt(xr[:, p, :], xA[:, p, :], row2[:, :], ALU.add).then_inc(sig("xr2_ready"), 1)
                    for _ in range(4):
                        step()

                    softmax_layer(2, 4)
                    pool.wait_ge(sig("xh2_ready"), NP)
                    for p in range(NP):
                        tt(xr[:, p, :], xA[:, p, :], row_b2[:, :], ALU.add).then_inc(sig("xr3_ready"), 1)
                    for _ in range(3 + HID // 128):
                        step()
                    rest()
                    pool.wait_ge(sig("xnT_ready"), KT)
                    for s in range(2):
                        ins = nc.gpsimd.tensor_copy(edge[:, s, :, :], hT[:, :, :, 0, s])
                    link(ins)
            clear_all()

        clear_all()
        last = GROUPS
        group_block(0, None)
        with nc.Fori(1, last) as turn:
            group_block(turn, turn - 1)
        group_block(None, last - 1)


_OUT = (B, L, E)


def kernel(**inputs):
    import numpy as np
    import concourse.bacc as bacc
    from concourse.bass_utils import run_bass_kernel_spmd

    nc = bacc.Bacc("TRN2", target_bir_lowering=False, num_devices=1)
    arrays, aps = {}, {}
    for name, value in inputs.items():
        value = np.ascontiguousarray(value)
        arrays[f"in_{name}"] = value
        aps[name] = nc.dram_tensor(f"in_{name}", value.shape, mybir.dt.from_np(value.dtype), kind="ExternalInput").ap()
    out = nc.dram_tensor("out_x", _OUT, F32, kind="ExternalOutput").ap()
    build(nc, aps, out)
    result = run_bass_kernel_spmd(nc, [arrays], core_ids=[0])
    return result.results[0]["out_x"]
```

```python
from contextlib import ExitStack

import concourse.bass as bass
from concourse import mybir
from concourse.alu_op_type import AluOpType as ALU

F32 = mybir.dt.float32
I32 = mybir.dt.int32
ACT = mybir.ActivationFunctionType
X = mybir.AxisListType.X

B, L, E = 64, 64, 256
NB = 8
NP = NB // 2
GROUPS = B // NB
TOK = NB * L
KT = E // 128
KVH, GQ, HD1 = 8, 4, 8
HD2, KEYS = 16, 2 * L
HPT = 128 // HD2
HID = 4 * E
HS = 8
NMIX, DM, DD = 5, 32, 64
LP = L + 1
SOFT = 6
MASKED = -1.0e30


def _vector_rows():
    rows, at = {}, 0
    for name, n in (("bn", 1), ("bm", 1), ("bl", 1), ("bo", 1), ("bq", GQ), ("bk", 1), ("bv", 1),
                    ("gamma", 2), ("beta", 2), ("q_b", 2), ("k_b", 2), ("v_b", 2), ("post", 2), ("b1", HID // 128),
                    ("ln1_w", 2), ("ln1_b", 2), ("ln2_w", 2), ("ln2_b", 2), ("maa_x", 2), ("maa", 2 * NMIX),
                    ("decay", 2), ("u", 2), ("gn_w", 2), ("gn_b", 2), ("ffn_k", 2), ("ffn_r", 2)):
        rows[name] = (at, n)
        at += n
    return rows, at


def build(nc, a, out):
    with ExitStack() as ctx:
        def sb(name, shape, dt=F32):
            return ctx.enter_context(nc.sbuf_tensor(name, shape, dt))

        sems = {}

        def sig(name):
            if name not in sems:
                sems[name] = ctx.enter_context(nc.semaphore(name))
            return sems[name]

        banks = [ctx.enter_context(nc.psum_tensor(f"bank{i}", [128, 512], F32)) for i in range(8)]
        RINGS = {"score": [0, 1], "turn": [2, 3], "value": [4], "total": [5], "late": [6, 7]}
        turns, fills, place = {}, {}, {}

        def new_block():
            turns.clear()
            fills.clear()
            place.clear()

        def fill(pe, ring, tile):
            b = RINGS[ring][turns.get(ring, 0) % len(RINGS[ring])]
            turns[ring] = turns.get(ring, 0) + 1
            n = fills.get(b, 0)
            if n:
                pe.wait_ge(sig(f"bank{b}_free"), n)
            fills[b] = n + 1
            place[tile] = (b, n + 1)
            return banks[b], sig(f"bank{b}_full")

        def take(eng, tile):
            b, n = place[tile]
            eng.wait_ge(sig(f"bank{b}_full"), n)
            return banks[b], sig(f"bank{b}_free")

        def linker(eng, name):
            count = [0]

            def link(ins):
                count[0] += 1
                ins.then_inc(sig(name), 1)
                eng.wait_ge(sig(name), count[0])
            return link

        ident = sb("ident", [128, 128])
        block8 = sb("block8", [128, 16, 8])
        center8 = sb("center8", [128, 128])
        pick = sb("pick", [128, HS, 128])
        kvmask = sb("kvmask", [128, KVH])
        hmask = sb("hmask", [128, HPT])
        parity = sb("parity", [128, 2])
        half = sb("half", [128, 2, 8])
        ones2 = sb("ones2", [128, 32])
        ones32 = sb("ones32", [128, 32])
        eps5 = sb("eps5", [128, 1])
        eps6 = sb("eps6", [128, 1])
        ROWS, NROWS = _vector_rows()
        vec = sb("vec", [128, 128])

        def v(name, n=0):
            return vec[:, ROWS[name][0] + n:ROWS[name][0] + n + 1]

        conv = {w: sb(f"conv_{w}", [128, 128]) for w in ("Wn", "Wm", "Wl", "Wo")}
        wq1 = sb("wq1", [128, KT, GQ, 64])
        wk1 = sb("wk1", [128, KT, KVH * HD1])
        wv1 = sb("wv1", [128, KT, KVH * HD1])
        wo1 = sb("wo1", [128, GQ, E])
        wq2 = sb("wq2", [128, KT, E])
        wkv2 = sb("wkv2", [128, KT, 2 * E])
        wo2 = sb("wo2", [128, KT, 2, E])
        w1 = sb("w1", [128, KT, HID])
        w2 = sb("w2", [128, HID // 128, E])
        maa1 = sb("maa1", [128, KT, NMIX * DM])
        maa2 = sb("maa2", [128, NMIX, E])
        td1 = sb("td1", [128, KT, DD])
        td2 = sb("td2", [128, E])
        SQUARE = ("Wr", "Wk", "Wv", "Wg", "Wo", "Wfk", "Wfr", "Wfv")
        wt = {w: sb(f"t_{w}", [128, KT, E]) for w in SQUARE}
        row1 = sb("row1", [128, E])
        row2 = sb("row2", [128, E])
        row_b2 = sb("row_b2", [128, E])
        row_gamma = sb("row_gamma", [128, E])

        x0 = sb("x0", [128, NP, E])
        c0 = sb("c0", [128, NP, E])
        mask1 = sb("mask1", [128, NP, L])
        mask2 = sb("mask2", [128, NB, KEYS])
        s0 = sb("s0", [128, KT, NB, HS])
        hT = sb("hT", [128, KT, NB, 2, L])
        stats = sb("stats", [128, 2 * NP, 6])
        mv = sb("mv", [128, 2 * NP, 2])
        rstd = sb("rstd", [128, 2 * NP])
        xA = sb("xA", [128, NP, E])
        xh, xr = c0, x0

        early = sb("early", [128, 11264])
        soft_ring = sb("soft_ring", [128, SOFT, 512])
        qring = sb("qring", [128, 2, HPT, L])
        seg_max = sb("seg_max", [128, SOFT, 8])
        vbd = sb("vbd", [128, NB, 4, 32])
        den0 = sb("den0", [128, 2 * NP, 2])
        rden0 = sb("rden0", [128, 2 * NP, 2])
        nmax0 = sb("nmax0", [128, 2 * NP, 2])
        late = sb("late", [128, 10856])
        x3 = sb("x3", [128, NP, E])
        edge = sb("edge", [128, 2, KT, NB])
        stats3 = sb("stats3", [128, NP, 6])
        mv3 = sb("mv3", [128, NP, 2])
        rstd3 = sb("rstd3", [128, NP])

        def lhsT_cols(ap):
            n = 1
            for size in ap.shape[1:]:
                n *= size
            return n

        def cut(t, at, *shape):
            n = 1
            for size in shape:
                n *= size
            flat = t[:, at:at + n]
            if len(shape) == 1:
                return flat
            names = "abcde"[:len(shape)]
            return flat.rearrange(f"p ({' '.join(names)}) -> p {' '.join(names)}",
                                  **{k: size for k, size in zip(names, shape)})

        vrows = early[:, 4096:4224]
        soft = soft_ring[:, :, :]
        bq_rows = vec[:, ROWS["bq"][0]:ROWS["bq"][0] + GQ]
        ch = cut(early, 0, NP, E)
        mn = cut(early, 1024, NP, E)
        mlT = cut(early, 2048, NP, 2, 128)
        mo = cut(early, 3072, NP, E)
        mmb = cut(early, 4096, NP, 2, E)
        xh0 = cut(early, 6144, NP, E)
        pT0 = cut(early, 6144, 2, 2, 2, 2, 128)
        pT1 = cut(early, 0, 2, 4, 2, GQ, L)
        pT2 = cut(early, 0, 4, KT, 512)
        attended = cut(early, 6144, 2, 4, 2 * L)
        over = cut(early, 7168, 2, 512)
        kT1 = cut(early, 0, NP, L)
        kbd = cut(early, 4096, NP, KVH, L)
        x1T = cut(early, 8192, 2, KT, 2, 2, L)
        qz = cut(early, 9216, NP, GQ, 2, L)
        k2T = cut(early, 4096, KT, NB, KEYS)
        q2T = cut(early, 8192, KT, NB, L)
        v2 = cut(early, 9216, NB, E)
        gT = cut(early, 0, HID // 128, TOK)
        xnT = cut(early, 8192, 2, KT, TOK // 2)
        PT = NB * LP
        kP = cut(late, 0, KT, NB, LP)
        vP = cut(late, 1040, KT, NB, LP)
        wP = cut(late, 2080, KT, NB, LP)
        rT = cut(late, 3120, KT, TOK)
        gg = cut(late, 4144, KT, TOK)
        xh3 = cut(late, 3120, NP, E)
        xaP = cut(late, 5168, KT, NB, LP)
        sx = cut(late, 6208, KT, TOK)
        xm = cut(late, 7232, 2, KT, TOK)
        xf = cut(late, 9280, 2, TOK)
        vj = cut(late, 5168, 3, PT)
        aj = cut(late, 6728, 2, PT)
        sj = cut(late, 7768, 2, PT)
        rs = cut(late, 8808, 2, 512)
        ruk = cut(late, 9832, KT, TOK)
        sq = cut(late, 6192, KT, TOK)
        rgn = cut(late, 7216, KT, TOK)
        ogT = cut(late, 8240, KT, TOK)
        x4 = cut(late, 3120, NP, E)
        xh4 = cut(late, 4144, NP, E)
        xcP = cut(late, 0, KT, NB, LP)
        sx2 = cut(late, 1040, KT, TOK)
        xk2 = cut(late, 5168, KT, TOK)
        xr2 = cut(late, 6192, KT, TOK)
        kkT = cut(late, 7216, KT, TOK)
        thn = cut(late, 9264, NP, E)

        def nat(name):
            return a[name].rearrange("b c t -> (b c) t").rearrange("(n p q) t -> n q p t", p=NP, q=128)
        x_in, c_in = nat("x"), nat("ctx_2048")
        out_v = out.rearrange("b c t -> (b c) t").rearrange("(n p q) t -> n q p t", p=NP, q=128)
        mask1_in = a["mask_Bx1xSxS2_ff0"].rearrange("b o l s -> (b o l) s").rearrange(
            "(n p q) s -> n q p s", p=NP, q=128)
        mask2_in = a["mask_BxS2_ik0"].rearrange("(n b) s -> n b s", b=NB)
        s0_in = a["ctx_2048"].rearrange("b c t -> b (c t)")[:, 2 * E:2 * E + HS * E].rearrange(
            "(n b) (k p j) -> n k p b j", b=NB, k=KT, j=HS)

        new_block()
        with nc.Block() as block:
            @block.gpsimd
            def _(pool):
                link = linker(pool, "pool_step")
                link(nc.gpsimd.memset(vrows, 0.0))
                for w in conv.values():
                    nc.gpsimd.memset(w[:, :], 0.0)
                for t in (wo1, maa2, td2, vbd, pick):
                    nc.gpsimd.memset(t[:, :] if len(t.shape) == 2 else t[tuple([slice(None)] * len(t.shape))], 0.0)
                nc.gpsimd.memset(eps5[:, :], 1e-5)
                nc.gpsimd.memset(eps6[:, :], 1e-6)
                nc.gpsimd.memset(ones32[:, :], 1.0)
                nc.gpsimd.memset(ones2[:, :], 1.0)
                link(nc.gpsimd.memset(mask2[:, :, :], 0.0))
                pool.sem_inc(sig("zeroed"), 1)

                def band(t, shape, step, width):
                    pattern = [[-step, shape[0]]] + ([[0, shape[1]]] if len(shape) > 1 else [])
                    up = [[step, shape[0]]] + ([[0, shape[1]]] if len(shape) > 1 else [])
                    link(nc.gpsimd.memset(t, 1.0))
                    link(nc.gpsimd.affine_select(out=t, in_=t, compare_op=ALU.is_ge, fill=0.0, base=0,
                                                 pattern=pattern, channel_multiplier=1))
                    link(nc.gpsimd.affine_select(out=t, in_=t, compare_op=ALU.is_ge, fill=0.0, base=width - 1,
                                                 pattern=up, channel_multiplier=-1))
                band(block8[:, :, :], (16, 8), 8, 8)
                band(hmask[:, :], (HPT,), HD2, HD2)
                band(half[:, :, :], (2, 8), 64, 64)
                band(ident[:, :], (128,), 1, 1)
                pool.sem_inc(sig("bands"), 1)

            @block.sync
            def _(sp):
                sp.wait_ge(sig("zeroed"), 1)
                for w in conv:
                    for h in range(2):
                        sp.dma_start(conv[w][64 * h:64 * h + 64, 64 * h:64 * h + 64], a[f"L0_xattn_{w}"]).then_inc(sig("conv_in"), 16)
                L3 = "L3_xattn_"
                srcs = [("gamma", "L1_xattn_gamma"), ("beta", "L1_xattn_beta"), ("q_b", "L2_xattn_q_b"),
                        ("post", "L2_xattn_postnorm_w"), ("b1", "L2_xattn_mlp_b1"), ("ln1_w", L3 + "ln1_w"),
                        ("ln1_b", L3 + "ln1_b"), ("ln2_w", L3 + "ln2_w"), ("ln2_b", L3 + "ln2_b"),
                        ("maa_x", L3 + "maa_x"), ("decay", L3 + "time_decay"), ("gn_w", L3 + "gn_w"),
                        ("gn_b", L3 + "gn_b"), ("ffn_k", L3 + "ffn_maa_k"), ("ffn_r", L3 + "ffn_maa_r")]
                for row, name in srcs:
                    r, n = ROWS[row]
                    sp.dma_start(vrows[r:r + n, :], a[name].rearrange("(n p) -> n p", p=128)).then_inc(sig("rows_in"), 16)
                r, n = ROWS["maa"]
                sp.dma_start(vrows[r:r + n, :], a[L3 + "maa_stack"].rearrange("o f (n p) -> (o f n) p", p=128)).then_inc(sig("rows_in"), 16)
                r, n = ROWS["u"]
                sp.dma_start(vrows[r:r + n, :], a[L3 + "u"].rearrange("h s o -> (h s o)").rearrange("(n p) -> n p", p=128)).then_inc(sig("rows_in"), 16)
                for h in range(2):
                    for row, name in (("bn", "L0_xattn_bn"), ("bm", "L0_xattn_bm"), ("bl", "L0_xattn_bl"),
                                      ("bo", "L0_xattn_bo"), ("bk", "L1_xattn_bk")):
                        r = ROWS[row][0]
                        sp.dma_start(vrows[r:r + 1, 64 * h:64 * h + 64], a[name].rearrange("(o c) -> o c", o=1)).then_inc(sig("rows_in"), 16)
                    r = ROWS["bq"][0]
                    for g in range(GQ):
                        sp.dma_start(vrows[r + g:r + g + 1, 64 * h:64 * h + 64].rearrange("o (k d) -> o k d", d=HD1),
                                     a["L1_xattn_bq"].rearrange("(o k g d) -> g o k d", o=1, g=GQ, d=HD1)[g]).then_inc(sig("rows_in"), 16)
                r = ROWS["bv"][0]
                sp.dma_start(vrows[r:r + 1, :].rearrange("o (j e) -> o j e", e=32)[:, :, 0:16],
                             a["L1_xattn_bv"].rearrange("(o j e) -> o j e", o=1, e=16)).then_inc(sig("rows_in"), 16)
                with nc.allow_non_contiguous_dma(reason="interleaved biases"):
                    for row, s in (("k_b", 0), ("v_b", 1)):
                        r, n = ROWS[row]
                        sp.dma_start(vrows[r:r + n, :].unsqueeze(2),
                                     a["L2_xattn_kv_b"].rearrange("(n p s) -> s n p", p=128, s=2)[s].unsqueeze(2)).then_inc(sig("rows_in"), 16)
                sp.wait_ge(sig("rows_in"), 16 * (len(srcs) + 2 + 10 + 2 * GQ + 1 + 2))
                sp.sem_inc(sig("rows_all"), 1)
                for t, name in ((row1, "L1_xattn_bo"), (row2, "L2_xattn_out_b"), (row_b2, "L2_xattn_mlp_b2"),
                                (row_gamma, "L1_xattn_gamma"), (cut(late, 1536, E), "L1_xattn_beta")):
                    sp.dma_start(t[:, :], a[name].rearrange("(o n) -> o n", o=1).broadcast_to([128, E])).then_inc(sig("spread_in"), 16)
                sp.wait_ge(sig("spread_in"), 80)
                sp.sem_inc(sig("spread_all"), 1)

            @block.scalar
            def _(act):
                act.wait_ge(sig("zeroed"), 1)
                for n, w in enumerate(SQUARE):
                    act.dma_start(cut(early, 512 * n, KT, E), a[f"L3_xattn_{w}"].rearrange("(k p) n -> p k n", p=128)).then_inc(sig("square_in"), 16)
                act.dma_start(cut(late, 0, KT, E), a["L2_xattn_out_w"].rearrange("(k p) n -> p k n", p=128)).then_inc(sig("plain_in"), 16)
                for t, name in ((cut(late, 512, KT, E), "L1_xattn_Wq"), (wk1, "L1_xattn_Wk"), (wv1, "L1_xattn_Wv"), (wq2, "L2_xattn_q_w"),
                                (wkv2, "L2_xattn_kv_w"), (w1, "L2_xattn_mlp_w1"), (w2, "L2_xattn_mlp_w2"),
                                (maa1, "L3_xattn_maa_w1"), (td1, "L3_xattn_td_w1")):
                    act.dma_start(t[:, :, :], a[name].rearrange("(k p) n -> p k n", p=128)).then_inc(sig("plain_in"), 16)
                for j in range(4):
                    for k in range(2):
                        act.dma_start(wo1[32 * j + 8 * k:32 * j + 8 * k + 8, :, :],
                                      a["L1_xattn_Wo"].rearrange("(k g d) n -> k d g n", g=GQ, d=HD1)[2 * j + k]).then_inc(sig("plain_in"), 16)
                act.dma_start(maa2[:, 0, :][0:32], a["L3_xattn_maa_w2"][0]).then_inc(sig("plain_in"), 16)
                for f in range(1, NMIX):
                    r = 32 * (f % 4)
                    act.dma_start(maa2[r:r + 32, f, :], a["L3_xattn_maa_w2"][f]).then_inc(sig("plain_in"), 16)
                act.dma_start(td2[64:64 + DD, :], a["L3_xattn_td_w2"]).then_inc(sig("plain_in"), 16)
                act.wait_ge(sig("plain_in"), 16 * (1 + 9 + 8 + 5 + 1))
                act.sem_inc(sig("plain_all"), 1)

            @block.tensor
            def _(pe):
                pe.wait_ge(sig("bands"), 1)
                pe.wait_ge(sig("rows_all"), 1)
                t, full = fill(pe, "turn", "vec")
                nc.tensor.transpose(t[:, 0:128], vrows, ident[:, :]).then_inc(full, 1)
                pe.wait_ge(sig("conv_in"), 128)
                t, full = fill(pe, "turn", "conv")
                for n, w in enumerate(conv):
                    ins = nc.tensor.transpose(t[:, 128 * n:128 * n + 128], conv[w][:, :], ident[:, :])
                ins.then_inc(full, 1)
                pe.wait_ge(sig("square_in"), 16 * len(SQUARE))
                for n, w in enumerate(SQUARE):
                    t, full = fill(pe, "turn", w)
                    src = cut(early, 512 * n, KT, E)
                    for i in range(KT):
                        for o in range(KT):
                            ins = nc.tensor.transpose(t[:, 256 * i + 128 * o:256 * i + 128 * o + 128],
                                                      src[:, o, 128 * i:128 * i + 128], ident[:, :])
                    ins.then_inc(full, 1)
                pe.wait_ge(sig("plain_all"), 1)
                pe.wait_ge(sig("bias_spread"), 1)
                t, full = fill(pe, "turn", "row1")
                for g in range(GQ):
                    ins = nc.tensor.matmul(t[:, 0:E], cut(late, 1024, 3, 128)[:, 0, :], wo1[:, g, :], start=g == 0, stop=g == GQ - 1)
                ins.then_inc(full, 1)
                t, full = fill(pe, "turn", "row2")
                for k in range(KT):
                    ins = nc.tensor.matmul(t[:, 0:E], cut(late, 1024, 3, 128)[:, 1 + k, :], cut(late, 0, KT, E)[:, k, :], start=k == 0, stop=k == KT - 1)
                ins.then_inc(full, 1)

            @block.vector
            def _(dve):
                link = linker(dve, "dve_step")
                dve.wait_ge(sig("bands"), 1)
                flat8 = block8[:, :, :].rearrange("p a b -> p (a b)")
                nc.vector.tensor_tensor(kvmask[:, :], block8[:, 0:8, 0], block8[:, 8:16, 0], ALU.add)
                nc.vector.tensor_reduce(parity[:, :], hmask[:, :].rearrange("p (j h) -> p h j", h=2), X, ALU.add)
                nc.vector.tensor_copy(ones2[:, 0:16], half[:, :, :].rearrange("p a b -> p (a b)"))
                link(nc.vector.scalar_tensor_tensor(out=center8[:, :], in0=flat8, scalar=-1.0 / HS, in1=ident[:, :], op0=ALU.mult, op1=ALU.add))
                for j in range(HS):
                    nc.vector.tensor_copy(pick[:, j, :].rearrange("p (h j) -> p h j", j=HS)[:, :, j], block8[:, :, j])
                t, free = take(dve, "vec")
                link(nc.vector.tensor_copy(vec[:, :], t[:, 0:128]))
                dve.sem_inc(free, 1)
                for w in ("gn_w", "gn_b"):
                    r = ROWS[w][0]
                    nc.vector.tensor_scalar(vec[:, r:r + 2], vec[:, r:r + 2], 0.5, None, ALU.mult)
                bias = cut(late, 1024, 3, 128)
                for n, col in enumerate((v("bv"), v("v_b", 0), v("v_b", 1))):
                    ins = nc.vector.tensor_copy(bias[:, n, :], col.broadcast_to([128, 128]))
                ins.then_inc(sig("bias_spread"), 1)
                t, free = take(dve, "conv")
                for n, w in enumerate(conv):
                    ins = nc.vector.tensor_copy(conv[w][:, :], t[:, 128 * n:128 * n + 128])
                ins.then_inc(free, 1)
                for w in SQUARE:
                    t, free = take(dve, w)
                    nc.vector.tensor_copy(wt[w][:, :, :].rearrange("p k n -> p (k n)"), t[:, :]).then_inc(free, 1)
                dve.wait_ge(sig("plain_all"), 1)
                for k in range(KT):
                    nc.vector.tensor_copy(wq1[:, k, :, :].rearrange("p g (h d) -> p h g d", d=HD1),
                                          cut(late, 512, KT, KVH, GQ, HD1)[:, k])
                    for h in range(2):
                        nc.vector.tensor_scalar(wo2[:, k, h, :], cut(late, 0, KT, E)[:, k, :], parity[:, h:h + 1], None, ALU.mult)
                dve.wait_ge(sig("spread_all"), 1)
                t, free = take(dve, "row1")
                nc.vector.tensor_tensor(row1[:, :], t[:, 0:E], row1[:, :], ALU.add).then_inc(free, 1)
                t, free = take(dve, "row2")
                link(nc.vector.tensor_tensor(row2[:, :], t[:, 0:E], row2[:, :], ALU.add))
                dve.sem_inc(free, 1)
                for t in (row2, row_b2):
                    nc.vector.tensor_tensor(t[:, :], t[:, :], cut(late, 1536, E), ALU.add)

        def clear_all():
            nums = sorted(s.num for s in sems.values())
            with nc.Block() as between:
                @between.gpsimd
                def _(pool):
                    lo = nums[0]
                    for n, m in zip(nums, nums[1:] + [None]):
                        if m != n + 1:
                            pool.sem_clear(range(lo, n + 1))
                            lo = m
        LOG_EXP, TANH, GELU = "natural_log_exp_and_others", "exp_and_others", "gelu_apprx_tanh_and_others"

        SCANS = KT * HS + 3
        STAGES = (["moments", "normalize", "turn", "shift", "maa", "mix 0", "mix 1", "td", "k", "mix 2", "decay", "v",
                   "mix 3", "mix 4", "r", "g", "r u k", "bonus"] + [("scan", n) for n in range(SCANS)] +
                  ["center", "variance", "gate", "project", "moments 2", "normalize 2", "turn 2", "shift 2", "ffn k", "ffn r", "ffn v"])
        MIXES = (1, 0, 2, 3, 4)
        due, at = {}, 0.0
        for stage in STAGES:
            due.setdefault(int(at), []).append(stage)
            at += 1.0 if stage[0] == "scan" else 1.6

        U0 = 2 * NP
        UNITS = 4 * NP
        A1 = U0 + 5
        A2 = A1 + UNITS + 5
        END = A2 + UNITS + 10

        def unit(i):
            if A1 <= i < A1 + UNITS:
                return i - A1
            return i - A2 + UNITS if A2 <= i < A2 + UNITS else -1

        def pair_of(i):
            return unit(i) // 4 if unit(i) >= 0 and unit(i) % 4 == 0 else -1

        def half_of(i):
            return i // 8 if i in (0, 8) else -1

        def group_block(now, before):
            new_block()

            def beside(layer3):
                count = [0]

                def step():
                    for stage in due.get(count[0], []) if before is not None else []:
                        layer3(stage)
                    count[0] += 1

                def rest():
                    while count[0] <= max(due):
                        step()
                return step, rest

            with nc.Block() as block:
                @block.sync
                def _(sp):
                    if now is not None:
                        sp.dma_start(c0[:, :, :], c_in[now]).then_inc(sig("c0_in"), 16)
                        sp.dma_start(x0[:, :, :], x_in[now]).then_inc(sig("x0_in"), 16)
                        sp.dma_start(mask1[:, :, :], mask1_in[now]).then_inc(sig("mask1_in"), 16)
                        sp.dma_start(mask2[:, :, 0:L].bitcast(I32), mask2_in[now].unsqueeze(0).broadcast_to([128, NB, L])).then_inc(sig("mask2_in"), 16)
                    if before is not None:
                        for k in range(KT):
                            sp.dma_start(s0[:, k, :, :], s0_in[before][k]).then_inc(sig("s0_in"), 16)
                        for n in range(KT * HS):
                            k, j = n // HS, n % HS
                            sp.wait_ge(sig("vP_ready"), k + 1)
                            if n < 3:
                                sp.wait_ge(sig("tanh_g"), KT)
                            else:
                                sp.wait_ge(sig("kv_done"), n - 2)
                            sp.dma_start(vj[:, n % 3, :], vP[j::HS, k, :, :].rearrange("h b t -> h (b t)").unsqueeze(1).broadcast_to(
                                [16, HS, PT])).then_inc(sig(f"vj{n % 3}_in"), 16)
                        sp.wait_ge(sig("out_ready"), NP)
                        sp.dma_start(out_v[before], thn[:, :, :]).then_inc(sig("stored"), 16)
                        sp.wait_ge(sig("stored"), 16)

                @block.tensor
                def _(pe):
                    mm, tr = nc.tensor.matmul, nc.tensor.transpose

                    def product(tile, cols, terms, ring="turn"):
                        t, full = fill(pe, ring, tile)
                        for n, (lhsT, rhs) in enumerate(terms):
                            ins = mm(t[0:lhsT_cols(lhsT), 0:cols], lhsT, rhs, start=n == 0, stop=n == len(terms) - 1)
                        ins.then_inc(full, 1)

                    def flip(tile, src, ring="turn"):
                        for k in range(KT):
                            t, full = fill(pe, ring, (tile, k))
                            for p in range(NP):
                                ins = tr(t[:, 128 * p:128 * p + 128], src[:, p, 128 * k:128 * k + 128], ident[:, :])
                            ins.then_inc(full, 1)

                    def natural(tile, q, lhsT, rhs, ring="turn"):
                        t, full = fill(pe, ring, (tile, q))
                        for p in range(2):
                            for k, r in enumerate(rhs):
                                ins = mm(t[:, E * p:E * p + E], lhsT(2 * q + p, k), r, start=k == 0, stop=k == len(rhs) - 1)
                        ins.then_inc(full, 1)

                    def layer3(stage):
                        def mix(f):
                            for m in range(KT):
                                product((stage, m), 512, [(maa2[:, f, 128 * m:128 * m + 128], xf[:, f // 4, :])], "late")

                        def square(w, moving):
                            for m in range(KT):
                                product((stage, m), 512, [(wt[w][:, k, 128 * m:128 * m + 128], moving(k)) for k in range(KT)], "late")

                        def mixed(n, w):
                            pe.wait_ge(sig("xm_ready"), KT * (n + 1))
                            square(w, lambda k: xm[:, (n + 1) % 2, k, :])

                        def project(w, moving):
                            for q in range(2):
                                natural(stage, q, lambda p, k: moving[:, k, 128 * p:128 * p + 128], [wt[w][:, k, :] for k in range(KT)], "late")

                        if stage == "turn":
                            pe.wait_ge(sig("xh3_ready"), NP)
                            flip(stage, xh3, "late")
                        elif stage == "maa":
                            pe.wait_ge(sig("x1m_ready"), KT)
                            product("maaA", 512, [(maa1[:, k, 0:128], xm[:, 0, k, :]) for k in range(KT)], "late")
                            product("maaB", 512, [(maa1[:, k, 128:160], xm[:, 0, k, :]) for k in range(KT)], "late")
                        elif stage[0:3] == "mix":
                            pe.wait_ge(sig("xf_ready"), 2)
                            pe.wait_ge(sig("xf_zero"), 1)
                            mix(MIXES[int(stage[4])])
                        elif stage == "td":
                            pe.wait_ge(sig("xm_ready"), KT)
                            product("td", 512, [(td1[:, k, :], xm[:, 1, k, :]) for k in range(KT)], "late")
                        elif stage == "decay":
                            pe.wait_ge(sig("td_ready"), 1)
                            for m in range(KT):
                                product((stage, m), 512, [(td2[:, 128 * m:128 * m + 128], xf[:, 1, :])], "late")
                        elif stage == "k":
                            mixed(1, "Wk")
                        elif stage == "v":
                            mixed(2, "Wv")
                        elif stage == "r":
                            mixed(3, "Wr")
                        elif stage == "g":
                            mixed(4, "Wg")
                        elif stage == "bonus":
                            for k in range(KT):
                                pe.wait_ge(sig("ruk_ready"), k + 1)
                                product((stage, k), 512, [(block8[:, :, :], ruk[:, k, :])], "late")
                        elif stage[0] == "scan":
                            n = stage[1] - 2
                            if 0 <= n < KT * HS:
                                k, j = n // HS, n % HS
                                if j == 0:
                                    t, full = fill(pe, "late", ("o3", k))
                                else:
                                    b, c = place["o3", k]
                                    t, full = banks[b], sig(f"bank{b}_full")
                                pe.wait_ge(sig("rs_ready"), n + 1)
                                mm(t[:, :], pick[:, j, :], rs[:, j % 2, :], start=j == 0, stop=j == HS - 1).then_inc(
                                    full if j == HS - 1 else sig("rs_used"), 1)
                        elif stage == "center":
                            for k in range(KT):
                                pe.wait_ge(sig("o3_ready"), k + 1)
                                product((stage, k), 512, [(center8[:, :], ruk[:, k, :])], "late")
                        elif stage == "variance":
                            for k in range(KT):
                                pe.wait_ge(sig("sq_ready"), k + 1)
                                product((stage, k), 512, [(block8[:, :, :], sq[:, k, :])], "late")
                        elif stage == "project":
                            pe.wait_ge(sig("ogT_ready"), KT)
                            project("Wo", ogT)
                        elif stage == "turn 2":
                            pe.wait_ge(sig("xh4_ready"), NP)
                            flip(stage, xh4, "late")
                        elif stage == "ffn k":
                            pe.wait_ge(sig("xk2_ready"), KT)
                            square("Wfk", lambda k: xk2[:, k, :])
                        elif stage == "ffn r":
                            pe.wait_ge(sig("xr2_ready"), KT)
                            project("Wfr", xr2)
                        elif stage == "ffn v":
                            pe.wait_ge(sig("kk_ready"), KT)
                            project("Wfv", kkT)

                    step, rest = beside(layer3)
                    if now is None:
                        rest()
                        return

                    step()
                    step()
                    pe.wait_ge(sig("c0_in"), 16)
                    flip("cT", c0)
                    step()
                    for q in range(2):
                        t, full = fill(pe, "turn", ("ml", q))
                        for p in range(2):
                            for s in range(2):
                                ins = mm(t[:, 256 * p + 128 * s:256 * p + 128 * s + 128], c0[:, 2 * q + p, 128 * s:128 * s + 128],
                                         conv["Wl"][:, :], start=True, stop=True)
                        ins.then_inc(full, 1)
                    step()
                    pe.wait_ge(sig("ch_ready"), NP)
                    for q in range(2):
                        product(("mm", q), 512, [(conv["Wm"][:, :], ch[:, 2 * q:2 * q + 2, :])])
                    pe.wait_ge(sig("xh_ready"), NP)
                    for q in range(2):
                        product(("mn", q), 512, [(conv["Wn"][:, :], xh0[:, 2 * q:2 * q + 2, :])])

                    def scores0(u):
                        pe.wait_ge(sig("mn_ready"), u // 4 + 1)
                        pe.wait_ge(sig("mmb_ready"), u // 4 + 1)
                        product(("s0", u), 512, [(mn[:, u // 2, 128 * (u % 2):128 * (u % 2) + 128], mmb[:, u // 2, :, :])], "score")

                    def turn0(u):
                        pe.wait_ge(sig("p0_ready"), u + 1)
                        t, full = fill(pe, "turn", ("t0", u))
                        for n in range(4):
                            ins = tr(t[:, 128 * n:128 * n + 128], soft[:, u % SOFT, 128 * n:128 * n + 128], ident[:, :])
                        ins.then_inc(full, 1)

                    def value0(p):
                        pe.wait_ge(sig("pT0_ready"), 2 * p + 2)
                        pe.wait_ge(sig("ml_ready"), p // 2 + 1)
                        t, full = fill(pe, "value", ("o0", p))
                        for b in range(2):
                            for s in range(2):
                                ins = mm(t[64 * b:64 * b + 64, 0:E], mlT[:, p, s, 64 * b:64 * b + 64], pT0[:, p % 2, :, b, s, :],
                                         start=s == 0, stop=s == 1)
                        ins.then_inc(full, 1)

                    def layer0(i):
                        if i < U0:
                            scores0(i)
                        if 2 <= i < U0 + 2:
                            turn0(i - 2)
                        if i >= 5 and (i - 5) % 2 == 0 and (i - 5) // 2 < NP:
                            value0((i - 5) // 2)
                        if i >= 7 and (i - 7) % 2 == 0 and (i - 7) // 2 < NP:
                            p = (i - 7) // 2
                            pe.wait_ge(sig("mo_ready"), p + 1)
                            product(("x1", p), E, [(conv["Wo"][:, :], mo[:, p, :])])

                    def turn_half(tile, src, h):
                        t, full = fill(pe, "turn", (tile, h))
                        for k in range(KT):
                            for p in range(2):
                                ins = tr(t[:, 256 * k + 128 * p:256 * k + 128 * p + 128], src[:, 2 * h + p, 128 * k:128 * k + 128], ident[:, :])
                        ins.then_inc(full, 1)

                    def keys1():
                        pe.wait_ge(sig("cT_ready"), KT)
                        t, full = fill(pe, "turn", "k1")
                        for b in range(2):
                            for k in range(KT):
                                ins = mm(t[64 * b:64 * b + 64, 0:256], wk1[:, k, :], hT[:, k, b::2, 0, :], start=k == 0, stop=k == KT - 1)
                        ins.then_inc(full, 1)

                    def values1():
                        t, full = fill(pe, "turn", "v1")
                        for b in range(NB):
                            r = 64 * (b % 2)
                            for k in range(KT):
                                ins = mm(t[r:r + 64, 64 * (b // 2):64 * (b // 2) + 64], hT[:, k, b, 0, :], wv1[:, k, :], start=k == 0, stop=k == KT - 1)
                        ins.then_inc(full, 1)

                    def queries1(h):
                        pe.wait_ge(sig("x1T_ready"), h + 1)
                        t, full = fill(pe, "turn", ("q1", h))
                        for g in range(GQ):
                            for b in range(2):
                                for k in range(KT):
                                    ins = mm(t[64 * b:64 * b + 64, 128 * g:128 * g + 128], wq1[:, k, g, :], x1T[:, h, k, :, b, :],
                                             start=k == 0, stop=k == KT - 1)
                        ins.then_inc(full, 1)

                    kv = wkv2[:, :, :].rearrange("p k (n s) -> p s k n", s=2)

                    def queries2(q):
                        pe.wait_ge(sig("lT_ready"), KT * (q + 1))
                        t, full = fill(pe, "turn", ("q2", q))
                        for h in range(KT):
                            for k in range(KT):
                                ins = mm(t[:, 256 * h:256 * h + 256], wq2[:, k, 128 * h:128 * h + 128], hT[:, k, 4 * q:4 * q + 4, 1, :],
                                         start=k == 0, stop=k == KT - 1)
                        ins.then_inc(full, 1)

                    def keys2(q):
                        for h in range(KT):
                            product(("k2", h, q), 512, [(kv[:, 0, k, 128 * h:128 * h + 128], hT[:, k, 4 * q:4 * q + 4, :, :]) for k in range(KT)])

                    def values2(q):
                        for p in (2 * q, 2 * q + 1):
                            t, full = fill(pe, "turn", ("v2", p))
                            for b in range(2):
                                for k in range(KT):
                                    ins = mm(t[:, 256 * b:256 * b + 256], hT[:, k, 2 * p + b, :, :], kv[:, 1, k, :], start=k == 0, stop=k == KT - 1)
                            ins.then_inc(full, 1)

                    def between(i):
                        if i == U0 + 2:
                            keys1()
                        if i == U0 + 6:
                            values1()
                        for h in range(2):
                            if i == 4 * h + 11:
                                pe.wait_ge(sig("x1_ready"), 2 * h + 2)
                                turn_half("x1T", xA, h)
                            if i == 4 * h + 12:
                                queries1(h)
                            if i == A1 + 8 * h + 17:
                                pe.wait_ge(sig("xh1_ready"), 2 * h + 2)
                                turn_half("lT", xh, h)
                            if i == A1 + 8 * h + 18:
                                queries2(h)
                            if i == A1 + 8 * h + 19:
                                keys2(h)
                            if i == A1 + 8 * h + 20:
                                values2(h)
                            if i == A2 + 8 * h + 17:
                                pe.wait_ge(sig("xh2_ready"), 2 * h + 2)
                                turn_half("xnT", xh, h)

                    def scores(u):
                        if u < UNITS:
                            p, g = u // 4, u % 4
                            pe.wait_ge(sig("kbd_ready"), p + 1)
                            pe.wait_ge(sig("qz_ready"), p // 2 + 1)
                            product(("s", u), 512, [(qz[:, p, g, :, :], kbd[:, p, :, :])], "score")
                            return
                        b, h = (u - UNITS) // 2, u % 2
                        pe.wait_ge(sig("k2_ready"), 2 * (b // 4) + 2)
                        pe.wait_ge(sig("qring_ready"), u - UNITS + 1)
                        t, full = fill(pe, "score", ("s", u))
                        for j in range(4):
                            ins = mm(t[:, 128 * j:128 * j + 128], qring[:, u % 2, 2 * j:2 * j + 2, :], k2T[:, h, b, :], start=True, stop=True)
                        ins.then_inc(full, 1)

                    def turned(u):
                        pe.wait_ge(sig("exp"), u + 1)
                        t, full = fill(pe, "turn", ("t", u))
                        for n in range(4):
                            ins = tr(t[:, 128 * n:128 * n + 128], soft[:, u % SOFT, 128 * n:128 * n + 128], ident[:, :])
                        ins.then_inc(full, 1)

                    def pair(c):
                        p = c % NP
                        pe.wait_ge(sig("pT_ready"), 4 * c + 4)
                        if c >= NP:
                            pe.wait_ge(sig("v2_ready"), p + 1)
                        for ring, ones in (("value", None), ("total", ones2 if c < NP else ones32)):
                            t, full = fill(pe, ring, (ring, c))
                            for b in range(2):
                                for j in range(4):
                                    if c < NP:
                                        ins = mm(t[32 * j:32 * j + 32, 256 * b:256 * b + 256], vbd[:, 2 * p + b, j, :] if ones is None else ones[:, :],
                                                 pT1[:, p % 2, j, b, :, :], start=True, stop=True)
                                        continue
                                    for h in range(2):
                                        at = 256 * b + 128 * h
                                        ins = mm(t[32 * j:32 * j + 32, at:at + 128],
                                                 v2[:, 2 * p + b, 128 * h + 32 * j:128 * h + 32 * j + 32] if ones is None else ones[:, :],
                                                 pT2[:, (2 * p + b) % 4, h, 128 * j:128 * j + 128], start=True, stop=True)
                            ins.then_inc(full, 1)

                    def project(c):
                        pe.wait_ge(sig("at_ready"), c + 1)
                        product(("out", c), E, [(attended[:, c % 2, n, :], wo1[:, n, :] if c < NP else wo2[:, n // 2, n % 2, :]) for n in range(4)])

                    for i in range(END):
                        step()
                        layer0(i)
                        if unit(i) >= 0:
                            scores(unit(i))
                        if unit(i - 3) >= 0:
                            turned(unit(i - 3))
                        if pair_of(i - 8) >= 0:
                            pair(pair_of(i - 8))
                        if pair_of(i - 10) >= 0:
                            project(pair_of(i - 10))
                        between(i)
                    pe.wait_ge(sig("xnT_ready"), 2 * KT)
                    for n in range(HID // 128):
                        product(("u", n), 512, [(w1[:, k, 128 * n:128 * n + 128], xnT[:, :, k, :]) for k in range(KT)])
                        step()
                    pe.wait_ge(sig("gT_ready"), HID // 128)
                    for q in range(2):
                        natural("y2", q, lambda p, k: gT[:, k, 128 * p:128 * p + 128], [w2[:, k, :] for k in range(HID // 128)])
                        step()
                    rest()

                @block.scalar
                def _(act):
                    link = linker(act, "act_step")
                    af = nc.scalar.activation
                    loaded = [None]

                    def tables(name):
                        if loaded[0] != name:
                            nc.scalar.preload_act_table_set(name)
                        loaded[0] = name

                    def rsqrt(dst, src, eps, scale, name):
                        link(af(dst, src, ACT.Ln, bias=eps[:, :], scale=scale))
                        af(dst, dst, ACT.Exp, scale=-0.5).then_inc(sig(name), 1)

                    def batches(ap):
                        return ap.rearrange("p (b l) -> p b l", l=L)

                    def drain(tile, dst, src, func, name, **kw):
                        t, free = take(act, tile)
                        link(af(dst, src(t), func, **kw))
                        act.sem_inc(free, 1)
                        act.sem_inc(sig(name), 1)

                    def layer3(stage):
                        def tanh(work):
                            back = loaded[0]
                            if back != GELU:
                                tables(TANH)
                            work()
                            tables(back)

                        def whole(t):
                            return t[:, :]

                        if stage == "moments":
                            act.wait_ge(sig("stats3_ready"), 1)
                            rsqrt(rstd3[:, :], mv3[:, :, 1], eps5, 1.0, "rstd3_ready")
                        elif stage == "turn":
                            for k in range(KT):
                                drain((stage, k), xaP[:, k, :, 1:LP], lambda t: batches(t[:, :]), ACT.Identity, "xaP_ready",
                                      bias=v("ln1_b", k), scale=v("ln1_w", k))
                        elif stage == "maa":
                            @tanh
                            def _():
                                drain("maaA", xf[:, 0, :], whole, ACT.Tanh, "xf_ready")
                                drain("maaB", xf[0:DM, 1, :], lambda t: t[0:DM, :], ACT.Tanh, "xf_ready")
                        elif stage == "k":
                            for k in range(KT):
                                drain((stage, k), kP[:, k, :, 1:LP], lambda t: batches(t[:, :]), ACT.Identity, "kP_ready")
                        elif stage == "td":
                            @tanh
                            def _():
                                drain("td", xf[64:64 + DD, 1, :], lambda t: t[0:DD, :], ACT.Tanh, "td_ready")
                        elif stage == "decay":
                            for k in range(KT):
                                drain((stage, k), wP[:, k, :, 1:LP], lambda t: batches(t[:, :]), ACT.Exp, "decay_read", bias=v("decay", k))
                            for k in range(KT):
                                af(wP[:, k, :, 1:LP], wP[:, k, :, 1:LP], ACT.Exp, scale=-1.0).then_inc(sig("wP_ready"), 1)
                        elif stage == "v":
                            for k in range(KT):
                                drain((stage, k), vP[:, k, :, 1:LP], lambda t: batches(t[:, :]), ACT.Identity, "vP_ready")
                        elif stage == "r":
                            for k in range(KT):
                                drain((stage, k), rT[:, k, :], whole, ACT.Identity, "rT_ready")
                        elif stage == "g":
                            @tanh
                            def _():
                                for k in range(KT):
                                    t, free = take(act, (stage, k))
                                    link(af(gg[:, k, :], t[:, :], ACT.Tanh, scale=0.5))
                                    link(af(ruk[:, k, :], t[:, :], ACT.Identity))
                                    act.sem_inc(free, 1)
                                    act.sem_inc(sig("tanh_g"), 1)
                        elif stage == "center":
                            for k in range(KT):
                                t, free = take(act, (stage, k))
                                af(ogT[:, k, :], t[:, :], ACT.Identity).then_inc(sig("oc_ready"), 1)
                                link(af(sq[:, k, :], t[:, :], ACT.Square))
                                act.sem_inc(free, 1)
                                act.sem_inc(sig("sq_ready"), 1)
                        elif stage == "variance":
                            for k in range(KT):
                                drain((stage, k), rgn[:, k, :], whole, ACT.Ln, "var_read", bias=eps5[:, :], scale=1.0 / HS)
                            for k in range(KT):
                                af(rgn[:, k, :], rgn[:, k, :], ACT.Exp, scale=-0.5).then_inc(sig("rgn_ready"), 1)
                        elif stage == "moments 2":
                            act.wait_ge(sig("stats4_ready"), 1)
                            rsqrt(rstd3[:, :], mv3[:, :, 1], eps5, 1.0, "rstd4_ready")
                        elif stage == "turn 2":
                            for k in range(KT):
                                drain((stage, k), xcP[:, k, :, 1:LP], lambda t: batches(t[:, :]), ACT.Identity, "xcP_ready",
                                      bias=v("ln2_b", k), scale=v("ln2_w", k))
                        elif stage == "ffn k":
                            for k in range(KT):
                                drain((stage, k), kkT[:, k, :], whole, ACT.Relu, "fk_read")
                            for k in range(KT):
                                af(kkT[:, k, :], kkT[:, k, :], ACT.Square).then_inc(sig("kk_ready"), 1)
                        elif stage == "ffn r":
                            @tanh
                            def _():
                                for q in range(2):
                                    drain((stage, q), thn[:, 2 * q:2 * q + 2, :], lambda t: t[:, :].rearrange("p (n e) -> p n e", n=2),
                                          ACT.Tanh, "thn_ready", scale=0.5)

                    step, rest = beside(layer3)
                    tables(LOG_EXP)
                    if now is None:
                        rest()
                        return

                    step()
                    step()
                    act.wait_ge(sig("stats0_ready"), 1)
                    rsqrt(rstd[:, :], mv[:, :, 1], eps5, 1.0, "rstd0_ready")
                    for k in range(KT):
                        drain(("cT", k), hT[:, k, :, 0, :], lambda t: batches(t[:, :]), ACT.Identity, "cT_ready")
                    step()
                    step()
                    for q in range(2):
                        t, free = take(act, ("mm", q))
                        if q == 0:
                            act.wait_ge(sig("mmb_zero"), 1)
                        for b in range(2):
                            r = slice(64 * b, 64 * b + 64)
                            ins = af(mmb[r, 2 * q:2 * q + 2, b, :], t[r, :].rearrange("p (n t) -> p n t", n=2),
                                     ACT.Identity, bias=v("bm")[r])
                        link(ins)
                        act.sem_inc(free, 1)
                        act.sem_inc(sig("mmb_ready"), 1)

                    def exps0(u):
                        t, free = take(act, ("s0", u))
                        act.wait_ge(sig("nmax0_ready"), u + 1)
                        if u >= SOFT:
                            act.wait_ge(sig("pT0_ready"), u - SOFT + 1)
                        for b in range(2):
                            ins = af(soft[:, u % SOFT, 256 * b:256 * b + 256], t[:, 256 * b:256 * b + 256], ACT.Exp,
                                     bias=nmax0[:, u, b:b + 1], accum_out=den0[:, u, b:b + 1])
                        link(ins)
                        act.sem_inc(free, 1)
                        act.sem_inc(sig("exp0"), 1)

                    def exps(u):
                        act.wait_ge(sig("sub"), u + 1)
                        af(soft[:, u % SOFT, :], soft[:, u % SOFT, :], ACT.Exp).then_inc(sig("exp"), 1)

                    def turned(u):
                        t, free = take(act, ("t", u))
                        if u < UNITS:
                            ins = af(pT1[:, (u // 4) % 2, :, :, u % 4, :], t[:, :].rearrange("p (j b l) -> p j b l", j=4, b=2), ACT.Identity)
                        else:
                            ins = af(pT2[:, (u // 2) % 4, u % 2, :], t[:, :], ACT.Identity)
                        ins.then_inc(sig("pT_ready"), 1)
                        act.wait_ge(sig("pT_ready"), u + 1)
                        act.sem_inc(free, 1)

                    def totals(c):
                        t, free = take(act, ("total", c))
                        if c >= 2:
                            act.wait_ge(sig("at_ready"), c - 1)
                        link(af(over[:, c % 2, :], t[:, :], ACT.Ln))
                        act.sem_inc(free, 1)
                        af(over[:, c % 2, :], over[:, c % 2, :], ACT.Exp, scale=-1.0).then_inc(sig("over_ready"), 1)

                    def between(i):
                        for h in range(2):
                            r = slice(2 * h, 2 * h + 2)
                            if i == 4 * h + 11:
                                drain(("x1T", h), x1T[:, h].rearrange("p k n b l -> p (k n b l)"), lambda t: t[:, :], ACT.Identity, "x1T_ready")
                            if i == A1 + 8 * h + 15:
                                act.wait_ge(sig("stats1_ready"), h + 1)
                                rsqrt(rstd[:, r], mv[:, r, 1], eps6, 1.0, "rstd1_ready")
                            if i == A1 + 8 * h + 17:
                                t, free = take(act, ("lT", h))
                                for k in range(KT):
                                    ins = af(hT[:, k, 4 * h:4 * h + 4, 1, :], batches(t[:, 256 * k:256 * k + 256]), ACT.Identity,
                                             bias=v("beta", k), scale=v("gamma", k)).then_inc(sig("lT_ready"), 1)
                                act.wait_ge(sig("lT_ready"), KT * (h + 1))
                                act.sem_inc(free, 1)
                            if i == A1 + 8 * h + 19:
                                for k in range(KT):
                                    drain(("k2", k, h), k2T[:, k, 4 * h:4 * h + 4, :], lambda t: t[:, :].rearrange("p (b n) -> p b n", n=KEYS),
                                          ACT.Identity, "k2_ready", bias=v("k_b", k))
                            if i == A2 + 8 * h + 15:
                                for p in (2 * h, 2 * h + 1):
                                    act.wait_ge(sig("x_added"), NP + p + 1)
                                    link(af(xh[:, p, :], xr[:, p, :], ACT.Square, accum_out=stats[:, p, 0:1]))
                                rsqrt(rstd[:, r], stats[:, r, 0], eps6, 1.0 / E, "rstd2_ready")
                            if i == A2 + 8 * h + 17:
                                t, free = take(act, ("xnT", h))
                                for k in range(KT):
                                    af(xnT[:, h, k, :], t[:, 256 * k:256 * k + 256], ACT.Identity, scale=v("post", k)).then_inc(sig("xnT_ready"), 1)
                                act.wait_ge(sig("xnT_ready"), KT * (h + 1))
                                act.sem_inc(free, 1)

                    for i in range(END):
                        step()
                        if unit(i - 3) >= 0:
                            turned(unit(i - 3))
                        if i < U0:
                            exps0(i)
                        if unit(i) >= 0:
                            exps(unit(i))
                        if pair_of(i - 8) >= 0:
                            totals(pair_of(i - 8))
                        between(i)
                    tables(GELU)
                    for n in range(HID // 128):
                        drain(("u", n), gT[:, n, :], lambda t: t[:, :], ACT.Gelu_apprx_tanh, "gT_ready", bias=v("b1", n))
                        step()
                    for q in range(2):
                        step()
                    rest()

                @block.vector
                def _(dve):
                    link = linker(dve, "dve_step")
                    tt, ts, stt = nc.vector.tensor_tensor, nc.vector.tensor_scalar, nc.vector.scalar_tensor_tensor

                    def filled(tile):
                        b, n = place[tile]
                        dve.wait_ge(sig(f"bank{b}_full"), n)

                    def batches(ap):
                        return ap.rearrange("p (b l) -> p b l", l=L)

                    def flat(ap):
                        return ap.rearrange("p n e -> p (n e)")

                    def moments(srcs, st, out_mv, name):
                        for n, s in enumerate(srcs):
                            ins = nc.vector.bn_stats(st[:, n, :], s)
                        link(ins)
                        for n in range(len(srcs)):
                            ins = nc.vector.bn_aggr(out_mv[:, n, :], st[:, n, :])
                        link(ins)
                        dve.sem_inc(sig(name), 1)

                    def normalize(dst, src, m, r, name):
                        for p in range(NP):
                            ts(dst[:, p, :], src[:, p, :], m[:, p, 0:1], r[:, p:p + 1], ALU.subtract, ALU.mult).then_inc(sig(name), 1)

                    def layer3(stage):
                        def mix(n, f):
                            if n:
                                filled({1: "maaB", 2: "td", 3: ("k", 1), 4: ("v", 1)}[n])
                            for k in range(KT):
                                t, free = take(dve, (stage, k))
                                m = xm[:, (n + 1) % 2, k, :]
                                link(stt(out=m, in0=t[:, :], scalar=v("maa", 2 * f + k), in1=sx[:, k, :], op0=ALU.add, op1=ALU.mult))
                                dve.sem_inc(free, 1)
                                tt(batches(m), batches(m), xaP[:, k, :, 1:LP], ALU.add).then_inc(sig("xm_ready"), 1)

                        def scan(n):
                            k = n // HS
                            dve.wait_ge(sig("aj_ready"), n + 1)
                            if n >= 2:
                                dve.wait_ge(sig("rs_ready"), n - 1)
                            nc.vector.tensor_tensor_scan(sj[:, n % 2, :], wP[:, k, :, :].rearrange("p b t -> p (b t)"), aj[:, n % 2, :], 0.0,
                                                         ALU.mult, ALU.add).then_inc(sig("sj_ready"), 1)

                        def read(n):
                            k = n // HS
                            dve.wait_ge(sig("sj_ready"), n + 1)
                            if n >= 2:
                                m = n - 2
                                if m % HS == HS - 1:
                                    filled(("o3", m // HS))
                                else:
                                    dve.wait_ge(sig("rs_used"), m - m // HS + 1)
                            tt(batches(rs[:, n % 2, :]), batches(rT[:, k, :]),
                               sj[:, n % 2, :].rearrange("p (b t) -> p b t", t=LP)[:, :, 0:L], ALU.mult).then_inc(sig("rs_ready"), 1)

                        def heads(k):
                            t, free = take(dve, ("o3", k))
                            link(tt(ruk[:, k, :], t[:, :], ruk[:, k, :], ALU.add))
                            dve.sem_inc(free, 1)
                            dve.sem_inc(sig("o3_ready"), 1)

                        if stage == "moments":
                            moments([x3[:, p, :] for p in range(NP)], stats3, mv3, "stats3_ready")
                        elif stage == "normalize":
                            dve.wait_ge(sig("rstd3_ready"), 1)
                            normalize(xh3, x3, mv3, rstd3, "xh3_ready")
                        elif stage == "shift":
                            dve.wait_ge(sig("edge3_ready"), 1)
                            for k in range(KT):
                                dve.wait_ge(sig("xaP_ready"), k + 1)
                                s = batches(sx[:, k, :])
                                link(tt(s, xaP[:, k, :, 0:L], xaP[:, k, :, 1:LP], ALU.subtract))
                                stt(out=batches(xm[:, 0, k, :]), in0=s, scalar=v("maa_x", k), in1=xaP[:, k, :, 1:LP],
                                    op0=ALU.mult, op1=ALU.add).then_inc(sig("x1m_ready"), 1)
                        elif stage[0:3] == "mix":
                            n = int(stage[4])
                            mix(n, MIXES[n])
                        elif stage == "r u k":
                            dve.wait_ge(sig("rT_ready"), KT)
                            dve.wait_ge(sig("wP_ready"), KT)
                            dve.wait_ge(sig("kP_ready"), KT)
                            dve.wait_ge(sig("tanh_g"), KT)
                            for k in range(KT):
                                link(stt(out=gg[:, k, :], in0=gg[:, k, :], scalar=1.0, in1=ruk[:, k, :], op0=ALU.add, op1=ALU.mult))
                                stt(out=batches(ruk[:, k, :]), in0=batches(rT[:, k, :]), scalar=v("u", k),
                                    in1=kP[:, k, :, 1:LP], op0=ALU.mult, op1=ALU.mult).then_inc(sig("ruk_ready"), 1)
                        elif stage == "bonus":
                            dve.wait_ge(sig("vP_ready"), KT)
                            for k in range(KT):
                                t, free = take(dve, (stage, k))
                                link(tt(batches(ruk[:, k, :]), batches(t[:, :]), vP[:, k, :, 1:LP], ALU.mult))
                                dve.sem_inc(free, 1)
                        elif stage[0] == "scan":
                            n = stage[1]
                            if n < KT * HS:
                                scan(n)
                            if 1 <= n < KT * HS + 1:
                                read(n - 1)
                            if n in (HS + 2, 2 * HS + 2):
                                heads(n // HS - 1)
                        elif stage == "gate":
                            for k in range(KT):
                                dve.wait_ge(sig("oc_ready"), k + 1)
                                dve.wait_ge(sig("rgn_ready"), k + 1)
                                link(tt(ogT[:, k, :], ogT[:, k, :], rgn[:, k, :], ALU.mult))
                                link(ts(ogT[:, k, :], ogT[:, k, :], v("gn_w", k), v("gn_b", k), ALU.mult, ALU.add))
                                tt(ogT[:, k, :], ogT[:, k, :], gg[:, k, :], ALU.mult).then_inc(sig("ogT_ready"), 1)
                        elif stage == "project":
                            for q in range(2):
                                t, free = take(dve, (stage, q))
                                link(tt(flat(x4[:, 2 * q:2 * q + 2, :]), t[:, :], flat(x3[:, 2 * q:2 * q + 2, :]), ALU.add))
                                dve.sem_inc(free, 1)
                        elif stage == "moments 2":
                            moments([x4[:, p, :] for p in range(NP)], stats3, mv3, "stats4_ready")
                        elif stage == "normalize 2":
                            dve.wait_ge(sig("rstd4_ready"), 1)
                            normalize(xh4, x4, mv3, rstd3, "xh4_ready")
                        elif stage == "shift 2":
                            dve.wait_ge(sig("edge4_ready"), 1)
                            for k in range(KT):
                                dve.wait_ge(sig("xcP_ready"), k + 1)
                                s = batches(sx2[:, k, :])
                                link(tt(s, xcP[:, k, :, 0:L], xcP[:, k, :, 1:LP], ALU.subtract))
                                for dst, name in ((xk2, "k"), (xr2, "r")):
                                    stt(out=batches(dst[:, k, :]), in0=s, scalar=v(f"ffn_{name}", k), in1=xcP[:, k, :, 1:LP],
                                        op0=ALU.mult, op1=ALU.add).then_inc(sig(f"x{name}2_ready"), 1)
                        elif stage == "ffn v":
                            for q in range(2):
                                t, free = take(dve, (stage, q))
                                dve.wait_ge(sig("thn_ready"), q + 1)
                                th = flat(thn[:, 2 * q:2 * q + 2, :])
                                link(stt(out=th, in0=th, scalar=1.0, in1=t[:, :], op0=ALU.add, op1=ALU.mult))
                                dve.sem_inc(free, 1)
                                stt(out=th, in0=th, scalar=0.5, in1=flat(x4[:, 2 * q:2 * q + 2, :]),
                                    op0=ALU.mult, op1=ALU.add).then_inc(sig("out_ready"), 2)

                    step, rest = beside(layer3)
                    if now is None:
                        rest()
                        return

                    step()
                    dve.wait_ge(sig("c0_in"), 16)
                    dve.wait_ge(sig("x0_in"), 16)
                    moments([c0[:, p, :] for p in range(NP)] + [x0[:, p, :] for p in range(NP)], stats, mv, "stats0_ready")
                    step()
                    step()
                    dve.wait_ge(sig("rstd0_ready"), 1)
                    normalize(ch, c0, mv, rstd, "ch_ready")
                    for q in range(2):
                        t, free = take(dve, ("ml", q))
                        link(nc.vector.tensor_copy(mlT[:, 2 * q:2 * q + 2, :, :].rearrange("p n s o -> p (n s o)"), t[:, :]))
                        dve.sem_inc(free, 1)
                        dve.sem_inc(sig("ml_ready"), 1)
                    normalize(xh0, x0, mv[:, NP:, :], rstd[:, NP:], "xh_ready")
                    step()
                    for q in range(2):
                        t, free = take(dve, ("mn", q))
                        link(ts(flat(mn[:, 2 * q:2 * q + 2, :]), t[:, :], v("bn"), None, ALU.add))
                        dve.sem_inc(free, 1)
                        dve.sem_inc(sig("mn_ready"), 1)

                    def layer0(i):
                        if i < U0:
                            t, _ = take(dve, ("s0", i))
                            nc.vector.tensor_reduce(nmax0[:, i, :], t[:, :].rearrange("p (b s) -> p b s", b=2), X, ALU.max,
                                                    negate=True).then_inc(sig("nmax0_ready"), 1)
                        if 1 <= i < U0 + 1:
                            dve.wait_ge(sig("exp0"), i)
                            nc.vector.reciprocal(rden0[:, i - 1, :], den0[:, i - 1, :]).then_inc(sig("rden0_ready"), 1)
                        if 3 <= i < U0 + 3:
                            u = i - 3
                            t, free = take(dve, ("t0", u))
                            if u >= 4:
                                filled(("o0", u // 2 - 2))
                            nc.vector.tensor_copy(pT0[:, (u // 2) % 2, u % 2].rearrange("p b s t -> p (b s t)"), t[:, :]).then_inc(sig("pT0_ready"), 1)
                            dve.wait_ge(sig("pT0_ready"), u + 1)
                            dve.sem_inc(free, 1)
                        if i >= 6 and (i - 6) % 2 == 0 and (i - 6) // 2 < NP:
                            p = (i - 6) // 2
                            t, free = take(dve, ("o0", p))
                            link(ts(mo[:, p, :], t[:, 0:E], v("bl"), None, ALU.add))
                            dve.sem_inc(free, 1)
                            dve.sem_inc(sig("mo_ready"), 1)
                        if i >= 8 and (i - 8) % 2 == 0 and (i - 8) // 2 < NP:
                            p = (i - 8) // 2
                            t, free = take(dve, ("x1", p))
                            link(stt(out=xA[:, p, :], in0=t[:, 0:E], scalar=v("bo"), in1=x0[:, p, :], op0=ALU.add, op1=ALU.add))
                            dve.sem_inc(free, 1)
                            dve.sem_inc(sig("x1_ready"), 1)

                    def cuts(u, ap):
                        return ap.rearrange("p (h s) -> p h s", h=KVH if u < UNITS else 4)

                    def masked(u):
                        t, free = take(dve, ("s", u))
                        if u >= SOFT:
                            dve.wait_ge(sig("pT_ready"), u - SOFT + 1)
                        if u == 0:
                            dve.wait_ge(sig("mask1_in"), 16)
                        if u == UNITS:
                            dve.wait_ge(sig("mask2_ready"), 1)
                        mask, segs, n = (mask1[:, u // 4, :], KVH, L) if u < UNITS else (mask2[:, (u - UNITS) // 2, :], 4, KEYS)
                        stt(out=cuts(u, soft[:, u % SOFT, :]), in0=cuts(u, t[:, :]), scalar=HD1 ** -0.5 if u < UNITS else 1.0 / HD2,
                            in1=mask.unsqueeze(1).broadcast_to([128, segs, n]), op0=ALU.mult, op1=ALU.add).then_inc(free, 1)

                    def largest(u):
                        b, k = place["s", u]
                        dve.wait_ge(sig(f"bank{b}_free"), k)
                        nc.vector.tensor_reduce(seg_max[:, u % SOFT, 0:KVH if u < UNITS else 4], cuts(u, soft[:, u % SOFT, :]),
                                                X, ALU.max).then_inc(sig("max"), 1)

                    def one_query(u):
                        if u >= 2:
                            filled(("s", UNITS + u - 2))
                        tt(qring[:, u % 2, :, :], q2T[:, u % 2, u // 2, :].unsqueeze(1).broadcast_to([128, HPT, L]),
                           hmask[:, :].unsqueeze(2).broadcast_to([128, HPT, L]), ALU.mult).then_inc(sig("qring_ready"), 1)

                    def divide(c):
                        t, free = take(dve, ("value", c))
                        dve.wait_ge(sig("over_ready"), c + 1)
                        if c >= 2:
                            filled(("out", c - 2))
                        link(tt(attended[:, c % 2].rearrange("p g (b l) -> p b g l", b=2), t[:, :].rearrange("p (b g l) -> p b g l", b=2, g=4),
                                over[:, c % 2, :].rearrange("p (b g l) -> p b g l", b=2, g=4), ALU.mult))
                        dve.sem_inc(free, 1)
                        dve.sem_inc(sig("at_ready"), 1)

                    def add(c):
                        t, free = take(dve, ("out", c))
                        p = c % NP
                        dve.wait_ge(sig("xr_ready"), c + 1)
                        link(tt(xr[:, p, :], t[:, 0:E], xr[:, p, :], ALU.add))
                        dve.sem_inc(free, 1)
                        dve.sem_inc(sig("x_added"), 1)

                    def between(i):
                        if i == U0 + 2:
                            t, free = take(dve, "k1")
                            link(ts(kT1[:, :, :].rearrange("p n s -> p (n s)"), t[:, 0:256], v("bk"), None, ALU.add))
                            dve.sem_inc(free, 1)
                            dve.sem_inc(sig("kT1_ready"), 1)
                        if i == U0 + 6:
                            t, free = take(dve, "v1")
                            for b in range(2):
                                for h in range(2):
                                    src = t[64 * b:64 * b + 64, 0:256].rearrange("p (n j h d) -> p h n j d", n=NP, h=2, d=HD1)[:, h]
                                    ins = nc.vector.tensor_copy(vbd[64 * h:64 * h + 64, b::2, :, 8 * h:8 * h + 8], src)
                            link(ins)
                            dve.sem_inc(free, 1)
                        for h in range(2):
                            r = slice(2 * h, 2 * h + 2)
                            if i == 4 * h + 12:
                                t, free = take(dve, ("q1", h))
                                dve.wait_ge(sig("qz_zero"), 1)
                                for b in range(2):
                                    rows = slice(64 * b, 64 * b + 64)
                                    ins = tt(qz[rows, r, :, b, :], t[rows, :].rearrange("p (g n l) -> p n g l", g=GQ, n=2),
                                             bq_rows[rows, :].unsqueeze(1).unsqueeze(3).broadcast_to([64, 2, GQ, L]), ALU.add)
                                link(ins)
                                dve.sem_inc(free, 1)
                                dve.sem_inc(sig("qz_ready"), 1)
                            if i == A1 + 8 * h + 15:
                                moments([xr[:, p, :] for p in (2 * h, 2 * h + 1)], stats[:, r, :], mv[:, r, :], "stats1_ready")
                            if i == A1 + 8 * h + 16:
                                dve.wait_ge(sig("rstd1_ready"), h + 1)
                                for p in (2 * h, 2 * h + 1):
                                    ts(xh[:, p, :], xr[:, p, :], mv[:, p, 0:1], rstd[:, p:p + 1], ALU.subtract, ALU.mult).then_inc(sig("xh1_ready"), 1)
                            if i == A1 + 8 * h + 18:
                                t, free = take(dve, ("q2", h))
                                for k in range(KT):
                                    ins = ts(q2T[:, k, 4 * h:4 * h + 4, :], batches(t[:, 256 * k:256 * k + 256]), v("q_b", k), None, ALU.add)
                                link(ins)
                                dve.sem_inc(free, 1)
                            if i == A1 + 8 * h + 20:
                                for p in (2 * h, 2 * h + 1):
                                    t, free = take(dve, ("v2", p))
                                    link(nc.vector.tensor_copy(v2[:, 2 * p:2 * p + 2, :].rearrange("p b n -> p (b n)"), t[:, :]))
                                    dve.sem_inc(free, 1)
                                    dve.sem_inc(sig("v2_ready"), 1)
                            if i == A2 + 8 * h + 16:
                                dve.wait_ge(sig("rstd2_ready"), h + 1)
                                for p in (2 * h, 2 * h + 1):
                                    ts(xh[:, p, :], xr[:, p, :], rstd[:, p:p + 1], None, ALU.mult).then_inc(sig("xh2_ready"), 1)
                        if i == A2 - 1:
                            for u in range(2):
                                one_query(u)

                    for i in range(END):
                        layer0(i)
                        if unit(i - 1) >= 0:
                            largest(unit(i - 1))
                        step()
                        if unit(i) >= 0:
                            masked(unit(i))
                        if A2 <= i < A2 + UNITS - 2:
                            one_query(i - A2 + 2)
                        if pair_of(i - 9) >= 0:
                            divide(pair_of(i - 9))
                        if pair_of(i - 11) >= 0:
                            add(pair_of(i - 11))
                        between(i)
                    for _ in range(HID // 128):
                        step()
                    for q in range(2):
                        t, free = take(dve, ("y2", q))
                        dve.wait_ge(sig("xr3_ready"), NP)
                        link(tt(flat(x3[:, 2 * q:2 * q + 2, :]), t[:, :], flat(xr[:, 2 * q:2 * q + 2, :]), ALU.add))
                        dve.sem_inc(free, 1)
                        step()
                    rest()

                @block.gpsimd
                def _(pool):
                    link = linker(pool, "pool_step")
                    tt, ts = nc.gpsimd.tensor_tensor, nc.gpsimd.tensor_scalar

                    def layer3(stage):
                        def products(n):
                            k = n // HS
                            pool.wait_ge(sig(f"vj{n % 3}_in"), 16 * (n // 3 + 1))
                            if n == 0:
                                pool.wait_ge(sig("s0_in"), 16 * KT)
                                pool.wait_ge(sig("kP_ready"), KT)
                            if n >= 2:
                                pool.wait_ge(sig("sj_ready"), n - 1)
                            tt(aj[:, n % 2, :], kP[:, k, :, :].rearrange("p b t -> p (b t)"), vj[:, n % 3, :], ALU.mult).then_inc(sig("kv_done"), 1)
                            pool.wait_ge(sig("kv_done"), n + 1)
                            nc.gpsimd.tensor_copy(aj[:, n % 2, :].rearrange("p (b t) -> p b t", t=LP)[:, :, 0], s0[:, k, :, n % HS]).then_inc(sig("aj_ready"), 1)

                        if stage == "turn":
                            for k in range(KT):
                                nc.gpsimd.tensor_copy(xaP[:, k, :, 0], edge[:, 1, k, :])
                                for t in (kP, vP, wP):
                                    ins = nc.gpsimd.memset(t[:, k, :, 0], 0.0)
                            link(ins)
                            pool.sem_inc(sig("edge3_ready"), 1)
                            link(nc.gpsimd.memset(xf[32:64, 1, :], 0.0))
                            pool.sem_inc(sig("xf_zero"), 1)
                        elif stage == "bonus":
                            products(0)
                        elif stage[0] == "scan" and stage[1] + 1 < KT * HS:
                            products(stage[1] + 1)
                        elif stage == "normalize 2":
                            pool.wait_ge(sig("o3_ready"), KT)
                            for k in range(KT):
                                ins = nc.gpsimd.tensor_copy(xcP[:, k, :, 0], edge[:, 0, k, :])
                            link(ins)
                            pool.sem_inc(sig("edge4_ready"), 1)

                    step, rest = beside(layer3)
                    if now is None:
                        rest()
                        return

                    link(nc.gpsimd.memset(mmb[0:64, :, 1, :], 0.0))
                    link(nc.gpsimd.memset(mmb[64:128, :, 0, :], 0.0))
                    pool.sem_inc(sig("mmb_zero"), 1)
                    for _ in range(4):
                        step()
                    link(nc.gpsimd.memset(qz[0:64, :, :, 1, :], 0.0))
                    link(nc.gpsimd.memset(qz[64:128, :, :, 0, :], 0.0))
                    pool.sem_inc(sig("qz_zero"), 1)

                    def subtract(u):
                        pool.wait_ge(sig("max"), u + 1)
                        segs = KVH if u < UNITS else 4
                        s = soft[:, u % SOFT, :].rearrange("p (h s) -> p h s", h=segs)
                        tt(s, s, seg_max[:, u % SOFT, 0:segs].unsqueeze(2).broadcast_to([128, segs, 512 // segs]),
                           ALU.subtract).then_inc(sig("sub"), 1)

                    for i in range(END):
                        step()
                        if i < U0:
                            pool.wait_ge(sig("rden0_ready"), i + 1)
                            for b in range(2):
                                s = soft[:, i % SOFT, 256 * b:256 * b + 256]
                                ins = ts(s, s, rden0[:, i, b:b + 1], None, ALU.mult)
                            ins.then_inc(sig("p0_ready"), 1)
                        if unit(i) >= 0:
                            subtract(unit(i))
                        for p in range(NP):
                            if i == U0 + 2 + p:
                                pool.wait_ge(sig("kT1_ready"), 1)
                                tt(kbd[:, p, :, :], kT1[:, p, :].unsqueeze(1).broadcast_to([128, KVH, L]),
                                   kvmask[:, :].unsqueeze(2).broadcast_to([128, KVH, L]), ALU.mult).then_inc(sig("kbd_ready"), 1)
                            if i == U0 + 5 + p:
                                pool.wait_ge(sig("x1_ready"), p + 1)
                                tt(xr[:, p, :], xA[:, p, :], row1[:, :], ALU.add).then_inc(sig("xr_ready"), 1)
                            if i == A1 + 8 * (p // 2) + 17:
                                pool.wait_ge(sig("xh1_ready"), p + 1)
                                link(tt(xA[:, p, :], xh[:, p, :], row_gamma[:, :], ALU.mult))
                                tt(xr[:, p, :], xA[:, p, :], row2[:, :], ALU.add).then_inc(sig("xr_ready"), 1)
                            if i == A2 + 8 * (p // 2) + 17:
                                pool.wait_ge(sig("xh2_ready"), p + 1)
                                tt(xr[:, p, :], xA[:, p, :], row_b2[:, :], ALU.add).then_inc(sig("xr3_ready"), 1)
                        if i == A1:
                            pool.wait_ge(sig("mask2_in"), 16)
                            m = mask2[:, :, 0:L]
                            ts(m, m.bitcast(I32), 0, MASKED, ALU.is_equal, ALU.mult).then_inc(sig("mask2_ready"), 1)
                    for _ in range(2 + HID // 128):
                        step()
                    rest()
                    pool.wait_ge(sig("xnT_ready"), KT)
                    for s in range(2):
                        ins = nc.gpsimd.tensor_copy(edge[:, s, :, :], hT[:, :, :, 0, s])
                    link(ins)
            clear_all()

        clear_all()
        last = GROUPS
        group_block(0, None)
        with nc.Fori(1, last) as turn:
            group_block(turn, turn - 1)
        group_block(None, last - 1)


_OUT = (B, L, E)


def kernel(**inputs):
    import numpy as np
    import concourse.bacc as bacc
    from concourse.bass_utils import run_bass_kernel_spmd

    nc = bacc.Bacc("TRN2", target_bir_lowering=False, num_devices=1)
    arrays, aps = {}, {}
    for name, value in inputs.items():
        value = np.ascontiguousarray(value)
        arrays[f"in_{name}"] = value
        aps[name] = nc.dram_tensor(f"in_{name}", value.shape, mybir.dt.from_np(value.dtype), kind="ExternalInput").ap()
    out = nc.dram_tensor("out_x", _OUT, F32, kind="ExternalOutput").ap()
    build(nc, aps, out)
    result = run_bass_kernel_spmd(nc, [arrays], core_ids=[0])
    return result.results[0]["out_x"]
```
